# Optimizing a Trainium2 kernel written in Bass

```python
import numpy as np
import jax
import jax.numpy as jnp

def _softmax(x, axis=-1):
    return jax.nn.softmax(x, axis=axis)

def _gelu(x):
    return jax.nn.gelu(x, approximate=True)

def _silu(x):
    return jax.nn.silu(x)

def _sigmoid(x):
    return jax.nn.sigmoid(x)

def _layernorm(x, axis=-1, eps=1e-05):
    m = jnp.mean(x, axis=axis, keepdims=True)
    v = jnp.var(x, axis=axis, keepdims=True)
    return (x - m) / jnp.sqrt(v + eps)

def _scatter_add(tgt, idx, src, axis=0):
    return tgt.at[idx].add(src)

def _segment_sum(src, seg, n):
    return jax.ops.segment_sum(src, seg, n)
kernel_name = 'mk_gps_d1_gnn_r16_641b1f'

def setup_inputs(seed: int=0):
    np.random.seed(seed)
    _w = jnp.asarray

    def _rec_inputs():
        import jax
        import jax.numpy as jnp
        _gk = jax.random.key(seed)
        x = -0.0006008 + 1.001 * jax.random.normal(jax.random.fold_in(_gk, 1), (3125, 256), jnp.float32)
        src = jax.random.randint(jax.random.fold_in(_gk, 2), (50000,), 0, 3125, jnp.int32)
        dst = jnp.minimum((3125 * jax.random.uniform(jax.random.fold_in(_gk, 3), (50000,)) ** 2.0).astype(jnp.int32), 49999)
        _o = jnp.argsort(dst, stable=True)
        src = src[_o]
        dst = dst[_o]
        return (x, src, dst)
    x, src, dst = _rec_inputs()

    def _L0_gnn_setup():
        import jax, jax.numpy as jnp
        import numpy as np
        N, E, D = (625, 20000, 256)
        key = jax.random.key(seed)
        k1, k2, k3, k4 = jax.random.split(key, 4)
        x = jax.random.normal(k1, (N, D), dtype=jnp.float32)
        edge_index = jax.random.randint(k2, (2, E), 0, N, dtype=jnp.int64)
        s = 1.0 / np.sqrt(D)
        w1 = jax.random.uniform(k3, (D, D), dtype=jnp.float32, minval=-s, maxval=s)
        b1 = jnp.zeros((D,), dtype=jnp.float32)
        w2 = jax.random.uniform(k4, (D, D), dtype=jnp.float32, minval=-s, maxval=s)
        b2 = jnp.zeros((D,), dtype=jnp.float32)
        return {'x': x, 'edge_index': edge_index, 'w1': w1, 'b1': b1, 'w2': w2, 'b2': b2}
    _L0_gnn_all = _L0_gnn_setup()
    _L0_gnn_in = {k: v for k, v in _L0_gnn_all.items() if k in ('w1', 'b1', 'w2', 'b2')}
    del _L0_gnn_all

    def _L0_mix_setup():
        import jax, jax.numpy as jnp
        import numpy as np
        A, Bc, Cc = (0.5, 1.0, 1.0)
        H = 8
        EPS = 1e-12

        def _normalize(t):
            n = jnp.linalg.norm(t, axis=-1, keepdims=True)
            return t / jnp.maximum(n, EPS)
        key = jax.random.key(seed)
        ks = jax.random.split(key, 5)
        B, N, C = (8, 128, 256)
        D = C // H
        x = jax.random.normal(ks[0], (B, N, C), dtype=jnp.float32)
        Wqkv = jax.random.normal(ks[1], (3 * H * D, C), dtype=jnp.float32) * 0.02
        bqkv = jnp.zeros((3 * H * D,), dtype=jnp.float32)
        Wproj = jax.random.normal(ks[2], (C, H * D), dtype=jnp.float32) * 0.02
        bproj = jnp.zeros((C,), dtype=jnp.float32)
        temperature = jnp.ones((1, H, 1, 1), dtype=jnp.float32)
        return {'x': x, 'Wqkv': Wqkv, 'bqkv': bqkv, 'Wproj': Wproj, 'bproj': bproj, 'temperature': temperature}
    _L0_mix_all = _L0_mix_setup()
    _L0_mix_in = {k: v for k, v in _L0_mix_all.items() if k in ('Wqkv', 'bqkv', 'Wproj', 'bproj', 'temperature')}
    del _L0_mix_all

    def _L0_ffn_setup():
        import jax, jax.numpy as jnp
        import numpy as np
        B, S, H, F, E, K = (8, 256, 256, 512, 16, 2)
        EPS = 1e-05
        key = jax.random.key(seed)
        ks = jax.random.split(key, 9)
        sc = 0.02
        return {'x': jax.random.normal(ks[0], (B, S, H), dtype=jnp.float32), 'gate_w': jax.random.normal(ks[1], (H, E), dtype=jnp.float32) * sc, 'gate_b': jnp.zeros((E,), dtype=jnp.float32), 'w1': jax.random.normal(ks[2], (E, H, F), dtype=jnp.float32) * sc, 'b1': jnp.zeros((E, F), dtype=jnp.float32), 'w2': jax.random.normal(ks[3], (E, F, H), dtype=jnp.float32) * sc, 'b2': jnp.zeros((E, H), dtype=jnp.float32), 'gamma': jnp.ones((H,), dtype=jnp.float32), 'beta': jnp.zeros((H,), dtype=jnp.float32)}
    _L0_ffn_all = _L0_ffn_setup()
    _L0_ffn_in = {k: v for k, v in _L0_ffn_all.items() if k in ('gate_w', 'gate_b', 'w1', 'b1', 'w2', 'b2', 'gamma', 'beta')}
    del _L0_ffn_all
    return {'x': x, 'src': src, 'dst': dst, 'L0_gnn_w1': _L0_gnn_in['w1'], 'L0_gnn_b1': _L0_gnn_in['b1'], 'L0_gnn_w2': _L0_gnn_in['w2'], 'L0_gnn_b2': _L0_gnn_in['b2'], 'L0_mix_Wqkv': _L0_mix_in['Wqkv'], 'L0_mix_bqkv': _L0_mix_in['bqkv'], 'L0_mix_Wproj': _L0_mix_in['Wproj'], 'L0_mix_bproj': _L0_mix_in['bproj'], 'L0_mix_temperature': _L0_mix_in['temperature'], 'L0_ffn_gate_w': _L0_ffn_in['gate_w'], 'L0_ffn_gate_b': _L0_ffn_in['gate_b'], 'L0_ffn_w1': _L0_ffn_in['w1'], 'L0_ffn_b1': _L0_ffn_in['b1'], 'L0_ffn_w2': _L0_ffn_in['w2'], 'L0_ffn_b2': _L0_ffn_in['b2'], 'L0_ffn_gamma': _L0_ffn_in['gamma'], 'L0_ffn_beta': _L0_ffn_in['beta']}

def reference(x, src, dst, L0_gnn_w1, L0_gnn_b1, L0_gnn_w2, L0_gnn_b2, L0_mix_Wqkv, L0_mix_bqkv, L0_mix_Wproj, L0_mix_bproj, L0_mix_temperature, L0_ffn_gate_w, L0_ffn_gate_b, L0_ffn_w1, L0_ffn_b1, L0_ffn_w2, L0_ffn_b2, L0_ffn_gamma, L0_ffn_beta):
    import jax
    import jax.numpy as jnp

    def _L0_gnn_ref(x, edge_index, w1, b1, w2, b2):
        import jax, jax.numpy as jnp
        import numpy as np
        N, E, D = (625, 20000, 256)

        def mlp(h):
            return jax.nn.relu(h @ w1 + b1) @ w2 + b2
        row, col = (edge_index[0], edge_index[1])
        msgs = mlp(x[col])
        agg = jax.ops.segment_sum(msgs, row, num_segments=x.shape[0])
        return mlp(x + agg)

    def _L0_mix_ref(x, Wqkv, bqkv, Wproj, bproj, temperature):
        import jax, jax.numpy as jnp
        import numpy as np
        A, Bc, Cc = (0.5, 1.0, 1.0)
        H = 8
        EPS = 1e-12

        def _normalize(t):
            n = jnp.linalg.norm(t, axis=-1, keepdims=True)
            return t / jnp.maximum(n, EPS)
        B, N, C = x.shape
        D = C // H
        scale = float(D) ** 0.25
        qkv = (x @ Wqkv.T + bqkv).reshape(B, N, 3, H, D)
        qkv = jnp.transpose(qkv, (2, 0, 3, 1, 4))
        q, k, v = (qkv[0], qkv[1], qkv[2])
        q = q * scale
        v1 = jnp.concatenate([jnp.ones((B, H, N, 1), dtype=v.dtype), v], axis=-1)
        qn = _normalize(q) * (scale * temperature)
        kn = _normalize(k) * scale
        vN = v1 / N
        kv_mod = jnp.einsum('bhni,bhnj,bhne->bhije', kn, kn, vN)
        kv = jnp.einsum('bhnd,bhne->bhde', kn, vN)
        vsum = jnp.sum(vN, axis=-2)[:, :, None, :]
        y = A * jnp.einsum('bhni,bhnj,bhije->bhne', qn, qn, kv_mod) + scale ** 2 * Bc * jnp.einsum('bhnd,bhde->bhne', qn, kv) + scale ** 4 * Cc * vsum
        y_norm, y = (y[..., :1], y[..., 1:])
        y = y / y_norm
        out = jnp.transpose(y, (0, 2, 1, 3)).reshape(B, N, H * D)
        return out @ Wproj.T + bproj

    def _L0_ffn_ref(x, gate_w, gate_b, w1, b1, w2, b2, gamma, beta):
        import jax, jax.numpy as jnp
        import numpy as np
        B, S, H, F, E, K = (8, 256, 256, 512, 16, 2)
        EPS = 1e-05
        gate_logits = x @ gate_w + gate_b
        topk_vals, topk_idx = jax.lax.top_k(gate_logits, K)
        topk_w = jax.nn.softmax(topk_vals, axis=-1)
        h = jax.nn.relu(jnp.einsum('bsh,ehf->bsef', x, w1) + b1)
        expert_out = jnp.einsum('bsef,efh->bseh', h, w2) + b2
        sel = jnp.take_along_axis(expert_out, topk_idx[:, :, :, None], axis=2)
        moe = jnp.sum(topk_w[..., None] * sel, axis=2)
        y = x + moe
        mu = jnp.mean(y, axis=-1, keepdims=True)
        var = jnp.var(y, axis=-1, keepdims=True)
        return (y - mu) / jnp.sqrt(var + EPS) * gamma + beta
    edge_index = jnp.stack([src, dst])
    xn = _layernorm(x, axis=-1)
    x = x + _L0_gnn_ref(xn, edge_index, L0_gnn_w1, L0_gnn_b1, L0_gnn_w2, L0_gnn_b2) + _L0_mix_ref(xn[None], L0_mix_Wqkv, L0_mix_bqkv, L0_mix_Wproj, L0_mix_bproj, L0_mix_temperature)[0]
    x = x + _L0_ffn_ref(_layernorm(x, axis=-1)[None], L0_ffn_gate_w, L0_ffn_gate_b, L0_ffn_w1, L0_ffn_b1, L0_ffn_w2, L0_ffn_b2, L0_ffn_gamma, L0_ffn_beta)[0]
    return x

_drawn_inputs = setup_inputs


def setup_inputs(seed=0):
    import zlib

    import numpy as np

    out = dict(_drawn_inputs(seed))
    spreads = {'L0_gnn_b1': (0.0, 0.1),
     'L0_gnn_b2': (0.0, 0.1),
     'L0_mix_bqkv': (0.0, 0.313),
     'L0_mix_bproj': (0.0, 0.1),
     'L0_mix_temperature': (1.0, 0.6),
     'L0_ffn_gate_b': (0.0, 0.282),
     'L0_ffn_b1': (0.0, 0.772),
     'L0_ffn_b2': (0.0, 0.1),
     'L0_ffn_gamma': (1.0, 0.2),
     'L0_ffn_beta': (0.0, 0.1)}
    factors = {'L0_mix_Wqkv': 24.644}
    for name, (base, spread) in spreads.items():
        noise = np.random.default_rng([zlib.crc32(name.encode()), seed]).standard_normal(out[name].shape)
        drawn = base * np.exp(spread * noise) if base else spread * noise
        out[name] = jnp.asarray(drawn.astype(out[name].dtype))
    for name, factor in factors.items():
        out[name] = (out[name] * factor).astype(out[name].dtype)
    return out
```

```python
import numpy as np
import concourse.bass as bass
from concourse import mybir
from contextlib import ExitStack

F32 = mybir.dt.float32
F16 = mybir.dt.float16
BF16 = mybir.dt.bfloat16
I32 = mybir.dt.int32
U32 = mybir.dt.uint32
ALU = mybir.AluOpType
ACT = mybir.ActivationFunctionType
AX = mybir.AxisListType

N, D, E = 3125, 256, 50000
P, T = 125, 25
G = 5
EC = E // P
SLOT = 128
NB = T
NQ = 416
GB = 8
NBATCH = NQ // GB
H, DH = 8, 32
HV = DH + 1
NX, FF = 16, 512
NT = 64
LAG = 2
MAGIC = 12582912.0
MID = 1562
SCALE2 = float(DH) ** 0.5
LN_EPS = 1e-5
assert NQ * SLOT >= E + NB * (SLOT - 1) - SLOT + 1 and NT * SLOT > 2 * N + NX * (SLOT - 1) - SLOT


class Region:

    def __init__(self, tensor, start=0, end=None):
        self.tensor, self.at, self.end = tensor, start, end

    def take(self, shape, dt=F32, parts=128):
        size = int(np.prod(shape))
        words = size if dt in (F32, I32, U32) else (size + 1) // 2
        view = self.tensor[0:parts, self.at:self.at + words]
        self.at += words
        assert self.end is None or self.at <= self.end, (self.at, self.end)
        if dt is not F32:
            view = view.bitcast(dt)
        if len(shape) == 2:
            view = view.rearrange("p (a b) -> p a b", a=shape[0])
        if len(shape) == 3:
            view = view.rearrange("p (a b c) -> p a b c", a=shape[0], b=shape[1])
        return view


class Chain:

    def __init__(self, eng, sem):
        self.eng, self.sem, self.base, self.n = eng, sem, 0, 0

    def add(self, ins):
        ins.then_inc(self.sem, 1)
        self.n += 1

    def wait(self):
        self.eng.wait_ge(self.sem, self.base + self.n)

    def enter(self, i, first, per):
        self.start, self.per = self.base + self.n, per
        self.base, self.n = self.start + (i - first) * per, 0

    def leave(self, rounds):
        assert self.n == self.per, (self.n, self.per)
        self.base, self.n = self.start + rounds * self.per, 0


class Semaphores:

    def __init__(self, sem):
        self.x_in = sem("x_in")
        self.edges_in = sem("edges_in")
        self.gnn_in = sem("gnn_in")
        self.raw_in = sem("raw_in")
        self.bias_in = sem("bias_in")
        self.gate_in = sem("gate_in")
        self.w_in = sem("w_in")
        self.late_in = sem("late_in")
        self.consts = sem("consts")
        self.preps = sem("preps")
        self.wT_mm = sem("wT_mm")
        self.dve_chain = sem("dve_chain")
        self.pool_chain = sem("pool_chain")
        self.act_chain = sem("act_chain")
        self.apart = sem("apart")
        self.ln_stats = sem("ln_stats")
        self.rstd_sd = sem("rstd_sd")
        self.xn_ready = sem("xn_ready")
        self.xnT_mm = sem("xnT_mm")
        self.xnT_ready = sem("xnT_ready")
        self.l1_mm = sem("l1_mm")
        self.h_ready = sem("h_ready")
        self.m_mm = sem("m_mm")
        self.m_evac = sem("m_evac")
        self.m_biased = sem("m_biased")
        self.qkv_mm = sem("qkv_mm")
        self.qkv_evac = sem("qkv_evac")
        self.qkv_biased = sem("qkv_biased")
        self.hT_copied = sem("hT_copied")
        self.norm_sum = sem("norm_sum")
        self.norm_root = sem("norm_root")
        self.norm_ok = sem("norm_ok")
        self.normed = sem("normed")
        self.cnt_ok = sem("cnt_ok")
        self.prefix_mm = sem("prefix_mm")
        self.n_col_ok = sem("n_col_ok")
        self.ends_mm = sem("ends_mm")
        self.past_ok = sem("past_ok")
        self.bucket_mm = sem("bucket_mm")
        self.col_hot_ok = sem("col_hot_ok")
        self.col_mm = sem("col_mm")
        self.sorted_mm = sem("sorted_mm")
        self.sorted_ok = sem("sorted_ok")
        self.msg_idx_ok = sem("msg_idx_ok")
        self.hot_src_ok = sem("hot_src_ok")
        self.agg_mm = sem("agg_mm")
        self.agg_add = sem("agg_add")
        self.v1_ones = sem("v1_ones")
        self.kd_ok = sem("kd_ok")
        self.v1_ok = sem("v1_ok")
        self.lin_mm = sem("lin_mm")
        self.k_diag_ok = sem("k_diag_ok")
        self.diag_mm = sem("diag_mm")
        self.pairs_ok = sem("pairs_ok")
        self.head_mm = sem("head_mm")
        self.kv_ok = sem("kv_ok")
        self.q_row_ok = sem("q_row_ok")
        self.split_ok = sem("split_ok")
        self.q_partsT_mm = sem("q_partsT_mm")
        self.qT_ok = sem("qT_ok")
        self.qnT_mm = sem("qnT_mm")
        self.q_ld_ok = sem("q_ld_ok")
        self.sel_mm = sem("sel_mm")
        self.q_pairs_ok = sem("q_pairs_ok")
        self.y_mm = sem("y_mm")
        self.y_ld_mm = sem("y_ld_mm")
        self.mix_row_ok = sem("mix_row_ok")
        self.mixT_mm = sem("mixT_mm")
        self.mixT_ok = sem("mixT_ok")
        self.proj_mm = sem("proj_mm")
        self.x_ok = sem("x_ok")
        self.b1_mm = sem("b1_mm")
        self.b1_ok = sem("b1_ok")
        self.f1_mm = sem("f1_mm")
        self.h2_ok = sem("h2_ok")
        self.f2_mm = sem("f2_mm")
        self.x2_add = sem("x2_add")
        self.ln2_stats = sem("ln2_stats")
        self.ln2_root = sem("ln2_root")
        self.xn2_ok = sem("xn2_ok")
        self.xn2_out = sem("xn2_out")
        self.xn2T_mm = sem("xn2T_mm")
        self.xn2T_ok = sem("xn2T_ok")
        self.gate_mm = sem("gate_mm")
        self.gate_ok = sem("gate_ok")
        self.gap_ok = sem("gap_ok")
        self.exp_ok = sem("exp_ok")
        self.trash_ok = sem("trash_ok")
        self.count_ok = sem("count_ok")
        self.route_mm = sem("route_mm")
        self.col_x_ok = sem("col_x_ok")
        self.ends_x_mm = sem("ends_x_mm")
        self.past_x_ok = sem("past_x_ok")
        self.expert_mm = sem("expert_mm")
        self.tok_hot_ok = sem("tok_hot_ok")
        self.tok_mm = sem("tok_mm")
        self.tok_ok = sem("tok_ok")
        self.tokT_mm = sem("tokT_mm")
        self.tokT_ok = sem("tokT_ok")
        self.ffn1_mm = sem("ffn1_mm")
        self.hid_ok = sem("hid_ok")
        self.hidT_mm = sem("hidT_mm")
        self.relu_ok = sem("relu_ok")
        self.ffn2_mm = sem("ffn2_mm")
        self.y_ok = sem("y_ok")
        self.beta_ok = sem("beta_ok")
        self.fin_stats = sem("fin_stats")
        self.fin_root = sem("fin_root")
        self.fin_norm = sem("fin_norm")
        self.fin_ok = sem("fin_ok")
        self.stored = sem("stored")


def windows(ap, shifts, step):
    dims = list(ap.ap)
    return bass.AP(ap.tensor, ap.offset, [dims[0], [step, shifts], *dims[1:]])


def program(nc, x, src, dst, gnn_w1, gnn_b1, gnn_w2, gnn_b2, Wqkv, bqkv, Wproj, bproj, temperature,
            gate_w, gate_b, ffn_w1, ffn_b1, ffn_w2, ffn_b2, gamma, beta, out):
    ctx = ExitStack()
    with ctx:
        def sb(name, words):
            return ctx.enter_context(nc.sbuf_tensor(name, [128, words], F32))

        def sem(name):
            return ctx.enter_context(nc.semaphore(name))

        x_buf = sb("x_buf", T * D)
        node_buf = sb("node_buf", T * D)
        big = sb("big", NX * 2048)
        mid = sb("mid", 4352)
        const = Region(sb("const", 3288), 0, 3288)

        x_sb = x_buf[0:P, :].rearrange("p (t c) -> p t c", t=T)
        node = node_buf[:, :].rearrange("p (t c) -> p t c", t=T)

        xn_rows = node[0:P, T - G:T, :]

        ident = const.take([128])
        ident_h = const.take([128], BF16)
        iota_q = const.take([NQ], F16)
        iota_r = const.take([128], F16)
        iota_loc = const.take([P])
        iota_x = const.take([NX])
        tri = const.take([P], parts=P)
        tri_in = const.take([NB], parts=NB)
        ones = const.take([P])
        row0 = const.take([P], parts=P)
        head_mask = const.take([4])
        pair_w = const.take([4])
        sel = const.take([4, 128], BF16, parts=96)
        trash_pad = const.take([1])
        edges_at = const.at
        edge_idx = const.take([NQ], I32)
        edge_loc = const.take([NQ])
        edge_bucket = const.take([NQ], I32, parts=1)
        stats = const.take([T, 6], parts=P)
        mv = const.take([T, 2], parts=P)
        rstd = const.take([T], parts=P)
        eps_t = const.take([1], parts=P)
        temp_t = const.take([H], parts=P)
        gnn_b1T = const.take([2])
        gate_w_sb = const.take([2, NX])
        gate_b_bc = const.take([NX], parts=P)
        tok_val = const.take([T, 2], parts=P)
        tok_pick = const.take([T, 2], parts=P)
        logits = const.take([G, NX], parts=P)
        top_val = const.take([G, 8], parts=P)
        top_idx = const.take([G, 8], U32, parts=P)
        b1T = const.take([NX * 4])
        score = const.take([T, 2], parts=P)
        choice = const.take([T, 2], parts=P)
        weight = const.take([T, 2], parts=P)

        c = Region(const.tensor, edges_at, edges_at + 3 * NQ)
        tok_gather = c.take([NT], I32)
        tok_scatter = c.take([NT], I32)
        tok_expert = c.take([NT], I32, parts=1)
        last_slot = c.take([NX], parts=P)
        count_x = c.take([NX], parts=P)
        tiles_x = c.take([NX], parts=P)
        incl_x = c.take([NX], parts=P)
        off_x = c.take([NX], parts=P)
        col_x = c.take([1], parts=NX)
        ends_x = c.take([1], parts=NX)
        past_x = c.take([NT], parts=NX)
        pos_x = c.take([2 * T], parts=P)
        slot_qx = c.take([2 * T], parts=P)
        slot_rx = c.take([2 * T], parts=P)
        unused = c.take([NT])
        out_row = c.take([NT])
        trash = c.take([NT // 2, 2])

        m = Region(mid, 0, 4352)
        w1_sb = m.take([2, D])
        w2_sb = m.take([2, D])
        wqkvT = m.take([2, 3 * D])
        wprojT = m.take([2, D])
        bqkv_bc = m.take([3 * D], parts=P)
        b2_bc = m.take([D], parts=P)
        bsum_bc = m.take([D], parts=P)

        m = Region(mid, 4 * D, 4352)
        hT2 = m.take([2, 2, P])
        xn2 = m.take([G, D], parts=P)
        xn2T = m.take([2, 2, P])
        b1_rows = m.take([128], parts=NX * 4)
        m = Region(mid, 0, 4352)
        hot_x = m.take([NX, 2 * T], parts=P)
        run_x = m.take([NX, 2 * T], parts=P)
        hot_qx = m.take([2 * T, NT], F16, parts=P)
        m = Region(node_buf, 0, T * D)
        hot_rx = m.take([2 * T, 128], F16, parts=P)
        val_qx = m.take([2 * T, 2, NT], F16, parts=P)
        m = Region(mid, 0, 4352)
        tok_rows = m.take([4, D])
        tokT = m.take([2, 2, 128])
        hid = m.take([2, FF])
        hidT = m.take([2, 4, 128])
        y_rows = m.take([2, D])
        m = Region(node_buf, 0, T * D)
        b2_x = m.take([NX, D])
        gamma_bc = m.take([D], parts=P)
        beta_bc = m.take([D], parts=P)
        experts = big[:, :].rearrange("p (e n) -> p e n", e=NX)
        m = Region(big, 0, NX * 2048)
        pick0 = m.take([T, D], parts=P)
        pick1 = m.take([T, D], parts=P)
        own = m.take([T, D], parts=P)

        b = Region(big, 0, NX * 2048)
        qkv = b.take([T, 3 * D], parts=P)
        phase = b.at
        src_i = b.take([EC], I32, parts=P)
        dst_i = b.take([EC], I32, parts=P)
        loc_f = b.take([EC], parts=P)
        bkt_h = b.take([EC], F16, parts=P)
        pos = b.take([EC], parts=P)
        slot_q = b.take([EC], parts=P)
        slot_r = b.take([EC], parts=P)
        val_dst = b.take([EC], parts=P)
        val_loc = b.take([EC], parts=P)
        sorting = b.at
        wave_hot = b.take([G, EC], F16, parts=P)
        wave_at = b.at
        wave_pos = b.take([G, EC], parts=P)
        after = b.at
        b.at = sorting
        col_hot = [(b.take([NQ], F16, parts=P), b.take([128], F16, parts=P), b.take([128], F16, parts=P))
                   for _ in range(8)]
        b.at = max(b.at, after)
        xnT = b.take([G, 2, P])
        hT = b.take([G, 2, P])
        m_rows = b.take([G, D], parts=P)
        raw_w = b.take([8, D])
        wave_pos_flat = big[0:96, wave_at:wave_at + 512]
        cnt = b.take([NB], parts=P)
        n_tiles = b.take([NB], parts=P)
        incl = b.take([NB], parts=P)
        off = b.take([NB], parts=P)
        n_col = b.take([1], parts=NB)
        ends = b.take([1], parts=NB)
        bproj_bc = b.take([D], parts=P)
        past_end = raw_w.rearrange("p a b -> p (a b)")[0:NB, 0:NQ]
        sq = raw_w.rearrange("p a b -> p (a b)")[0:P, 512:1024]
        norm = raw_w.rearrange("p a b -> p (a b)")[0:P, 1024:1024 + T * 16].rearrange("p (t h) -> p t h", t=T)

        b = Region(big, phase, NX * 2048)
        msgs = b.take([GB, D])
        hot_src = b.take([2, GB, P])
        kv = b.take([H, 4, HV])
        kv_lin = b.take([2, 4 * HV])
        kv_diag = b.take([2, 4 * HV])
        v_sum = b.take([H * HV], parts=P)
        idx_ring = b.take([2, GB], I32)
        by_turn = b.at
        pairs = b.take([H, 512], parts=P)
        kd = b.take([2, H, 48], parts=P)
        k_row = b.take([2, H, DH], parts=P)
        v1 = b.take([2, H, HV], parts=P)
        k_diag = b.take([H, DH], parts=P)
        k_tmp = b.take([H, DH], parts=P)
        k_sum = b.take([H], parts=P)
        b.at = by_turn
        q_pairs = b.take([4, 4, P])
        q_row = b.take([H, DH], parts=P)
        q_rest = b.take([H, DH], parts=P)
        q_parts = b.take([H, 3, DH], BF16, parts=P)
        qT = b.take([H, 128], BF16, parts=96)
        q_lin = b.take([2, P])
        q_sq = b.take([2, P])
        y_rcp = b.take([H], parts=P)
        mix_row = b.take([H, DH], parts=P)
        mixT = b.take([2, P])

        bank = [ctx.enter_context(nc.psum_tensor(f"bank{i}", [128, 512], F32)) for i in range(8)]

        def bview(i, a, c, parts=128, at=0):
            return bank[i][0:parts, at:at + a * c].rearrange("p (a c) -> p a c", a=a)

        lin_ps = [bank[2][:, 264:264 + 4 * HV], bank[3][:, 264:264 + 4 * HV]]
        diag_ps = [bank[3][:, 0:4 * HV], bank[3][:, 4 * HV:8 * HV]]
        agg_ps = [bank[4 + k // 2][:, 256 * (k % 2):256 * (k % 2) + 2 * P] for k in range(4)]
        q_partsT_ps = bank[0][0:96, :].bitcast(BF16).rearrange("p (h n) -> p h n", h=H)

        msg_rows = nc.dram_tensor("msg_rows", (N, D), F32).ap()
        xn2_rows = nc.dram_tensor("xn2_rows", (N, D), F32).ap()
        moe_rows = nc.dram_tensor("moe_rows", (2 * N + 2 * SLOT, D), F32).ap()
        tiled = lambda rows: rows.rearrange("(p t) c -> p t c", t=T)

        s = Semaphores(sem)
        m_out = [sem(f"m_out{j}") for j in range(G)]
        msgs_in = [sem(f"msgs_in{k}") for k in range(GB)]
        tok_in = [sem(f"tok_in{k}") for k in range(4)]
        y_out = [sem(f"y_out{k}") for k in range(2)]
        fin_in = [sem(f"fin_in{g}") for g in range(T // G)]

        block = ctx.enter_context(nc.Block())

        def mixer_tiles(eng, tile):
            tile(0, 0)
            with eng.Fori(0, (T - 3) // 2) as i:
                tile(i * 2 + 1, 1)
                tile(i * 2 + 2, 0)
            tile(T - 2, 1)
            tile(T - 1, 0)

        def at(t, tiles):
            return isinstance(t, int) and t in tiles

        def apart(eng):
            eng.sem_inc(s.apart, 1)

        SMALL = [(bqkv_bc, bqkv.partition_broadcast(P)), (b2_bc, gnn_b2.partition_broadcast(P)),
                 (bsum_bc, gnn_b2.partition_broadcast(P)), (bproj_bc, bproj.partition_broadcast(P)),
                 (temp_t, temperature.rearrange("a h b c -> (a h b c)").partition_broadcast(P)),
                 *[(gnn_b1T[:, k:k + 1], gnn_b1[128 * k:128 * k + 128].rearrange("(p o) -> p o", o=1)) for k in range(2)]]

        @block.sync
        def _(sp):
            xt = tiled(x)
            def load_x(g):
                for lo, hi in ((0, 112), (112, P)):
                    sp.dma_start(x_sb[lo:hi, G * g:G * g + G, :], xt[lo:hi, G * g:G * g + G, :]).then_inc(s.x_in, 16)
            load_x(0)
            sp.dma_start(src_i, src.rearrange("(p e) -> p e", e=EC)).then_inc(s.edges_in, 16)
            sp.dma_start(dst_i, dst.rearrange("(p e) -> p e", e=EC)).then_inc(s.edges_in, 16)
            sp.dma_start(w1_sb, gnn_w1.rearrange("(k p) f -> p k f", p=128)).then_inc(s.gnn_in, 16)
            sp.dma_start(w2_sb, gnn_w2.rearrange("(k p) f -> p k f", p=128)).then_inc(s.gnn_in, 16)
            for g in range(1, T // G):
                sp.wait_ge(s.x_in, 32 * g)
                load_x(g)
                if g == 1:
                    sp.dma_start(raw_w[:, 0:6, :], Wqkv.rearrange("(k p) c -> p k c", p=128)).then_inc(s.raw_in, 16)
                    sp.dma_start(raw_w[:, 6:8, :], Wproj.rearrange("(k p) c -> p k c", p=128)).then_inc(s.raw_in, 16)
                    for view, dram in SMALL:
                        sp.dma_start(view, dram).then_inc(s.bias_in, 16)
            with sp.Fori(0, T // G) as g:
                for j in range(G):
                    sp.wait_ge(s.m_biased, g * G + j + 1)
                    sp.dma_start(tiled(msg_rows)[:, bass.ds(g * G + j, 1), :].rearrange("p a c -> p (a c)"),
                                 m_rows[:, j, :]).then_inc(m_out[j], 16)
            sp.dma_start(gate_w_sb, gate_w.rearrange("(k p) e -> p k e", p=128)).then_inc(s.gate_in, 16)
            sp.dma_start(gate_b_bc, gate_b.partition_broadcast(P)).then_inc(s.gate_in, 16)
            def load_expert(e):
                sp.dma_start(experts[:, e, 0:1024].rearrange("p (k f) -> p k f", k=2),
                             ffn_w1[e].rearrange("(k p) f -> p k f", p=128)).then_inc(s.w_in, 16)
                sp.dma_start(experts[:, e, 1024:2048].rearrange("p (c h) -> p c h", c=4),
                             ffn_w2[e].rearrange("(c p) h -> p c h", p=128)).then_inc(s.w_in, 16)

            sp.wait_ge(s.x_ok, T)
            sp.dma_start(b1_rows, ffn_b1.rearrange("e (c p) -> (e c) p", p=128)).then_inc(s.gate_in, 16)
            early = phase // 2048
            for e in range(early):
                load_expert(e)
            sp.wait_ge(s.agg_add, NBATCH * GB)
            for e in range(early, NX):
                load_expert(e)
            sp.wait_ge(s.tok_mm, 1)
            sp.dma_start(b2_x, ffn_b2.partition_broadcast(128)).then_inc(s.late_in, 16)
            sp.dma_start(gamma_bc, gamma.partition_broadcast(P)).then_inc(s.late_in, 16)
            sp.dma_start(beta_bc, beta.partition_broadcast(P)).then_inc(s.late_in, 16)
            for k in range(2):
                sp.wait_ge(y_out[k], 16 * (NT // 2))
            for g in range(T // G):
                rows = slice(G * g, G * g + G)
                for view, dram in ((pick0, moe_rows[0:N]), (pick1, moe_rows[N:2 * N]), (own, xn2_rows)):
                    for lo, hi in ((0, 112), (112, P)):
                        sp.dma_start(view[lo:hi, rows, :], tiled(dram)[lo:hi, rows, :]).then_inc(fin_in[g], 16)
            for g in range(T // G):
                rows = slice(G * g, G * g + G)
                sp.wait_ge(s.fin_ok, G * g + G)
                for lo, hi in ((0, 112), (112, P)):
                    sp.dma_start(tiled(out)[lo:hi, rows, :], pick0[lo:hi, rows, :]).then_inc(s.stored, 16)
            sp.wait_ge(s.stored, 32 * (T // G))

        @block.gpsimd
        def _(pool):
            chain = Chain(pool, s.pool_chain)
            def zero(ap):
                chain.add(pool.memset(ap, 0.0))
            zero(ident)
            zero(tri)
            zero(tri_in)
            zero(row0)
            zero(head_mask)
            pool.memset(ones, 1.0)
            pool.memset(eps_t, LN_EPS)
            chain.add(pool.memset(pair_w, 0.5 / N))
            pool.iota(iota_q, [[1, NQ]], base=0, channel_multiplier=0, allow_small_or_imprecise_dtypes=True)
            pool.iota(iota_r, [[1, 128]], base=0, channel_multiplier=0, allow_small_or_imprecise_dtypes=True)
            pool.iota(iota_loc, [[1, P]], base=1, channel_multiplier=0, allow_small_or_imprecise_dtypes=True)
            pool.iota(iota_x, [[1, NX]], base=0, channel_multiplier=0, allow_small_or_imprecise_dtypes=True)
            pool.iota(tok_val, [[1, T], [0, 2]], base=-MID, channel_multiplier=T, allow_small_or_imprecise_dtypes=True)
            pool.iota(tok_pick, [[0, T], [1, 2]], base=1, channel_multiplier=0, allow_small_or_imprecise_dtypes=True)
            chain.wait()
            pool.affine_select(out=ident, in_=ident, compare_op=ALU.not_equal, fill=1.0, base=0,
                               pattern=[[-1, 128]], channel_multiplier=1)
            pool.affine_select(out=tri, in_=tri, compare_op=ALU.is_ge, fill=1.0, base=0,
                               pattern=[[-1, P]], channel_multiplier=1)
            pool.affine_select(out=tri_in, in_=tri_in, compare_op=ALU.is_gt, fill=1.0, base=0,
                               pattern=[[-1, NB]], channel_multiplier=1)
            pool.affine_select(out=row0, in_=row0, compare_op=ALU.is_gt, fill=1.0, base=0,
                               pattern=[[0, P]], channel_multiplier=1)
            def alone(ins):
                chain.add(ins)
                chain.wait()

            alone(pool.memset(trash_pad, 0.0))
            for h in range(4):
                alone(pool.memset(head_mask[32 * h:32 * h + 32, h:h + 1], 1.0))
            alone(pool.memset(pair_w[96:128, 3:4], 0.25 / N))
            pool.tensor_copy(ident_h, ident).then_inc(s.consts, 1)
            selw = wave_pos_flat
            chain.add(pool.memset(selw, 0.0))
            chain.wait()
            for base, step in ((0, 0), (-1, -1), (31, -1)):
                for k in range(3):
                    v = selw[32 * k:32 * k + 32, :].rearrange("p (d i) -> p d i", i=32)
                    alone(pool.affine_select(out=v, in_=v, compare_op=ALU.not_equal, fill=1.0, base=base,
                                             pattern=[[step, 16], [-1, 32]], channel_multiplier=1))
            pool.tensor_copy(sel.rearrange("p a b -> p (a b)"), selw).then_inc(s.preps, 1)
            pool.wait_ge(s.bias_in, 16 * len(SMALL))
            pool.tensor_tensor(bsum_bc, bsum_bc, bproj_bc, ALU.add).then_inc(s.preps, 1)
            pool.tensor_scalar(temp_t, temp_t, SCALE2, None, ALU.mult).then_inc(s.preps, 1)
            with pool.Fori(0, T // G) as g:
                for j in range(G):
                    t = g * G + j
                    pool.wait_ge(s.xnT_ready, t + 1)
                    pool.tensor_copy(node[:, bass.ds(t, 1), :].rearrange("p a c -> p (a c)")[:, 0:2 * P],
                                     xnT[:, j, :, :].rearrange("p k n -> p (k n)")).then_inc(s.hT_copied, 1)
                    pool.wait_ge(s.qkv_evac, t + 1)
                    row = qkv[:, bass.ds(t, 1), :].rearrange("p a c -> p (a c)")
                    pool.tensor_tensor(row, row, bqkv_bc, ALU.add).then_inc(s.qkv_biased, 1)
                    pool.wait_ge(s.m_evac, t + 1)
                    pool.tensor_tensor(m_rows[:, j, :], m_rows[:, j, :], b2_bc, ALU.add).then_inc(s.m_biased, 1)
            pool.wait_ge(s.qkv_biased, T)
            pool.wait_ge(s.preps, 3)
            with pool.Fori(0, T) as t:
                chain.enter(t, 0, 6)
                qk = qkv[:, bass.ds(t, 1), 0:2 * D].rearrange("p a c -> p (a c)")
                chain.add(pool.tensor_tensor(sq, qk, qk, ALU.mult))
                rows = x_sb[:, bass.ds(t, 1), :].rearrange("p a c -> p (a c)")
                pool.tensor_tensor(rows, rows, bsum_bc, ALU.add)
                part = sq.rearrange("p (h d) -> p h d", h=2 * H)
                for w in (16, 8, 4, 2):
                    chain.wait()
                    chain.add(pool.tensor_tensor(part[:, :, 0:w], part[:, :, 0:w], part[:, :, w:2 * w], ALU.add))
                chain.wait()
                chain.add(pool.tensor_tensor(norm[:, bass.ds(t, 1), :].rearrange("p a h -> p (a h)").unsqueeze(2),
                                             part[:, :, 0:1], part[:, :, 1:2], ALU.add))
                chain.wait()
            chain.leave(T)
            chain.wait()
            pool.memset(sq[:, 0:1], 0.0).then_inc(s.norm_sum, 1)
            pool.wait_ge(s.norm_ok, 1)
            with pool.Fori(0, T) as t:
                qk = qkv[:, bass.ds(t, 1), 0:2 * D].rearrange("p a (h d) -> p (a h) d", d=DH)
                by = norm[:, bass.ds(t, 1), :].rearrange("p a h -> p (a h)").unsqueeze(2).broadcast_to([P, 2 * H, DH])
                pool.tensor_tensor(qk, qk, by, ALU.mult).then_inc(s.normed, 1)
            for j in range(G):
                pool.wait_ge(m_out[j], 16 * (T // G))
            pool.wait_ge(s.sorted_ok, 1)
            pool.wait_ge(s.normed, T)
            chain.add(pool.memset(v1[:, :, :, 0:1], 1.0))
            chain.wait()
            pool.memset(trash_pad, 0.0).then_inc(s.v1_ones, 1)

            def gather_batch(n, half, first=False):
                pool.tensor_copy(idx_ring[:, half, :], edge_idx[:, bass.ds(n * GB, GB)]).then_inc(s.msg_idx_ok, 1)
                pool.wait_ge(s.msg_idx_ok, n + 1)
                for k in range(GB):
                    if not first:
                        pool.wait_ge(s.agg_mm, n * GB + k - (GB - 1))
                        apart(pool)
                    pool.indirect_dma_start(msgs[:, k, :], None, msg_rows,
                                            bass.IndirectOffsetOnAxis(idx_ring[:, half, k:k + 1], 0)).then_inc(msgs_in[k], 16)

            gather_batch(0, 0, first=True)
            gather_batch(1, 1)
            with pool.Fori(1, NBATCH // 2) as i:
                gather_batch(i * 2, 0)
                gather_batch(i * 2 + 1, 1)
            pool.wait_ge(s.agg_add, NBATCH * GB)
            pool.iota(trash, [[0, NT // 2], [SLOT, 2]], base=3 * N - MID, channel_multiplier=1,
                      allow_small_or_imprecise_dtypes=True).then_inc(s.trash_ok, 1)
            with pool.Fori(0, T // G) as g:
                pool.wait_ge(s.xn2_ok, g * G + G)
                pool.dma_start(tiled(xn2_rows)[:, bass.ds(g * G, G), :], xn2).then_inc(s.xn2_out, 16)
            pool.wait_ge(s.xn2_out, 16 * (T // G))
            pool.wait_ge(s.tok_ok, 1)
            pool.wait_ge(s.tok_mm, 1)

            def gather_tokens(n):
                if n >= 4:
                    pool.wait_ge(s.tokT_mm, n - 3)
                pool.indirect_dma_start(tok_rows[:, n % 4, :], None, xn2_rows,
                                        bass.IndirectOffsetOnAxis(tok_gather[:, n:n + 1], 0)).then_inc(tok_in[n % 4], 16)

            for n in range(4):
                gather_tokens(n)
            for n in range(NT):
                if n + 4 < NT:
                    gather_tokens(n + 4)
                pool.wait_ge(s.y_ok, n + 1)
                pool.indirect_dma_start(moe_rows, bass.IndirectOffsetOnAxis(tok_scatter[:, n:n + 1], 0),
                                        y_rows[:, n % 2, :], None).then_inc(y_out[n % 2], 16)
                if n == 8:
                    pool.wait_ge(s.late_in, 48)
                    with pool.Fori(0, T) as t:
                        rows = x_sb[:, bass.ds(t, 1), :].rearrange("p a c -> p (a c)")
                        pool.tensor_tensor(rows, rows, beta_bc, ALU.add).then_inc(s.beta_ok, 1)
            pool.wait_ge(s.beta_ok, T)
            for t in range(T):
                pool.wait_ge(s.fin_norm, t + 1)
                chain.add(pool.tensor_tensor(pick0[:, t, :], pick0[:, t, :], gamma_bc, ALU.mult))
                chain.wait()
                pool.tensor_tensor(pick0[:, t, :], pick0[:, t, :], x_sb[:, t, :], ALU.add).then_inc(s.fin_ok, 1)

        @block.scalar
        def _(act):
            act.wait_ge(s.consts, 1)
            def root(lo, hi, n):
                act.wait_ge(s.ln_stats, n)
                act.activation(rstd[:, lo:hi], mv[:, lo:hi, 1], ACT.Sqrt, bias=eps_t).then_inc(s.rstd_sd, 1)

            root(0, G, 1)
            for k in range(4):
                act.wait_ge(s.wT_mm, k + 1)
                got = bview(4 + k, 4, 128)
                if k < 3:
                    for i in range(2):
                        last = act.activation(wqkvT[:, :, (2 * k + i) * 128:(2 * k + i + 1) * 128],
                                              got[:, 2 * i:2 * i + 2, :], ACT.Copy)
                else:
                    for i in range(2):
                        last = act.activation(wprojT[:, :, i * 128:(i + 1) * 128], got[:, 2 * i:2 * i + 2, :], ACT.Copy)
                last.then_inc(s.act_chain, 1)

            def evac_xnT(g, j):
                act.wait_ge(s.xnT_mm, g * G + j + 1)
                if j == 0:
                    act.wait_ge(s.qkv_mm, g * G)
                    act.wait_ge(s.hT_copied, g * G)
                act.activation(xnT[:, j, :, :], bview(j % 2, 2, P), ACT.Copy).then_inc(s.xnT_ready, 1)

            act.wait_ge(s.gnn_in, 32)
            act.wait_ge(s.bias_in, 16 * len(SMALL))
            def front(lo, hi):
              with act.Fori(lo, hi) as g:
                evac_xnT(g, 0)
                for j in range(G):
                    t = g * G + j
                    act.wait_ge(s.l1_mm, t + 1)
                    for k in range(2):
                        last = act.activation(hT[:, j, k, :], bview(2 + j % 2, 2, P)[:, k, :], ACT.Relu, bias=gnn_b1T[:, k:k + 1])
                    last.then_inc(s.h_ready, 1)
                    if j < G - 1:
                        evac_xnT(g, j + 1)
                    act.wait_ge(s.qkv_mm, t + 1)
                    for half in range(2):
                        last = act.activation(qkv[:, bass.ds(t, 1), 384 * half:384 * half + 384].rearrange("p a c -> p (a c)"),
                                              bank[5 + half][0:P, 0:384], ACT.Copy)
                    last.then_inc(s.qkv_evac, 1)
                    act.wait_ge(s.m_mm, t + 1)
                    act.wait_ge(m_out[j], g * 16)
                    act.activation(m_rows[:, j, :], bank[4][0:P, 0:D], ACT.Copy).then_inc(s.m_evac, 1)
            front(0, 1)
            root(G, T, 2)
            front(1, T // G)
            act.wait_ge(s.norm_sum, 1)
            act.activation(norm[:, :, 0:H], norm[:, :, 0:H], ACT.Sqrt, scale=SCALE2 * 1.0)
            act.activation(norm[:, :, H:2 * H], norm[:, :, H:2 * H], ACT.Sqrt).then_inc(s.norm_root, 1)

            def heads_of(t, part):
                return qkv[:, bass.ds(t, 1), D * part:D * part + D].rearrange("p a (h d) -> p (a h) d", h=H)

            act.wait_ge(s.sorted_ok, 1)
            act.wait_ge(s.normed, T)
            act.wait_ge(s.v1_ones, 1)

            def k_rows(t, turn):
                if not at(t, (0, 1)):
                    act.wait_ge(s.pairs_ok, t * H - H)
                    act.wait_ge(s.k_diag_ok, t - 1)
                    act.wait_ge(s.lin_mm, t - 1)
                act.activation(k_row[:, turn, :, :], heads_of(t, 1), ACT.Copy)
                act.activation(kd[:, turn, :, 0:DH], heads_of(t, 1), ACT.Copy)
                act.activation(kd[:, turn, :, DH:48], heads_of(t, 1)[:, :, 0:16], ACT.Copy).then_inc(s.kd_ok, 1)
                if not at(t, (0, 1)):
                    act.wait_ge(s.head_mm, t * H - H)
                    act.wait_ge(s.diag_mm, t - 1)
                act.activation(v1[:, turn, :, 1:HV], heads_of(t, 2), ACT.Copy).then_inc(s.v1_ok, 1)

            mixer_tiles(act, k_rows)

            def q_row_of(t):
                if not at(t, (0,)):
                    act.wait_ge(s.split_ok, t)
                    act.wait_ge(s.qnT_mm, t)
                act.activation(q_row, heads_of(t, 0), ACT.Copy).then_inc(s.q_row_ok, 1)

            def qT_of(t):
                act.wait_ge(s.q_partsT_mm, t + 1)
                if not at(t, (0,)):
                    act.wait_ge(s.sel_mm, t * H)
                act.activation(qT[:, :, 0:P], q_partsT_ps[:, :, 0:P], ACT.Copy).then_inc(s.qT_ok, 1)
                act.wait_ge(s.qnT_mm, t + 1)
                if not at(t, (0,)):
                    act.wait_ge(s.y_ld_mm, t)
                act.activation(q_lin, bview(1, 2, P), ACT.Copy)
                act.activation(q_sq, bview(1, 2, P), ACT.Square).then_inc(s.q_ld_ok, 1)

            def mixT_of(t):
                act.wait_ge(s.mixT_mm, t + 1)
                act.activation(mixT, bview(6, 2, P), ACT.Copy).then_inc(s.mixT_ok, 1)

            def q_tile(t, turn):
                if not at(t, (T - 1,)):
                    q_row_of(t + 1)
                for h in range(H):
                    act.wait_ge(s.sel_mm, t * H + h + 1)
                    if not (at(t, (0,)) and h < 4):
                        act.wait_ge(s.y_mm, t * H + h - 3)
                    act.activation(q_pairs[:, h % 4, :, :], bview(2 + h % 2, 4, P), ACT.Square).then_inc(s.q_pairs_ok, 1)
                    if h == 1 and not at(t, (0,)):
                        mixT_of(t - 1)
                if not at(t, (T - 1,)):
                    qT_of(t + 1)

            act.wait_ge(s.kv_ok, 1)
            q_row_of(0)
            qT_of(0)
            mixer_tiles(act, q_tile)
            mixT_of(T - 1)

            act.wait_ge(s.b1_mm, 1)
            act.activation(b1T, bank[7][:, 0:NX * 4], ACT.Copy).then_inc(s.b1_ok, 1)

            def second_pass(g):
                for j in range(G):
                    t = g * G + j
                    act.wait_ge(s.f1_mm, t + 1)
                    act.wait_ge(s.f2_mm, t - 1 if j >= 2 else g * G)
                    for k in range(2):
                        last = act.activation(hT2[:, j % 2, k, :], bview(j % 2, 2, P)[:, k, :], ACT.Relu, bias=gnn_b1T[:, k:k + 1])
                    last.then_inc(s.h2_ok, 1)
                act.wait_ge(s.ln2_stats, g + 1)
                act.activation(rstd[:, 0:G], mv[:, 0:G, 1], ACT.Sqrt, bias=eps_t).then_inc(s.ln2_root, 1)

            def xn2T_of(g):
                for j in range(G):
                    t = g * G + j
                    act.wait_ge(s.xn2T_mm, t + 1)
                    act.wait_ge(s.gate_mm, t - 1 if j >= 2 else g * G)
                    act.activation(xn2T[:, j % 2, :, :], bview(3 + j % 2, 2, P), ACT.Copy).then_inc(s.xn2T_ok, 1)

            second_pass(0)
            with act.Fori(1, T // G) as g:
                second_pass(g)
                xn2T_of(g - 1)
            xn2T_of(T // G - 1)
            act.wait_ge(s.gap_ok, 1)
            act.activation(weight[:, :, 1:2], weight[:, :, 0:1], ACT.Exp).then_inc(s.exp_ok, 1)

            act.wait_ge(s.tok_ok, 1)
            act.wait_ge(s.b1_ok, 1)

            def relu_tile(i, j, expert):
                n = i * 4 + 1 + j
                act.wait_ge(s.hidT_mm, n + 1)
                if not (isinstance(i, int) and n < 2):
                    act.wait_ge(s.ffn2_mm, n - 1)
                apart(act)
                for c in range(4):
                    last = act.activation(hidT[:, (1 + j) % 2, c, :], bview(4 + (1 + j) % 2, 4, 128)[:, c, :], ACT.Relu,
                                          bias=b1T[:, bass.ds(expert * 4 + c, 1)])
                last.then_inc(s.relu_ok, 1)

            def hid_tile(i, j):
                n = i * 4 + 2 + j
                act.wait_ge(s.ffn1_mm, n + 1)
                if not (isinstance(i, int) and n < 2):
                    act.wait_ge(s.hidT_mm, n - 1)
                act.activation(hid[:, j % 2, :], bank[2 + j % 2][:, :], ACT.Copy).then_inc(s.hid_ok, 1)

            def chosen(at, count):
                return nc.values_load_multi_w_load_instructions(
                    tok_expert[:, bass.ds(at, count)], engines=[mybir.EngineType.Activation], min_val=0, max_val=NX - 1,
                    skip_runtime_bounds_check_because="clamped to the last expert when written")[1]

            e = chosen(0, 1)
            hid_tile(-1, 2)
            hid_tile(-1, 3)
            relu_tile(-1, 3, e[0])
            with act.Fori(0, (NT - 4) // 4) as i:
                e = chosen(i * 4 + 1, 4)
                for j in range(4):
                    hid_tile(i, j)
                    relu_tile(i, j, e[j])
            i = (NT - 4) // 4
            e = chosen(NT - 3, 3)
            for j in range(2):
                hid_tile(i, j)
                relu_tile(i, j, e[j])
            relu_tile(i, 2, e[2])
            for g in range(T // G):
                act.wait_ge(s.fin_stats, g + 1)
                act.activation(rstd[:, g * G:g * G + G], mv[:, g * G:g * G + G, 1], ACT.Sqrt, bias=eps_t).then_inc(s.fin_root, 1)

        @block.vector
        def _(dve):
            chain = Chain(dve, s.dve_chain)
            def step(ins):
                chain.add(ins)
                chain.wait()

            def moments(lo, hi):
                for t in range(lo, hi):
                    if t % G == 0:
                        dve.wait_ge(s.x_in, 32 * (t // G + 1))
                    last = dve.bn_stats(stats[:, t, :], x_sb[:, t, :])
                step(last)
                for t in range(lo, hi):
                    last = dve.bn_aggr(mv[:, t, :], stats[:, t, :])
                last.then_inc(s.ln_stats, 1)

            def inverse(lo, hi, n):
                dve.wait_ge(s.rstd_sd, n)
                step(dve.reciprocal(rstd[:, lo:hi], rstd[:, lo:hi]))

            def normalise(g):
                if g:
                    dve.wait_ge(s.xnT_mm, G * g)
                for j in range(G):
                    t = g * G + j
                    dve.tensor_scalar(xn_rows[:, j, :], x_sb[:, t, :], mv[:, t, 0:1], rstd[:, t:t + 1],
                                      ALU.subtract, ALU.mult).then_inc(s.xn_ready, 1)

            moments(0, G)
            inverse(0, G, 1)
            normalise(0)
            moments(G, T)
            inverse(G, T, 2)
            dve.wait_ge(s.edges_in, 32)
            step(dve.tensor_scalar(loc_f, src_i, 0.5, 1.0 / T, ALU.add, ALU.mult))
            step(dve.tensor_scalar(loc_f, loc_f, -0.5, MAGIC, ALU.add, ALU.add))
            step(dve.tensor_scalar(loc_f, loc_f, MAGIC, None, ALU.subtract))
            step(dve.scalar_tensor_tensor(bkt_h, loc_f, -float(T), src_i, ALU.mult, ALU.add))
            dve.tensor_scalar(val_dst, dst_i, -float(MID), None, ALU.add)
            dve.tensor_scalar(val_loc, loc_f, 1.0, None, ALU.add)
            for w in range(NB // G):
                for j in range(G):
                    last = dve.tensor_scalar(wave_hot[:, j, :], bkt_h, float(w * G + j), 0.0, ALU.is_equal, ALU.add,
                                             accum_out=cnt[:, w * G + j:w * G + j + 1])
                chain.add(last)
                if w < NB // G - 1:
                    chain.wait()
            chain.wait()
            dve.memset(pos, 0.0).then_inc(s.cnt_ok, 1)
            normalise(1)
            dve.wait_ge(s.prefix_mm, 1)
            before, total, col = bank[7][0:P, 0:NB], bank[7][0:P, 64:64 + NB], bank[7][0:NB, 128:129]
            half = (SLOT - 1) / 2.0
            for dst_, src_ in ((n_tiles, total), (n_col, col)):
                chain.add(dve.tensor_scalar(dst_, src_, half, 1.0 / SLOT, ALU.add, ALU.mult))
            chain.wait()
            for dst_ in (n_tiles, n_col):
                chain.add(dve.tensor_scalar(dst_, dst_, MAGIC, None, ALU.add))
            chain.wait()
            chain.add(dve.tensor_scalar(n_tiles, n_tiles, MAGIC, None, ALU.subtract))
            dve.tensor_scalar(n_col, n_col, MAGIC, None, ALU.subtract).then_inc(s.n_col_ok, 1)
            chain.wait()
            step(dve.tensor_tensor_scan(incl, ones[0:P, 0:NB], n_tiles, 0.0, ALU.mult, ALU.add))
            step(dve.tensor_tensor(incl, incl, n_tiles, ALU.subtract))
            step(dve.scalar_tensor_tensor(off, incl, float(SLOT), before, ALU.mult, ALU.add))
            step(dve.tensor_scalar(off, off, -1.0, None, ALU.add))
            dve.wait_ge(s.preps, 1)
            for w in range(NB // G):
                if w in (1, 2, 4):
                    normalise({1: 2, 2: 3, 4: 4}[w])
                for j in range(G):
                    last = dve.tensor_scalar(wave_hot[:, j, :], bkt_h, float(w * G + j), None, ALU.is_equal)
                step(last)
                for j in range(G):
                    last = dve.tensor_tensor_scan(wave_pos[:, j, :], ones[0:P, 0:1].broadcast_to([P, EC]), wave_hot[:, j, :],
                                                  off[:, w * G + j:w * G + j + 1], ALU.mult, ALU.add)
                step(last)
                step(dve.tensor_tensor(wave_pos, wave_pos, wave_hot, ALU.mult))
                for j in range(G):
                    step(dve.tensor_tensor(pos, pos, wave_pos[:, j, :], ALU.add))
            step(dve.tensor_scalar(slot_q, pos, -half, 1.0 / SLOT, ALU.add, ALU.mult))
            step(dve.tensor_scalar(slot_q, slot_q, MAGIC, None, ALU.add))
            step(dve.tensor_scalar(slot_q, slot_q, MAGIC, None, ALU.subtract))
            step(dve.scalar_tensor_tensor(slot_r, slot_q, -float(SLOT), pos, ALU.mult, ALU.add))
            def columns(i, first=False):
                for c in range(16):
                    hot_q, hot_d, hot_l = col_hot[c % 8]
                    at = lambda a: a[:, bass.ds(i * 16 + c, 1)]
                    if c >= 8 or not first:
                        dve.wait_ge(s.col_mm, i * 16 + c - 7)
                    dve.tensor_scalar(hot_q, iota_q[0:P, :], at(slot_q), None, ALU.is_equal)
                    dve.tensor_scalar(hot_d, iota_r[0:P, :], at(slot_r), at(val_dst), ALU.is_equal, ALU.mult)
                    dve.tensor_scalar(hot_l, iota_r[0:P, :], at(slot_r), at(val_loc), ALU.is_equal, ALU.mult).then_inc(s.col_hot_ok, 1)

            columns(0, True)
            with dve.Fori(1, 16) as i:
                columns(i)
            dve.wait_ge(s.norm_root, 1)
            step(dve.tensor_scalar(norm, norm, 1e-12, None, ALU.max))
            step(dve.reciprocal(norm, norm))
            dve.tensor_tensor(norm[:, :, 0:H], norm[:, :, 0:H], temp_t.unsqueeze(1).broadcast_to([P, T, H]), ALU.mult)
            dve.tensor_scalar(norm[:, :, H:2 * H], norm[:, :, H:2 * H], SCALE2 ** 0.5, None, ALU.mult).then_inc(s.norm_ok, 1)
            with dve.Fori(16, T) as i:
                columns(i)
            dve.wait_ge(s.ends_mm, 1)
            step(dve.tensor_copy(ends, bank[7][0:NB, 0:1]))
            dve.tensor_scalar(past_end, iota_q[0:NB, :], ends, None, ALU.is_ge).then_inc(s.past_ok, 1)
            dve.wait_ge(s.bucket_mm, 1)
            dve.tensor_scalar(edge_bucket, bank[6][0:1, 0:NQ], float(NB - 1), None, ALU.min)
            dve.wait_ge(s.sorted_mm, 1)
            dve.tensor_scalar(edge_idx, bank[0][:, 0:NQ], float(MID), None, ALU.add)
            dve.tensor_copy(edge_loc, bank[1][:, 0:NQ]).then_inc(s.sorted_ok, 1)

            def hot_batch(n, turn):
                dve.tensor_tensor(hot_src[:, turn, :, :], iota_loc.unsqueeze(1).broadcast_to([128, GB, P]),
                                  edge_loc[:, bass.ds(n * GB, GB)].unsqueeze(2).broadcast_to([128, GB, P]),
                                  ALU.is_equal).then_inc(s.hot_src_ok, 1)

            def buckets(m, count):
                return nc.values_load_multi_w_load_instructions(
                    edge_bucket[:, bass.ds(m, count)], engines=[mybir.EngineType.DVE], min_val=0, max_val=NB - 1,
                    skip_runtime_bounds_check_because="clamped to the last bucket when written")[1]

            def buckets_of(n):
                return [None] * LAG + list(buckets(0, GB - LAG)) if at(n, (0,)) else buckets(n * GB - LAG, GB)

            def add_pair(n, k, bucket):
                if k % 2 == 0 or bucket[k] is None:
                    return
                dve.wait_ge(s.agg_mm, n * GB + k + 1 - LAG)
                for j in (k - 1, k):
                    m = n * GB + j - LAG
                    if not at(m, (0,)):
                        dve.wait_ge(s.agg_add, m)
                    rows = node[:, bass.ds(bucket[j], 1), 0:2 * P].rearrange("p a c -> p (a c)")
                    dve.tensor_tensor(rows, rows, agg_ps[(j - LAG) % 4], ALU.add).then_inc(s.agg_add, 1)

            def k_tile(t, turn):
                bucket = buckets_of(t)
                dve.wait_ge(s.kd_ok, t + 1)
                k = kd[:, turn, :, :]
                for h in range(H):
                    if not at(t, (0,)):
                        dve.wait_ge(s.head_mm, t * H + h - (H - 1))
                    dve.tensor_tensor(pairs[:, h, :].rearrange("p (d i) -> p d i", i=DH),
                                      k[:, h, 0:DH].unsqueeze(1).broadcast_to([P, 16, DH]),
                                      windows(k[:, h, 1:DH + 1], 16, 1), ALU.mult).then_inc(s.pairs_ok, 1)
                    if h == 0:
                        chain.add(dve.reduce_sum(k_sum, k[:, :, 0:DH], axis=AX.X))
                    if h == 1:
                        chain.wait()
                        chain.add(dve.scalar_tensor_tensor(k_tmp, k[:, :, 0:DH], 2.0,
                                                           k_sum.unsqueeze(2).broadcast_to([P, H, DH]), ALU.mult, ALU.subtract))
                    if h == 2:
                        chain.wait()
                        if not at(t, (0,)):
                            dve.wait_ge(s.diag_mm, t)
                        dve.tensor_tensor(k_diag, k[:, :, 0:DH], k_tmp, ALU.mult).then_inc(s.k_diag_ok, 1)
                    add_pair(t, h, bucket)
                    if h == 3:
                        hot_batch(t + 1, 1 - turn)

            def chained(tile, per):
                def run(t, turn):
                    if isinstance(t, int):
                        tile(t, turn)
                    else:
                        if turn == 1:
                            chain.enter(t, 1, per)
                        start = chain.n
                        tile(t, turn)
                        assert chain.n - start == per
                        if turn == 0:
                            chain.n -= per
                            chain.leave(T - 3)
                return run

            dve.wait_ge(s.sorted_ok, 1)
            dve.wait_ge(s.normed, T)
            dve.wait_ge(s.v1_ones, 1)
            dve.wait_ge(s.hT_copied, T)
            hot_batch(0, 0)
            mixer_tiles(dve, chained(k_tile, 2))
            dve.wait_ge(s.head_mm, T * H)
            dve.wait_ge(s.diag_mm, T)
            for i in range(3):
                n = min(3, H - 3 * i)
                dve.tensor_tensor(kv[:, 3 * i:3 * i + n, :, :],
                                  bank[i][:, 0:n * 4 * HV].rearrange("p (h c e) -> p h c e", h=n, c=4),
                                  pair_w.unsqueeze(1).unsqueeze(3).broadcast_to([128, n, 4, HV]), ALU.mult)
            for i in range(2):
                mask = head_mask.unsqueeze(2).broadcast_to([128, 4, HV])
                dve.scalar_tensor_tensor(kv_lin[:, i, :].rearrange("p (h e) -> p h e", h=4),
                                         lin_ps[i].rearrange("p (h e) -> p h e", h=4), SCALE2 / N, mask, ALU.mult, ALU.mult)
                dve.scalar_tensor_tensor(kv_diag[:, i, :].rearrange("p (h e) -> p h e", h=4),
                                         diag_ps[i].rearrange("p (h e) -> p h e", h=4), 0.5 / N, mask, ALU.mult, ALU.mult)
            dve.tensor_scalar(v_sum, bank[6][0:P, 0:H * HV], SCALE2 ** 2 / N, None, ALU.mult).then_inc(s.kv_ok, 1)

            def split(t, part):
                if part == 0:
                    dve.wait_ge(s.q_row_ok, t + 1)
                    if not at(t, (0,)):
                        dve.wait_ge(s.q_partsT_mm, t)
                    chain.add(dve.tensor_copy(q_parts[:, :, 0, :], q_row))
                if part == 1:
                    chain.wait()
                    chain.add(dve.tensor_tensor(q_rest, q_row, q_parts[:, :, 0, :], ALU.subtract))
                if part == 2:
                    chain.wait()
                    chain.add(dve.tensor_copy(q_parts[:, :, 1, :], q_rest))
                if part == 3:
                    chain.wait()
                    dve.tensor_tensor(q_parts[:, :, 2, :], q_rest, q_parts[:, :, 1, :], ALU.subtract).then_inc(s.split_ok, 1)

            def add_mix(t):
                dve.wait_ge(s.proj_mm, t + 1)
                rows = x_sb[:, bass.ds(t, 1), :].rearrange("p a c -> p (a c)")
                dve.tensor_tensor(rows, rows, bank[6][0:P, 256:512], ALU.add).then_inc(s.x_ok, 1)

            def q_tile(t, turn):
                n = t + T
                bucket = buckets_of(n)
                for h in range(H):
                    add_pair(n, h, bucket)
                    if 0 <= h - 1 < 4 and not at(t, (T - 1,)):
                        split(t + 1, h - 1)
                    if h == 3:
                        hot_batch(n + 1, turn)
                    if h == 6 and not at(t, (0,)):
                        add_mix(t - 1)
                dve.wait_ge(s.y_mm, t * H + H)
                y = bank[7][0:P, 0:H * HV].rearrange("p (h e) -> p h e", h=H)
                chain.add(dve.reciprocal(y_rcp.unsqueeze(2), y[:, :, 0:1]))
                chain.wait()
                if not at(t, (0,)):
                    dve.wait_ge(s.mixT_mm, t)
                dve.tensor_tensor(mix_row, y[:, :, 1:HV], y_rcp.unsqueeze(2).broadcast_to([P, H, DH]),
                                  ALU.mult).then_inc(s.mix_row_ok, 1)

            for part in range(4):
                split(0, part)
            mixer_tiles(dve, chained(q_tile, 4))
            add_mix(T - 1)
            for n in range(2 * T, NBATCH):
                bucket = buckets_of(n)
                for k in range(GB):
                    add_pair(n, k, bucket)
                    if k == 3 and n < NBATCH - 1:
                        hot_batch(n + 1, (n + 1) % 2)
            bucket = buckets(NQ - LAG, LAG)
            for k in range(LAG):
                add_pair(NBATCH, k, bucket)

            def second_pass(g, first=False):
                for j in range(G):
                    t = g * G + j
                    dve.wait_ge(s.f2_mm, t + 1)
                    rows = x_sb[:, bass.ds(t, 1), :].rearrange("p a c -> p (a c)")
                    dve.tensor_tensor(rows, rows, bank[2][0:P, 0:D], ALU.add).then_inc(s.x2_add, 1)
                    dve.wait_ge(s.x2_add, t + 1)
                    apart(dve)
                    last = dve.bn_stats(stats[:, j, :], rows)
                chain.add(last)
                chain.wait()
                apart(dve)
                for j in range(G):
                    last = dve.bn_aggr(mv[:, j, :], stats[:, j, :])
                last.then_inc(s.ln2_stats, 1)
                dve.wait_ge(s.ln2_root, g + 1)
                chain.add(dve.reciprocal(rstd[:, 0:G], rstd[:, 0:G]))
                chain.wait()
                dve.wait_ge(s.xn2T_mm, g * G)
                dve.wait_ge(s.xn2_out, g * 16)
                for j in range(G):
                    t = g * G + j
                    rows = x_sb[:, bass.ds(t, 1), :].rearrange("p a c -> p (a c)")
                    dve.tensor_scalar(xn2[:, j, :], rows, mv[:, j, 0:1], rstd[:, j:j + 1], ALU.subtract,
                                      ALU.mult).then_inc(s.xn2_ok, 1)

            def choose(g):
                dve.wait_ge(s.gate_mm, g * G + G)
                dve.tensor_tensor(logits, bview(5, G, NX, P), gate_b_bc.unsqueeze(1).broadcast_to([P, G, NX]),
                                  ALU.add).then_inc(s.gate_ok, 1)
                dve.wait_ge(s.gate_ok, g + 1)
                apart(dve)
                for j in range(G):
                    last = dve.max(top_val[:, j, :], logits[:, j, :])
                chain.add(last)
                chain.wait()
                apart(dve)
                for j in range(G):
                    last = dve.max_index(top_idx[:, j, :], top_val[:, j, :], logits[:, j, :])
                chain.add(last)
                chain.wait()
                dve.tensor_copy(score[:, bass.ds(g * G, G), :], top_val[:, :, 0:2])
                chain.add(dve.tensor_copy(choice[:, bass.ds(g * G, G), :], top_idx[:, :, 0:2]))
                chain.wait()

            dve.wait_ge(s.gate_in, 32)
            second_pass(0)
            with dve.Fori(1, T // G) as g:
                chain.enter(g, 1, 5)
                second_pass(g)
                choose(g - 1)
            chain.leave(T // G - 1)
            choose(T // G - 1)
            dve.tensor_tensor(weight[:, :, 0:1], score[:, :, 1:2], score[:, :, 0:1], ALU.subtract).then_inc(s.gap_ok, 1)
            pick = choice.rearrange("p t k -> p (t k)")
            dve.wait_ge(s.xn2_out, 16 * (T // G))
            step(dve.tensor_tensor(hot_x, iota_x[0:P, :].unsqueeze(2).broadcast_to([P, NX, 2 * T]),
                                   pick.unsqueeze(1).broadcast_to([P, NX, 2 * T]), ALU.is_equal))
            step(dve.tensor_tensor_scan(run_x.rearrange("p e c -> p (e c)"), ones[0:P, 0:1].broadcast_to([P, NX * 2 * T]),
                                        hot_x.rearrange("p e c -> p (e c)"), 0.0, ALU.mult, ALU.add))
            step(dve.tensor_copy(last_slot.unsqueeze(2), run_x[:, :, 2 * T - 1:2 * T]))
            step(dve.tensor_copy(count_x, last_slot))
            dve.tensor_tensor(count_x[:, 1:NX], last_slot[:, 1:NX], last_slot[:, 0:NX - 1], ALU.subtract).then_inc(s.count_ok, 1)
            dve.wait_ge(s.count_ok, 1)
            step(dve.tensor_tensor(last_slot, last_slot, count_x, ALU.subtract))
            dve.wait_ge(s.route_mm, 1)
            for dst_, src_ in ((tiles_x, bank[7][0:P, 128:128 + NX]), (col_x, bank[7][0:NX, 192:193])):
                chain.add(dve.tensor_scalar(dst_, src_, half, 1.0 / SLOT, ALU.add, ALU.mult))
            chain.wait()
            for dst_ in (tiles_x, col_x):
                chain.add(dve.tensor_scalar(dst_, dst_, MAGIC, None, ALU.add))
            chain.wait()
            chain.add(dve.tensor_scalar(tiles_x, tiles_x, MAGIC, None, ALU.subtract))
            dve.tensor_scalar(col_x, col_x, MAGIC, None, ALU.subtract).then_inc(s.col_x_ok, 1)
            chain.wait()
            step(dve.tensor_tensor_scan(incl_x, ones[0:P, 0:NX], tiles_x, 0.0, ALU.mult, ALU.add))
            step(dve.tensor_tensor(incl_x, incl_x, tiles_x, ALU.subtract))
            step(dve.scalar_tensor_tensor(off_x, incl_x, float(SLOT), bank[7][0:P, 64:64 + NX], ALU.mult, ALU.add))
            step(dve.scalar_tensor_tensor(off_x, off_x, -1.0, last_slot, ALU.add, ALU.subtract))
            step(dve.tensor_tensor(run_x, run_x, off_x.unsqueeze(2).broadcast_to([P, NX, 2 * T]), ALU.add))
            step(dve.tensor_tensor(run_x, run_x, hot_x, ALU.mult))
            step(dve.reduce_sum(pos_x, run_x.rearrange("p e c -> p c e"), axis=AX.X))
            step(dve.tensor_scalar(slot_qx, pos_x, -half, 1.0 / SLOT, ALU.add, ALU.mult))
            step(dve.tensor_scalar(slot_qx, slot_qx, MAGIC, None, ALU.add))
            step(dve.tensor_scalar(slot_qx, slot_qx, MAGIC, None, ALU.subtract))
            step(dve.scalar_tensor_tensor(slot_rx, slot_qx, -float(SLOT), pos_x, ALU.mult, ALU.add))
            wide = lambda v, n: v.unsqueeze(2).broadcast_to([P, 2 * T, n])
            dve.tensor_tensor(hot_rx, iota_r[0:P, :].unsqueeze(1).broadcast_to([P, 2 * T, 128]), wide(slot_rx, 128), ALU.is_equal)
            step(dve.tensor_tensor(hot_qx, iota_q[0:P, 0:NT].unsqueeze(1).broadcast_to([P, 2 * T, NT]), wide(slot_qx, NT), ALU.is_equal))
            dve.tensor_tensor(val_qx[:, :, 0, :], hot_qx, wide(tok_val.rearrange("p t k -> p (t k)"), NT), ALU.mult)
            dve.tensor_tensor(val_qx[:, :, 1, :], hot_qx, wide(tok_pick.rearrange("p t k -> p (t k)"), NT),
                              ALU.mult).then_inc(s.tok_hot_ok, 1)
            dve.wait_ge(s.exp_ok, 1)
            step(dve.tensor_scalar(weight[:, :, 0:1], weight[:, :, 1:2], 1.0, None, ALU.add))
            step(dve.reciprocal(weight[:, :, 0:1], weight[:, :, 0:1]))
            chain.add(dve.tensor_tensor(weight[:, :, 1:2], weight[:, :, 1:2], weight[:, :, 0:1], ALU.mult))
            dve.wait_ge(s.ends_x_mm, 1)
            step(dve.tensor_copy(ends_x, bank[6][0:NX, 0:1]))
            dve.tensor_scalar(past_x, iota_q[0:NX, 0:NT], ends_x, None, ALU.is_ge).then_inc(s.past_x_ok, 1)
            dve.wait_ge(s.expert_mm, 1)
            chain.add(dve.tensor_scalar(tok_expert, bank[6][0:1, 64:64 + NT], float(NX - 1), None, ALU.min))
            dve.wait_ge(s.tok_mm, 1)
            ids, picks = bank[5][:, 0:NT], bank[5][:, NT:2 * NT]
            dve.tensor_scalar(tok_gather, ids, float(MID), None, ALU.add)
            dve.wait_ge(s.trash_ok, 1)
            step(dve.scalar_tensor_tensor(unused, picks, 0.0, trash.rearrange("p a b -> p (a b)"), ALU.is_equal, ALU.mult))
            step(dve.scalar_tensor_tensor(out_row, picks, float(N), unused, ALU.mult, ALU.add))
            dve.scalar_tensor_tensor(tok_scatter, ids, float(MID - N), out_row, ALU.add, ALU.add).then_inc(s.tok_ok, 1)

            def tokT_tile(n, par, first=False):
                dve.wait_ge(s.tokT_mm, n + 1)
                if not first:
                    dve.wait_ge(s.ffn1_mm, n - 1)
                dve.tensor_copy(tokT[:, par, :, :], bview(par, 2, 128)).then_inc(s.tokT_ok, 1)

            def y_tile(i, j, expert):
                n = i * 4 + j
                dve.wait_ge(s.ffn2_mm, n + 1)
                dve.wait_ge(y_out[j % 2], (i * 2 + j // 2) * 16)
                dve.tensor_tensor(y_rows[:, j % 2, :], bank[6 + j % 2][:, 0:D],
                                  b2_x[:, bass.ds(expert, 1), :].rearrange("p a c -> p (a c)"), ALU.add).then_inc(s.y_ok, 1)

            def chosen(at, count):
                return nc.values_load_multi_w_load_instructions(
                    tok_expert[:, bass.ds(at, count)], engines=[mybir.EngineType.DVE], min_val=0, max_val=NX - 1,
                    skip_runtime_bounds_check_because="clamped to the last expert when written")[1]

            dve.wait_ge(s.tok_ok, 1)
            for n in range(3):
                tokT_tile(n, n % 2, first=n < 2)
            dve.wait_ge(s.late_in, 48)
            with dve.Fori(0, (NT - 4) // 4) as i:
                e = chosen(i * 4, 4)
                for j in range(4):
                    tokT_tile(i * 4 + 3 + j, (3 + j) % 2)
                    y_tile(i, j, e[j])
            tokT_tile(NT - 1, 1)
            e = chosen(NT - 4, 4)
            for j in range(4):
                y_tile((NT - 4) // 4, j, e[j])

            for g in range(T // G):
                tiles = range(G * g, G * g + G)
                dve.wait_ge(fin_in[g], 6 * 16)
                for t in tiles:
                    last = dve.scalar_tensor_tensor(pick0[:, t, :], pick0[:, t, :], weight[:, t, 0:1], own[:, t, :], ALU.mult, ALU.add)
                step(last)
                for t in tiles:
                    last = dve.scalar_tensor_tensor(pick1[:, t, :], pick1[:, t, :], weight[:, t, 1:2], pick0[:, t, :], ALU.mult, ALU.add)
                step(last)
                for t in tiles:
                    last = dve.bn_stats(stats[:, t, :], pick1[:, t, :])
                step(last)
                for t in tiles:
                    last = dve.bn_aggr(mv[:, t, :], stats[:, t, :])
                last.then_inc(s.fin_stats, 1)
                dve.wait_ge(s.fin_root, g + 1)
                step(dve.reciprocal(rstd[:, G * g:G * g + G], rstd[:, G * g:G * g + G]))
                for t in tiles:
                    dve.tensor_scalar(pick0[:, t, :], pick1[:, t, :], mv[:, t, 0:1], rstd[:, t:t + 1], ALU.subtract,
                                      ALU.mult).then_inc(s.fin_norm, 1)

        @block.tensor
        def _(pe):
            mm = pe.matmul
            pe.wait_ge(s.consts, 1)
            pe.wait_ge(s.raw_in, 32)
            for k in range(4):
                for i in range(2):
                    for c in range(2):
                        last = pe.transpose(bview(4 + k, 4, 128)[:, 2 * i + c, :], raw_w[:, 2 * k + i, 128 * c:128 * c + 128], ident)
                last.then_inc(s.wT_mm, 1)

            def transpose_rows(g, j):
                t = g * G + j
                pe.wait_ge(s.xn_ready, t + 1)
                pe.wait_ge(s.xnT_ready, t - 1 if j >= 2 else g * G)
                for k in range(2):
                    last = pe.transpose(bview(j % 2, 2, P)[:, k, :],
                                        xn_rows[:, j, 128 * k:128 * k + 128], ident[0:P, 0:P])
                last.then_inc(s.xnT_mm, 1)

            def front(lo, hi):
                with pe.Fori(lo, hi) as g:
                    transpose_rows(g, 0)
                    for j in range(G):
                        t = g * G + j
                        pe.wait_ge(s.xnT_ready, t + 1)
                        pe.wait_ge(s.h_ready, t - 1 if j >= 2 else g * G)
                        for f in range(2):
                            for k in range(2):
                                last = mm(bview(2 + j % 2, 2, P)[:, f, :], w1_sb[:, k, 128 * f:128 * f + 128],
                                          xnT[:, j, k, :], start=k == 0, stop=k == 1)
                        last.then_inc(s.l1_mm, 1)
                        if j < G - 1:
                            transpose_rows(g, j + 1)
                        pe.wait_ge(s.qkv_evac, t)
                        for half in range(2):
                            for k in range(2):
                                last = mm(bank[5 + half][0:P, 0:384], xnT[:, j, k, :], wqkvT[:, k, 384 * half:384 * half + 384],
                                          start=k == 0, stop=k == 1)
                        last.then_inc(s.qkv_mm, 1)
                        pe.wait_ge(s.h_ready, t + 1)
                        pe.wait_ge(s.m_evac, t)
                        for k in range(2):
                            last = mm(bank[4][0:P, 0:D], hT[:, j, k, :], w2_sb[:, k, :], start=k == 0, stop=k == 1)
                        last.then_inc(s.m_mm, 1)

            pe.wait_ge(s.gnn_in, 32)
            pe.wait_ge(s.act_chain, 4)
            front(0, 2)
            pe.wait_ge(s.cnt_ok, 1)
            mm(bank[7][0:P, 0:NB], tri, cnt, start=True, stop=True)
            mm(bank[7][0:P, 64:64 + NB], ones[0:P, :], cnt, start=True, stop=True)
            mm(bank[7][0:NB, 128:129], cnt, ones[0:P, 0:1], start=True, stop=True).then_inc(s.prefix_mm, 1)
            front(2, T // G)
            pe.wait_ge(s.n_col_ok, 1)
            pe.wait_ge(s.col_hot_ok, 1)
            mm(bank[7][0:NB, 0:1], tri_in, n_col, start=True, stop=True).then_inc(s.ends_mm, 1)
            def columns(i, first=False, last_one=False):
                for c in range(16):
                    hot_q, hot_d, hot_l = col_hot[c % 8]
                    pe.wait_ge(s.col_hot_ok, i * 16 + c + 1)
                    mm(bank[0][:, 0:NQ], hot_d, hot_q, start=first and c == 0, stop=last_one and c == 15)
                    mm(bank[1][:, 0:NQ], hot_l, hot_q, start=first and c == 0, stop=last_one and c == 15).then_inc(s.col_mm, 1)

            columns(0, first=True)
            with pe.Fori(1, T - 1) as i:
                columns(i)
            columns(T - 1, last_one=True)
            pe.wait_ge(s.past_ok, 1)
            mm(bank[6][0:1, 0:NQ], ones[0:NB, 0:1], past_end, start=True, stop=True).then_inc(s.bucket_mm, 1)
            mm(bank[7][0:1, 0:1], ones[0:NB, 0:1], ones[0:NB, 0:1], start=True, stop=True).then_inc(s.sorted_mm, 1)

            def agg_tile(n, k, turn):
                if k == 0:
                    pe.wait_ge(s.hot_src_ok, n + 1)
                pe.wait_ge(msgs_in[k], n * 16 + 16)
                if k % 2 == 0 and not (at(n, (0,)) and k < 4):
                    pe.wait_ge(s.agg_add, n * GB + k - 2)
                for c in range(2):
                    last = mm(agg_ps[k % 4][:, P * c:P * c + P], msgs[:, k, 128 * c:128 * c + 128], hot_src[:, turn, k, :],
                              start=True, stop=True, skip_group_check=True)
                last.then_inc(s.agg_mm, 1)

            def k_tile(t, turn):
                first = at(t, (0,))
                pe.wait_ge(s.kd_ok, t + 1)
                pe.wait_ge(s.v1_ok, t + 1)
                group = dict(stop=at(t, (T - 1,)), skip_group_check=True)
                values = v1[:, turn, :, :]
                for i in range(2):
                    mm(lin_ps[i], k_row[:, turn, 4 * i:4 * i + 4, :], values[:, 4 * i:4 * i + 4, :], start=first, **group)
                mm(bank[6][0:P, 0:H * HV], ones[0:P, :], values, start=first, **group).then_inc(s.lin_mm, 1)
                for h in range(H):
                    pe.wait_ge(s.pairs_ok, t * H + h + 1)
                    for c in range(4):
                        last = mm(bank[h // 3][:, (h % 3 * 4 + c) * HV:(h % 3 * 4 + c + 1) * HV], pairs[:, h, 128 * c:128 * c + 128],
                                  values[:, h, :], start=first and h in (0, 3) and c == 0, **group)
                    last.then_inc(s.head_mm, 1)
                    agg_tile(t, h, turn)
                    if h == 4:
                        pe.wait_ge(s.k_diag_ok, t + 1)
                        for i in range(2):
                            last = mm(diag_ps[i], k_diag[:, 4 * i:4 * i + 4, :], values[:, 4 * i:4 * i + 4, :], start=False, **group)
                        last.then_inc(s.diag_mm, 1)

            mixer_tiles(pe, k_tile)

            def mixT_of(t):
                pe.wait_ge(s.mix_row_ok, t + 1)
                if not at(t, (0,)):
                    pe.wait_ge(s.mixT_ok, t)
                for k in range(2):
                    last = pe.transpose(bview(6, 2, P)[:, k, :], mix_row[:, 4 * k:4 * k + 4, :], ident[0:P, 0:P])
                last.then_inc(s.mixT_mm, 1)

            def project(t):
                pe.wait_ge(s.mixT_ok, t + 1)
                if not at(t, (0,)):
                    pe.wait_ge(s.x_ok, t)
                for k in range(2):
                    last = mm(bank[6][0:P, 256:512], mixT[:, k, :], wprojT[:, k, :], start=k == 0, stop=k == 1)
                last.then_inc(s.proj_mm, 1)

            def qT_of(t):
                pe.wait_ge(s.split_ok, t + 1)
                if not at(t, (0,)):
                    pe.wait_ge(s.qT_ok, t)
                for h in range(H):
                    last = pe.transpose(q_partsT_ps[:, h, 0:P], q_parts[:, h, :, :].rearrange("p a b -> p (a b)"), ident_h[0:P, 0:P])
                last.then_inc(s.q_partsT_mm, 1)
                if not at(t, (0,)):
                    pe.wait_ge(s.q_ld_ok, t)
                for k in range(2):
                    last = pe.transpose(bview(1, 2, P)[:, k, :], q_row[:, 4 * k:4 * k + 4, :], ident[0:P, 0:P])
                last.then_inc(s.qnT_mm, 1)

            def q_tile(t, turn):
                y = bank[7][0:P, 0:H * HV]

                def sums(h):
                    if not (at(t, (0,)) and h < 2):
                        pe.wait_ge(s.q_pairs_ok, t * H + h - 1)
                    for c in range(4):
                        last = mm(bview(2 + h % 2, 4, P)[:, c, :], sel[:, c, :], qT[:, h, 0:P], start=True, stop=True,
                                  skip_group_check=True)
                    last.then_inc(s.sel_mm, 1)

                group = dict(stop=False, skip_group_check=True)
                pe.wait_ge(s.qT_ok, t + 1)
                sums(0)
                sums(1)
                if not at(t, (0,)):
                    mixT_of(t - 1)
                mm(y, row0, v_sum, start=True, **group)
                pe.wait_ge(s.q_ld_ok, t + 1)
                for i in range(2):
                    mm(y[:, 4 * HV * i:4 * HV * (i + 1)], q_lin[:, i, :], kv_lin[:, i, :], start=False, **group)
                    last = mm(y[:, 4 * HV * i:4 * HV * (i + 1)], q_sq[:, i, :], kv_diag[:, i, :], start=False, **group)
                last.then_inc(s.y_ld_mm, 1)
                for h in range(H):
                    pe.wait_ge(s.q_pairs_ok, t * H + h + 1)
                    for c in range(4):
                        last = mm(y[:, HV * h:HV * h + HV], q_pairs[:, h % 4, c, :], kv[:, h, c, :], start=False,
                                  stop=c == 3, skip_group_check=True)
                    last.then_inc(s.y_mm, 1)
                    if h < H - 2:
                        sums(h + 2)
                    if h == 3 and not at(t, (0,)):
                        project(t - 1)
                    if h == 5 and not at(t, (T - 1,)):
                        qT_of(t + 1)
                    agg_tile(t + T, h, 1 - turn)

            pe.wait_ge(s.kv_ok, 1)
            qT_of(0)
            mixer_tiles(pe, q_tile)
            mixT_of(T - 1)
            project(T - 1)
            for n in range(2 * T, NBATCH):
                for k in range(GB):
                    agg_tile(n, k, n % 2)

            pe.wait_ge(s.gate_in, 48)
            pe.transpose(bank[7][:, 0:NX * 4], b1_rows, ident[0:NX * 4, 0:NX * 4]).then_inc(s.b1_mm, 1)
            pe.wait_ge(s.agg_add, NBATCH * GB)
            pe.wait_ge(s.x_ok, T)

            def second_pass(g):
                def up(j):
                    t = g * G + j
                    pe.wait_ge(s.h2_ok, t - 1 if j >= 2 else g * G)
                    h = node[:, bass.ds(t, 1), :].rearrange("p a c -> p (a c)")
                    for f in range(2):
                        for k in range(2):
                            last = mm(bview(j % 2, 2, P)[:, f, :], w1_sb[:, k, 128 * f:128 * f + 128], h[:, P * k:P * k + P],
                                      start=k == 0, stop=k == 1)
                    last.then_inc(s.f1_mm, 1)

                up(0)
                for j in range(G):
                    if j < G - 1:
                        up(j + 1)
                    t = g * G + j
                    pe.wait_ge(s.h2_ok, t + 1)
                    pe.wait_ge(s.x2_add, t)
                    for k in range(2):
                        last = mm(bank[2][0:P, 0:D], hT2[:, j % 2, k, :], w2_sb[:, k, :], start=k == 0, stop=k == 1)
                    last.then_inc(s.f2_mm, 1)

            def gate(g):
                def rows(j):
                    t = g * G + j
                    pe.wait_ge(s.xn2_ok, t + 1)
                    pe.wait_ge(s.xn2T_ok, t - 1 if j >= 2 else g * G)
                    for k in range(2):
                        last = pe.transpose(bview(3 + j % 2, 2, P)[:, k, :], xn2[:, j, 128 * k:128 * k + 128], ident[0:P, 0:P])
                    last.then_inc(s.xn2T_mm, 1)

                rows(0)
                for j in range(G):
                    if j < G - 1:
                        rows(j + 1)
                    t = g * G + j
                    pe.wait_ge(s.xn2T_ok, t + 1)
                    if j == 0:
                        pe.wait_ge(s.gate_ok, g)
                    for k in range(2):
                        last = mm(bank[5][0:P, NX * j:NX * j + NX], xn2T[:, j % 2, k, :], gate_w_sb[:, k, :], start=k == 0, stop=k == 1)
                    last.then_inc(s.gate_mm, 1)

            second_pass(0)
            with pe.Fori(1, T // G) as g:
                second_pass(g)
                gate(g - 1)
            gate(T // G - 1)
            pe.wait_ge(s.count_ok, 1)
            mm(bank[7][0:P, 64:64 + NX], tri, count_x, start=True, stop=True)
            mm(bank[7][0:P, 128:128 + NX], ones[0:P, :], count_x, start=True, stop=True)
            mm(bank[7][0:NX, 192:193], count_x, ones[0:P, 0:1], start=True, stop=True).then_inc(s.route_mm, 1)
            pe.wait_ge(s.col_x_ok, 1)
            mm(bank[6][0:NX, 0:1], tri_in[0:NX, 0:NX], col_x, start=True, stop=True).then_inc(s.ends_x_mm, 1)
            pe.wait_ge(s.tok_hot_ok, 1)
            for c in range(2 * T):
                last = mm(bank[5][:, 0:2 * NT], hot_rx[:, c, :], val_qx[:, c, :, :].rearrange("p a b -> p (a b)"),
                          start=c == 0, stop=c == 2 * T - 1)
            last.then_inc(s.tok_mm, 1)
            pe.wait_ge(s.past_x_ok, 1)
            mm(bank[6][0:1, 64:64 + NT], ones[0:NX, 0:1], past_x, start=True, stop=True).then_inc(s.expert_mm, 1)

            def tokT_of(i, j):
                n = i * 4 + j
                pe.wait_ge(tok_in[j % 4], (i + j // 4) * 16 + 16)
                if not (isinstance(i, int) and n < 2):
                    pe.wait_ge(s.tokT_ok, n - 1)
                for k in range(2):
                    last = pe.transpose(bview(j % 2, 2, 128)[:, k, :], tok_rows[:, j % 4, 128 * k:128 * k + 128], ident)
                last.then_inc(s.tokT_mm, 1)

            def up_of(i, j, expert):
                n = i * 4 + j
                pe.wait_ge(s.tokT_ok, n + 1)
                if not (isinstance(i, int) and n < 2):
                    pe.wait_ge(s.hid_ok, n - 1)
                w = experts[:, bass.ds(expert, 1), 0:1024].rearrange("p a n -> p (a n)")
                for k in range(2):
                    last = mm(bank[2 + j % 2][:, :], tokT[:, j % 2, k, :], w[:, FF * k:FF * k + FF], start=k == 0, stop=k == 1)
                last.then_inc(s.ffn1_mm, 1)

            def hidT_of(i, j):
                n = i * 4 + j
                pe.wait_ge(s.hid_ok, n + 1)
                if not (isinstance(i, int) and n < 2):
                    pe.wait_ge(s.relu_ok, n - 1)
                for c in range(4):
                    last = pe.transpose(bview(4 + j % 2, 4, 128)[:, c, :], hid[:, j % 2, 128 * c:128 * c + 128], ident)
                last.then_inc(s.hidT_mm, 1)

            def down_of(i, j, expert):
                n = i * 4 + j
                pe.wait_ge(s.relu_ok, n + 1)
                if not (isinstance(i, int) and n < 2):
                    pe.wait_ge(s.y_ok, n - 1)
                w = experts[:, bass.ds(expert, 1), 1024:2048].rearrange("p a n -> p (a n)")
                for c in range(4):
                    last = mm(bank[6 + j % 2][:, 0:D], hidT[:, j % 2, c, :], w[:, D * c:D * c + D], start=c == 0, stop=c == 3)
                last.then_inc(s.ffn2_mm, 1)

            def chosen(at, count):
                return nc.values_load_multi_w_load_instructions(
                    tok_expert[:, bass.ds(at, count)], engines=[mybir.EngineType.PE], min_val=0, max_val=NX - 1,
                    skip_runtime_bounds_check_because="clamped to the last expert when written")[1]

            pe.wait_ge(s.tok_ok, 1)
            pe.wait_ge(s.w_in, 32 * NX)
            tokT_of(0, 0)
            tokT_of(0, 1)
            e = chosen(0, 2)
            up_of(0, 0, e[0])
            up_of(0, 1, e[1])
            hidT_of(0, 0)
            tokT_of(0, 2)

            def four_tiles(i):
                e = chosen(i * 4, 6)
                for j in range(4):
                    up_of(i, j + 2, e[j + 2])
                    hidT_of(i, j + 1)
                    tokT_of(i, j + 3)
                    down_of(i, j, e[j])

            four_tiles(0)
            with pe.Fori(1, (NT - 4) // 4) as i:
                four_tiles(i)
            i = (NT - 4) // 4
            e = chosen(NT - 4, 4)
            for j in range(4):
                if j < 2:
                    up_of(i, j + 2, e[j + 2])
                if j < 3:
                    hidT_of(i, j + 1)
                if j < 1:
                    tokT_of(i, j + 3)
                down_of(i, j, e[j])


INPUTS = ("x src dst L0_gnn_w1 L0_gnn_b1 L0_gnn_w2 L0_gnn_b2 L0_mix_Wqkv L0_mix_bqkv L0_mix_Wproj L0_mix_bproj "
          "L0_mix_temperature L0_ffn_gate_w L0_ffn_gate_b L0_ffn_w1 L0_ffn_b1 L0_ffn_w2 L0_ffn_b2 L0_ffn_gamma "
          "L0_ffn_beta").split()


def kernel(**inputs):
    import concourse.bacc as _bacc
    from concourse.bass_utils import run_bass_kernel_spmd as _run

    nc = _bacc.Bacc("TRN2", target_bir_lowering=False, num_devices=1)
    arrays, args = {}, []
    for name in INPUTS:
        a = np.ascontiguousarray(inputs[name])
        arrays[name] = a
        args.append(nc.dram_tensor(name, a.shape, mybir.dt.from_np(a.dtype), kind="ExternalInput").ap())
    args.append(nc.dram_tensor("out", (N, D), F32, kind="ExternalOutput").ap())
    program(nc, *args)
    return _run(nc, [arrays], core_ids=[0]).results[0]["out"]
```

```python
import numpy as np
import concourse.bass as bass
from concourse import mybir
from contextlib import ExitStack

F32 = mybir.dt.float32
F16 = mybir.dt.float16
BF16 = mybir.dt.bfloat16
I32 = mybir.dt.int32
U32 = mybir.dt.uint32
ALU = mybir.AluOpType
ACT = mybir.ActivationFunctionType
AX = mybir.AxisListType

N, D, E = 3125, 256, 50000
P, T = 125, 25
G = 5
EC = E // P
SLOT = 128
NB = T
NQ = 416
GB = 8
NBATCH = NQ // GB
H, DH = 8, 32
HV = DH + 1
NX, FF = 16, 512
NT = 64
MAGIC = 12582912.0
MID = 1562
SCALE2 = float(DH) ** 0.5
LN_EPS = 1e-5
assert NQ * SLOT >= E + NB * (SLOT - 1) - SLOT + 1 and NT * SLOT > 2 * N + NX * (SLOT - 1) - SLOT


class Region:

    def __init__(self, tensor, start=0, end=None):
        self.tensor, self.at, self.end = tensor, start, end

    def take(self, shape, dt=F32, parts=128):
        size = int(np.prod(shape))
        words = size if dt in (F32, I32, U32) else (size + 1) // 2
        view = self.tensor[0:parts, self.at:self.at + words]
        self.at += words
        assert self.end is None or self.at <= self.end, (self.at, self.end)
        if dt is not F32:
            view = view.bitcast(dt)
        if len(shape) == 2:
            view = view.rearrange("p (a b) -> p a b", a=shape[0])
        if len(shape) == 3:
            view = view.rearrange("p (a b c) -> p a b c", a=shape[0], b=shape[1])
        return view


class Chain:

    def __init__(self, eng, sem):
        self.eng, self.sem, self.base, self.n = eng, sem, 0, 0

    def add(self, ins):
        ins.then_inc(self.sem, 1)
        self.n += 1

    def wait(self):
        self.eng.wait_ge(self.sem, self.base + self.n)

    def enter(self, i, first, per):
        self.start, self.per = self.base + self.n, per
        self.base, self.n = self.start + (i - first) * per, 0

    def leave(self, rounds):
        assert self.n == self.per, (self.n, self.per)
        self.base, self.n = self.start + rounds * self.per, 0


class Semaphores:

    def __init__(self, sem):
        self.x_in = sem("x_in")
        self.edges_in = sem("edges_in")
        self.gnn_in = sem("gnn_in")
        self.raw_in = sem("raw_in")
        self.bias_in = sem("bias_in")
        self.gate_in = sem("gate_in")
        self.w_in = sem("w_in")
        self.late_in = sem("late_in")
        self.consts = sem("consts")
        self.preps = sem("preps")
        self.wT_mm = sem("wT_mm")
        self.dve_chain = sem("dve_chain")
        self.pool_chain = sem("pool_chain")
        self.act_chain = sem("act_chain")
        self.apart = sem("apart")
        self.ln_stats = sem("ln_stats")
        self.rstd_sd = sem("rstd_sd")
        self.xn_ready = sem("xn_ready")
        self.xnT_mm = sem("xnT_mm")
        self.xnT_ready = sem("xnT_ready")
        self.l1_mm = sem("l1_mm")
        self.h_ready = sem("h_ready")
        self.m_mm = sem("m_mm")
        self.m_evac = sem("m_evac")
        self.m_biased = sem("m_biased")
        self.qkv_mm = sem("qkv_mm")
        self.qkv_evac = sem("qkv_evac")
        self.qkv_biased = sem("qkv_biased")
        self.xn_row_ok = sem("xn_row_ok")
        self.sq_ok = sem("sq_ok")
        self.norm_part = sem("norm_part")
        self.norm_root = sem("norm_root")
        self.norm_ok = sem("norm_ok")
        self.cnt_ok = sem("cnt_ok")
        self.prefix_mm = sem("prefix_mm")
        self.n_col_ok = sem("n_col_ok")
        self.ends_mm = sem("ends_mm")
        self.past_ok = sem("past_ok")
        self.bucket_mm = sem("bucket_mm")
        self.col_hot_ok = sem("col_hot_ok")
        self.col_mm = sem("col_mm")
        self.sorted_ok = sem("sorted_ok")
        self.msg_idx_ok = sem("msg_idx_ok")
        self.hot_src_ok = sem("hot_src_ok")
        self.agg_mm = sem("agg_mm")
        self.agg_add = sem("agg_add")
        self.v1_ones = sem("v1_ones")
        self.kd_ok = sem("kd_ok")
        self.k_row_ok = sem("k_row_ok")
        self.v1_ok = sem("v1_ok")
        self.lin_mm = sem("lin_mm")
        self.k_diag_ok = sem("k_diag_ok")
        self.diag_mm = sem("diag_mm")
        self.pairs_ok = sem("pairs_ok")
        self.head_mm = sem("head_mm")
        self.kv_ok = sem("kv_ok")
        self.split_ok = sem("split_ok")
        self.q_partsT_mm = sem("q_partsT_mm")
        self.qT_ok = sem("qT_ok")
        self.qnT_mm = sem("qnT_mm")
        self.q_ld_ok = sem("q_ld_ok")
        self.sel_mm = sem("sel_mm")
        self.q_pairs_ok = sem("q_pairs_ok")
        self.y_mm = sem("y_mm")
        self.y_ld_mm = sem("y_ld_mm")
        self.mix_row_ok = sem("mix_row_ok")
        self.mixT_mm = sem("mixT_mm")
        self.mixT_ok = sem("mixT_ok")
        self.proj_mm = sem("proj_mm")
        self.x_ok = sem("x_ok")
        self.b1_mm = sem("b1_mm")
        self.b1_ok = sem("b1_ok")
        self.f1_mm = sem("f1_mm")
        self.h2_ok = sem("h2_ok")
        self.f2_mm = sem("f2_mm")
        self.x2_add = sem("x2_add")
        self.ln2_stats = sem("ln2_stats")
        self.ln2_root = sem("ln2_root")
        self.xn2_ok = sem("xn2_ok")
        self.xn2_out = sem("xn2_out")
        self.xn2T_mm = sem("xn2T_mm")
        self.xn2T_ok = sem("xn2T_ok")
        self.gate_mm = sem("gate_mm")
        self.gate_ok = sem("gate_ok")
        self.gap_ok = sem("gap_ok")
        self.exp_ok = sem("exp_ok")
        self.trash_ok = sem("trash_ok")
        self.count_ok = sem("count_ok")
        self.route_mm = sem("route_mm")
        self.col_x_ok = sem("col_x_ok")
        self.ends_x_mm = sem("ends_x_mm")
        self.past_x_ok = sem("past_x_ok")
        self.expert_mm = sem("expert_mm")
        self.tok_hot_ok = sem("tok_hot_ok")
        self.tok_mm = sem("tok_mm")
        self.tok_ok = sem("tok_ok")
        self.tokT_mm = sem("tokT_mm")
        self.tokT_ok = sem("tokT_ok")
        self.ffn1_mm = sem("ffn1_mm")
        self.hid_ok = sem("hid_ok")
        self.hidT_mm = sem("hidT_mm")
        self.relu_ok = sem("relu_ok")
        self.ffn2_mm = sem("ffn2_mm")
        self.y_ok = sem("y_ok")
        self.beta_ok = sem("beta_ok")
        self.fin_stats = sem("fin_stats")
        self.fin_root = sem("fin_root")
        self.fin_norm = sem("fin_norm")
        self.fin_ok = sem("fin_ok")
        self.stored = sem("stored")


def windows(ap, shifts, step):
    dims = list(ap.ap)
    return bass.AP(ap.tensor, ap.offset, [dims[0], [step, shifts], *dims[1:]])


def program(nc, x, src, dst, gnn_w1, gnn_b1, gnn_w2, gnn_b2, Wqkv, bqkv, Wproj, bproj, temperature,
            gate_w, gate_b, ffn_w1, ffn_b1, ffn_w2, ffn_b2, gamma, beta, out):
    ctx = ExitStack()
    with ctx:
        def sb(name, words):
            return ctx.enter_context(nc.sbuf_tensor(name, [128, words], F32))

        def sem(name):
            return ctx.enter_context(nc.semaphore(name))

        x_buf = sb("x_buf", T * D)
        node_buf = sb("node_buf", T * D)
        big = sb("big", NX * 2048)
        mid = sb("mid", 4352)
        const = Region(sb("const", 3288), 0, 3288)

        x_sb = x_buf[0:P, :].rearrange("p (t c) -> p t c", t=T)
        node = node_buf[:, :].rearrange("p (t c) -> p t c", t=T)

        xn_rows = node[0:P, T - G:T, :]

        ident = const.take([128])
        ident_h = const.take([128], BF16)
        iota_q = const.take([NQ], F16)
        iota_r = const.take([128], F16)
        iota_loc = const.take([P])
        iota_x = const.take([NX])
        tri = const.take([P], parts=P)
        tri_in = const.take([NB], parts=NB)
        ones = const.take([P])
        row0 = const.take([P], parts=P)
        head_mask = const.take([4])
        pair_w = const.take([4])
        sel = const.take([4, 128], BF16, parts=96)
        trash_pad = const.take([1])
        edges_at = const.at
        edge_idx = const.take([NQ], I32)
        edge_loc = const.take([NQ])
        edge_bucket = const.take([NQ], I32, parts=1)
        stats = const.take([T, 6], parts=P)
        mv = const.take([T, 2], parts=P)
        rstd = const.take([T], parts=P)
        eps_t = const.take([1], parts=P)
        temp_t = const.take([H], parts=P)
        gnn_b1T = const.take([2])
        gate_w_sb = const.take([2, NX])
        gate_b_bc = const.take([NX], parts=P)
        tok_val = const.take([T, 2], parts=P)
        tok_pick = const.take([T, 2], parts=P)
        logits = const.take([G, NX], parts=P)
        top_val = const.take([G, 8], parts=P)
        top_idx = const.take([G, 8], U32, parts=P)
        b1T = const.take([NX * 4])
        score = const.take([T, 2], parts=P)
        choice = const.take([T, 2], parts=P)
        weight = const.take([T, 2], parts=P)

        c = Region(const.tensor, edges_at, edges_at + 3 * NQ)
        tok_gather = c.take([NT], I32)
        tok_scatter = c.take([NT], I32)
        tok_expert = c.take([NT], I32, parts=1)
        last_slot = c.take([NX], parts=P)
        count_x = c.take([NX], parts=P)
        tiles_x = c.take([NX], parts=P)
        incl_x = c.take([NX], parts=P)
        off_x = c.take([NX], parts=P)
        col_x = c.take([1], parts=NX)
        ends_x = c.take([1], parts=NX)
        past_x = c.take([NT], parts=NX)
        pos_x = c.take([2 * T], parts=P)
        slot_qx = c.take([2 * T], parts=P)
        slot_rx = c.take([2 * T], parts=P)
        unused = c.take([NT])
        out_row = c.take([NT])
        trash = c.take([NT // 2, 2])

        m = Region(mid, 0, 4352)
        w1_sb = m.take([2, D])
        w2_sb = m.take([2, D])
        wqkvT = m.take([2, 3 * D])
        wprojT = m.take([2, D])
        bqkv_bc = m.take([3 * D], parts=P)
        b2_bc = m.take([D], parts=P)
        bsum_bc = m.take([D], parts=P)

        m = Region(mid, 4 * D, 4352)
        hT2 = m.take([2, 2, P])
        xn2 = m.take([G, D], parts=P)
        xn2T = m.take([2, 2, P])
        b1_rows = m.take([128], parts=NX * 4)
        m = Region(mid, 0, 4352)
        hot_x = m.take([NX, 2 * T], parts=P)
        run_x = m.take([NX, 2 * T], parts=P)
        hot_qx = m.take([2 * T, NT], F16, parts=P)
        m = Region(node_buf, 0, T * D)
        hot_rx = m.take([2 * T, 128], F16, parts=P)
        val_qx = m.take([2 * T, 2, NT], F16, parts=P)
        m = Region(mid, 0, 4352)
        tok_rows = m.take([4, D])
        tokT = m.take([2, 2, 128])
        hid = m.take([2, FF])
        hidT = m.take([2, 4, 128])
        y_rows = m.take([2, D])
        m = Region(node_buf, 0, T * D)
        b2_x = m.take([NX, D])
        gamma_bc = m.take([D], parts=P)
        beta_bc = m.take([D], parts=P)
        experts = big[:, :].rearrange("p (e n) -> p e n", e=NX)
        m = Region(big, 0, NX * 2048)
        pick0 = m.take([T, D], parts=P)
        pick1 = m.take([T, D], parts=P)
        own = m.take([T, D], parts=P)

        b = Region(big, 0, NX * 2048)
        qkv = b.take([T, 3 * D], parts=P)
        phase = b.at
        src_i = b.take([EC], I32, parts=P)
        dst_i = b.take([EC], I32, parts=P)
        loc_f = b.take([EC], parts=P)
        bkt_h = b.take([EC], F16, parts=P)
        pos = b.take([EC], parts=P)
        slot_q = b.take([EC], parts=P)
        slot_r = b.take([EC], parts=P)
        val_dst = b.take([EC], parts=P)
        val_loc = b.take([EC], parts=P)
        cnt = b.take([NB], parts=P)
        n_tiles = b.take([NB], parts=P)
        incl = b.take([NB], parts=P)
        off = b.take([NB], parts=P)
        n_col = b.take([1], parts=NB)
        ends = b.take([1], parts=NB)
        shift = b.take([T], parts=P)
        past_end = big[0:NB, phase:phase + NQ]
        sorting = b.at
        wave_hot = b.take([G, EC], F16, parts=P)
        wave_at = b.at
        wave_pos = b.take([G, EC], parts=P)
        after = b.at
        b.at = sorting
        col_hot = [(b.take([NQ], F16, parts=P), b.take([128], F16, parts=P), b.take([128], F16, parts=P))
                   for _ in range(8)]
        b.at = max(b.at, after)
        sort_end = b.at
        norm = b.take([T, 2 * H], parts=P)
        features = b.at
        xnT = b.take([G, 2, P])
        hT = b.take([G, 2, P])
        m_rows = b.take([G, D], parts=P)
        raw_w = b.take([8, D])
        wave_pos_flat = big[0:96, wave_at:wave_at + 512]
        bproj_bc = b.take([D], parts=P)
        sq = raw_w.rearrange("p a b -> p (a b)")[0:P, 0:512]

        b = Region(big, phase, sort_end)
        msgs = b.take([GB, D])
        hot_src = b.take([2, GB, P])
        kv = b.take([H, 4, HV])
        kv_lin = b.take([2, 4 * HV])
        kv_diag = b.take([2, 4 * HV])
        v_sum = b.take([H * HV], parts=P)
        idx_ring = b.take([2, 2 * GB], I32)
        b = Region(big, features, NX * 2048)
        pairs = b.take([H, 512], parts=P)
        kd = b.take([2, H, 48], parts=P)
        k_row = b.take([2, H, DH], parts=P)
        v1 = b.take([2, H, HV], parts=P)
        k_diag = b.take([H, DH], parts=P)
        k_tmp = b.take([H, DH], parts=P)
        k_sum = b.take([H], parts=P)
        b.at = features
        q_pairs = b.take([4, 4, P])
        q_row = b.take([H, DH], parts=P)
        q_rest = b.take([H, DH], parts=P)
        q_parts = b.take([H, 3, DH], BF16, parts=P)
        qT = b.take([H, 128], BF16, parts=96)
        q_lin = b.take([2, P])
        q_sq = b.take([2, P])
        y_rcp = b.take([H], parts=P)
        mix_row = b.take([H, DH], parts=P)
        mixT = b.take([2, P])

        bank = [ctx.enter_context(nc.psum_tensor(f"bank{i}", [128, 512], F32)) for i in range(8)]

        def bview(i, a, c, parts=128, at=0):
            return bank[i][0:parts, at:at + a * c].rearrange("p (a c) -> p a c", a=a)

        lin_ps = [bank[2][:, 264:264 + 4 * HV], bank[3][:, 264:264 + 4 * HV]]
        diag_ps = [bank[3][:, 0:4 * HV], bank[3][:, 4 * HV:8 * HV]]
        agg_ps = [bank[4 + k // 2][:, 256 * (k % 2):256 * (k % 2) + 2 * P] for k in range(4)]
        q_partsT_ps = bank[0][0:96, :].bitcast(BF16).rearrange("p (h n) -> p h n", h=H)

        msg_rows = nc.dram_tensor("msg_rows", (N, D), F32).ap()
        xn2_rows = nc.dram_tensor("xn2_rows", (N, D), F32).ap()
        moe_rows = nc.dram_tensor("moe_rows", (2 * N + 2 * SLOT, D), F32).ap()
        tiled = lambda rows: rows.rearrange("(p t) c -> p t c", t=T)

        s = Semaphores(sem)
        m_out = [sem(f"m_out{j}") for j in range(G)]
        msgs_in = [sem(f"msgs_in{k}") for k in range(GB)]
        tok_in = [sem(f"tok_in{k}") for k in range(4)]
        y_out = [sem(f"y_out{k}") for k in range(2)]
        fin_in = [sem(f"fin_in{g}") for g in range(T // G)]

        block = ctx.enter_context(nc.Block())

        def sum_tiles(eng, tile):
            tile(0, 0)
            with eng.Fori(0, (T - 3) // 2) as i:
                tile(i * 2 + 1, 1)
                tile(i * 2 + 2, 0)
            tile(T - 2, 1)

        def at(t, tiles):
            return isinstance(t, int) and t in tiles

        def apart(eng):
            eng.sem_inc(s.apart, 1)

        SMALL = [(bqkv_bc, bqkv.partition_broadcast(P)), (b2_bc, gnn_b2.partition_broadcast(P)),
                 (bsum_bc, gnn_b2.partition_broadcast(P)), (bproj_bc, bproj.partition_broadcast(P)),
                 (temp_t, temperature.rearrange("a h b c -> (a h b c)").partition_broadcast(P)),
                 *[(gnn_b1T[:, k:k + 1], gnn_b1[128 * k:128 * k + 128].rearrange("(p o) -> p o", o=1)) for k in range(2)]]

        @block.sync
        def _(sp):
            xt = tiled(x)
            def load_x(g):
                for lo, hi in ((0, 112), (112, P)):
                    sp.dma_start(x_sb[lo:hi, G * g:G * g + G, :], xt[lo:hi, G * g:G * g + G, :]).then_inc(s.x_in, 16)
            load_x(0)
            sp.dma_start(src_i, src.rearrange("(p e) -> p e", e=EC)).then_inc(s.edges_in, 16)
            sp.dma_start(dst_i, dst.rearrange("(p e) -> p e", e=EC)).then_inc(s.edges_in, 16)
            sp.dma_start(w1_sb, gnn_w1.rearrange("(k p) f -> p k f", p=128)).then_inc(s.gnn_in, 16)
            sp.dma_start(w2_sb, gnn_w2.rearrange("(k p) f -> p k f", p=128)).then_inc(s.gnn_in, 16)
            for g in range(1, T // G):
                sp.wait_ge(s.x_in, 32 * g)
                load_x(g)
                if g == 1:
                    sp.dma_start(raw_w[:, 0:6, :], Wqkv.rearrange("(k p) c -> p k c", p=128)).then_inc(s.raw_in, 16)
                    sp.dma_start(raw_w[:, 6:8, :], Wproj.rearrange("(k p) c -> p k c", p=128)).then_inc(s.raw_in, 16)
                    for view, dram in SMALL:
                        sp.dma_start(view, dram).then_inc(s.bias_in, 16)
            with sp.Fori(0, T // G) as g:
                for j in range(G):
                    sp.wait_ge(s.m_biased, g * G + j + 1)
                    sp.dma_start(tiled(msg_rows)[:, bass.ds(g * G + j, 1), :].rearrange("p a c -> p (a c)"),
                                 m_rows[:, j, :]).then_inc(m_out[j], 16)
            sp.dma_start(gate_w_sb, gate_w.rearrange("(k p) e -> p k e", p=128)).then_inc(s.gate_in, 16)
            sp.dma_start(gate_b_bc, gate_b.partition_broadcast(P)).then_inc(s.gate_in, 16)
            def load_expert(e):
                sp.dma_start(experts[:, e, 0:1024].rearrange("p (k f) -> p k f", k=2),
                             ffn_w1[e].rearrange("(k p) f -> p k f", p=128)).then_inc(s.w_in, 16)
                sp.dma_start(experts[:, e, 1024:2048].rearrange("p (c h) -> p c h", c=4),
                             ffn_w2[e].rearrange("(c p) h -> p c h", p=128)).then_inc(s.w_in, 16)

            sp.wait_ge(s.x_ok, T)
            sp.dma_start(b1_rows, ffn_b1.rearrange("e (c p) -> (e c) p", p=128)).then_inc(s.gate_in, 16)
            early = phase // 2048
            for e in range(early):
                load_expert(e)
            sp.wait_ge(s.agg_add, NBATCH * GB)
            for e in range(early, NX):
                load_expert(e)
            sp.wait_ge(s.tok_mm, 1)
            sp.dma_start(b2_x, ffn_b2.partition_broadcast(128)).then_inc(s.late_in, 16)
            sp.dma_start(gamma_bc, gamma.partition_broadcast(P)).then_inc(s.late_in, 16)
            sp.dma_start(beta_bc, beta.partition_broadcast(P)).then_inc(s.late_in, 16)
            for k in range(2):
                sp.wait_ge(y_out[k], 16 * (NT // 2))
            for g in range(T // G):
                rows = slice(G * g, G * g + G)
                for view, dram in ((pick0, moe_rows[0:N]), (pick1, moe_rows[N:2 * N]), (own, xn2_rows)):
                    for lo, hi in ((0, 112), (112, P)):
                        sp.dma_start(view[lo:hi, rows, :], tiled(dram)[lo:hi, rows, :]).then_inc(fin_in[g], 16)
            for g in range(T // G):
                rows = slice(G * g, G * g + G)
                sp.wait_ge(s.fin_ok, G * g + G)
                for lo, hi in ((0, 112), (112, P)):
                    sp.dma_start(tiled(out)[lo:hi, rows, :], pick0[lo:hi, rows, :]).then_inc(s.stored, 16)
            sp.wait_ge(s.stored, 32 * (T // G))

        @block.gpsimd
        def _(pool):
            chain = Chain(pool, s.pool_chain)
            def zero(ap):
                chain.add(pool.memset(ap, 0.0))
            zero(ident)
            zero(tri)
            zero(tri_in)
            zero(row0)
            zero(head_mask)
            pool.memset(ones, 1.0)
            pool.memset(eps_t, LN_EPS)
            chain.add(pool.memset(pair_w, 0.5 / N))
            pool.iota(iota_q, [[1, NQ]], base=0, channel_multiplier=0, allow_small_or_imprecise_dtypes=True)
            pool.iota(iota_r, [[1, 128]], base=0, channel_multiplier=0, allow_small_or_imprecise_dtypes=True)
            pool.iota(iota_loc, [[1, P]], base=1, channel_multiplier=0, allow_small_or_imprecise_dtypes=True)
            pool.iota(iota_x, [[1, NX]], base=0, channel_multiplier=0, allow_small_or_imprecise_dtypes=True)
            pool.iota(tok_val, [[1, T], [0, 2]], base=-MID, channel_multiplier=T, allow_small_or_imprecise_dtypes=True)
            pool.iota(tok_pick, [[0, T], [1, 2]], base=1, channel_multiplier=0, allow_small_or_imprecise_dtypes=True)
            chain.wait()
            pool.affine_select(out=ident, in_=ident, compare_op=ALU.not_equal, fill=1.0, base=0,
                               pattern=[[-1, 128]], channel_multiplier=1)
            pool.affine_select(out=tri, in_=tri, compare_op=ALU.is_ge, fill=1.0, base=0,
                               pattern=[[-1, P]], channel_multiplier=1)
            pool.affine_select(out=tri_in, in_=tri_in, compare_op=ALU.is_gt, fill=1.0, base=0,
                               pattern=[[-1, NB]], channel_multiplier=1)
            pool.affine_select(out=row0, in_=row0, compare_op=ALU.is_gt, fill=1.0, base=0,
                               pattern=[[0, P]], channel_multiplier=1)
            def alone(ins):
                chain.add(ins)
                chain.wait()

            alone(pool.memset(trash_pad, 0.0))
            for h in range(4):
                alone(pool.memset(head_mask[32 * h:32 * h + 32, h:h + 1], 1.0))
            alone(pool.memset(pair_w[96:128, 3:4], 0.25 / N))
            pool.tensor_copy(ident_h, ident).then_inc(s.consts, 1)
            selw = wave_pos_flat
            chain.add(pool.memset(selw, 0.0))
            chain.wait()
            for base, step in ((0, 0), (-1, -1), (31, -1)):
                for k in range(3):
                    v = selw[32 * k:32 * k + 32, :].rearrange("p (d i) -> p d i", i=32)
                    alone(pool.affine_select(out=v, in_=v, compare_op=ALU.not_equal, fill=1.0, base=base,
                                             pattern=[[step, 16], [-1, 32]], channel_multiplier=1))
            pool.tensor_copy(sel.rearrange("p a b -> p (a b)"), selw).then_inc(s.preps, 1)
            pool.wait_ge(s.bias_in, 16 * len(SMALL))
            pool.tensor_tensor(bsum_bc, bsum_bc, bproj_bc, ALU.add).then_inc(s.preps, 1)
            pool.tensor_scalar(temp_t, temp_t, SCALE2, None, ALU.mult).then_inc(s.preps, 1)
            def halve(t):
                part = sq.rearrange("p (h d) -> p h d", h=2 * H)
                pool.wait_ge(s.sq_ok, t + 1)
                for w in (16, 8, 4, 2):
                    chain.add(pool.tensor_tensor(part[:, :, 0:w], part[:, :, 0:w], part[:, :, w:2 * w], ALU.add))
                    chain.wait()
                pool.tensor_tensor(norm[:, bass.ds(t, 1), :].rearrange("p a h -> p (a h)").unsqueeze(2),
                                   part[:, :, 0:1], part[:, :, 1:2], ALU.add).then_inc(s.norm_part, 1)

            def front(g):
                for j in range(G):
                    t = g * G + j
                    pool.wait_ge(s.qkv_evac, t + 1)
                    row = qkv[:, bass.ds(t, 1), :].rearrange("p a c -> p (a c)")
                    pool.tensor_tensor(row, row, bqkv_bc, ALU.add).then_inc(s.qkv_biased, 1)
                    pool.wait_ge(s.m_evac, t + 1)
                    pool.tensor_tensor(m_rows[:, j, :], m_rows[:, j, :], b2_bc, ALU.add).then_inc(s.m_biased, 1)
                    if not at(t, (0,)):
                        halve(t - 1)

            front(0)
            with pool.Fori(1, T // G) as g:
                chain.enter(g, 1, 4 * G)
                front(g)
            chain.leave(T // G - 1)
            halve(T - 1)
            for j in range(G):
                pool.wait_ge(m_out[j], 16 * (T // G))
            chain.add(pool.memset(v1[:, :, :, 0:1], 1.0))
            chain.wait()
            pool.memset(trash_pad, 0.0).then_inc(s.v1_ones, 1)
            pool.wait_ge(s.preps, 3)
            pool.wait_ge(s.norm_ok, 1)

            def k_features(t, turn):
                k = kd[:, turn, :, :]
                if not at(t, (0, 1)):
                    pool.wait_ge(s.k_diag_ok, t - 1)
                    pool.wait_ge(s.k_row_ok, t - 1)
                heads = qkv[:, bass.ds(t, 1), D:2 * D].rearrange("p a (h d) -> p (a h) d", h=H)
                by = norm[:, bass.ds(t, 1), H:2 * H].rearrange("p a h -> p (a h)").unsqueeze(2)
                pool.tensor_tensor(k[:, :, 0:DH], heads, by.broadcast_to([P, H, DH]), ALU.mult)
                pool.tensor_tensor(k[:, :, DH:48], heads[:, :, 0:16], by.broadcast_to([P, H, 16]), ALU.mult).then_inc(s.kd_ok, 1)
                rows = x_sb[:, bass.ds(t, 1), :].rearrange("p a c -> p (a c)")
                pool.tensor_tensor(rows, rows, bsum_bc, ALU.add)
                pool.wait_ge(s.kd_ok, t + 1)
                for h in range(H):
                    if not at(t, (0,)):
                        pool.wait_ge(s.head_mm, t * H + h - (H - 1))
                    pool.tensor_tensor(pairs[:, h, :].rearrange("p (d i) -> p d i", i=DH),
                                       k[:, h, 0:DH].unsqueeze(1).broadcast_to([P, 16, DH]),
                                       windows(k[:, h, 1:DH + 1], 16, 1), ALU.mult).then_inc(s.pairs_ok, 1)

            sum_tiles(pool, k_features)
            k_features(T - 1, 0)
            pool.wait_ge(s.sorted_ok, 1)

            def gather(n, half):
                pool.tensor_copy(idx_ring[:, half, :], edge_idx[:, bass.ds(n * 2 * GB, 2 * GB)]).then_inc(s.msg_idx_ok, 1)
                pool.wait_ge(s.msg_idx_ok, n + 1)
                for k in range(2 * GB):
                    if not (at(n, (0,)) and k < GB):
                        pool.wait_ge(s.agg_mm, n * 2 * GB + k - (GB - 1))
                        apart(pool)
                    pool.indirect_dma_start(msgs[:, k % GB, :], None, msg_rows,
                                            bass.IndirectOffsetOnAxis(idx_ring[:, half, k:k + 1], 0)).then_inc(msgs_in[k % GB], 16)

            gather(0, 0)
            gather(1, 1)
            with pool.Fori(1, NBATCH // 4) as i:
                gather(i * 2, 0)
                gather(i * 2 + 1, 1)
            pool.wait_ge(s.agg_add, NBATCH * GB)
            pool.iota(trash, [[0, NT // 2], [SLOT, 2]], base=3 * N - MID, channel_multiplier=1,
                      allow_small_or_imprecise_dtypes=True).then_inc(s.trash_ok, 1)
            with pool.Fori(0, T // G) as g:
                pool.wait_ge(s.xn2_ok, g * G + G)
                pool.dma_start(tiled(xn2_rows)[:, bass.ds(g * G, G), :], xn2).then_inc(s.xn2_out, 16)
            pool.wait_ge(s.xn2_out, 16 * (T // G))
            pool.wait_ge(s.tok_ok, 1)
            pool.wait_ge(s.tok_mm, 1)

            def gather_tokens(n):
                if n >= 4:
                    pool.wait_ge(s.tokT_mm, n - 3)
                pool.indirect_dma_start(tok_rows[:, n % 4, :], None, xn2_rows,
                                        bass.IndirectOffsetOnAxis(tok_gather[:, n:n + 1], 0)).then_inc(tok_in[n % 4], 16)

            for n in range(4):
                gather_tokens(n)
            for n in range(NT):
                if n + 4 < NT:
                    gather_tokens(n + 4)
                pool.wait_ge(s.y_ok, n + 1)
                pool.indirect_dma_start(moe_rows, bass.IndirectOffsetOnAxis(tok_scatter[:, n:n + 1], 0),
                                        y_rows[:, n % 2, :], None).then_inc(y_out[n % 2], 16)
                if n == 8:
                    pool.wait_ge(s.late_in, 48)
                    with pool.Fori(0, T) as t:
                        rows = x_sb[:, bass.ds(t, 1), :].rearrange("p a c -> p (a c)")
                        pool.tensor_tensor(rows, rows, beta_bc, ALU.add).then_inc(s.beta_ok, 1)
            pool.wait_ge(s.beta_ok, T)
            for t in range(T):
                pool.wait_ge(s.fin_norm, t + 1)
                chain.add(pool.tensor_tensor(pick0[:, t, :], pick0[:, t, :], gamma_bc, ALU.mult))
                chain.wait()
                pool.tensor_tensor(pick0[:, t, :], pick0[:, t, :], x_sb[:, t, :], ALU.add).then_inc(s.fin_ok, 1)

        @block.scalar
        def _(act):
            act.wait_ge(s.consts, 1)
            def root(lo, hi, n):
                act.wait_ge(s.ln_stats, n)
                act.activation(rstd[:, lo:hi], mv[:, lo:hi, 1], ACT.Sqrt, bias=eps_t).then_inc(s.rstd_sd, 1)

            root(0, G, 1)
            for k in range(4):
                act.wait_ge(s.wT_mm, k + 1)
                got = bview(4 + k, 4, 128)
                if k < 3:
                    for i in range(2):
                        last = act.activation(wqkvT[:, :, (2 * k + i) * 128:(2 * k + i + 1) * 128],
                                              got[:, 2 * i:2 * i + 2, :], ACT.Copy)
                else:
                    for i in range(2):
                        last = act.activation(wprojT[:, :, i * 128:(i + 1) * 128], got[:, 2 * i:2 * i + 2, :], ACT.Copy)
                last.then_inc(s.act_chain, 1)

            act.wait_ge(s.gnn_in, 32)
            act.wait_ge(s.bias_in, 16 * len(SMALL))

            def evac_xnT(g, j):
                t = g * G + j
                act.wait_ge(s.xnT_mm, t + 1)
                if j == 0 and not at(g, (0,)):
                    act.wait_ge(s.qkv_mm, g * G)
                act.activation(xnT[:, j, :, :], bview(j % 2, 2, P), ACT.Copy)
                act.activation(node[:, bass.ds(t, 1), :].rearrange("p a c -> p (a c)")[:, 0:2 * P],
                               bank[j % 2][:, 0:2 * P], ACT.Copy).then_inc(s.xnT_ready, 1)

            def squares(t):
                act.wait_ge(s.qkv_biased, t + 1)
                if not at(t, (0,)):
                    act.wait_ge(s.norm_part, t)
                apart(act)
                act.activation(sq, qkv[:, bass.ds(t, 1), 0:2 * D].rearrange("p a c -> p (a c)"), ACT.Square).then_inc(s.sq_ok, 1)

            def front(g, rows_follow):
                evac_xnT(g, 0)
                for j in range(G):
                    t = g * G + j
                    act.wait_ge(s.l1_mm, t + 1)
                    for k in range(2):
                        last = act.activation(hT[:, j, k, :], bview(2 + j % 2, 2, P)[:, k, :], ACT.Relu, bias=gnn_b1T[:, k:k + 1])
                    last.then_inc(s.h_ready, 1)
                    if rows_follow:
                        act.activation(xn_rows[:, j, :], x_sb[:, bass.ds(t + G, 1), :].rearrange("p a c -> p (a c)"), ACT.Identity,
                                       scale=rstd[:, bass.ds(t + G, 1)], bias=shift[:, bass.ds(t + G, 1)]).then_inc(s.xn_row_ok, 1)
                    if j < G - 1:
                        evac_xnT(g, j + 1)
                    act.wait_ge(s.qkv_mm, t + 1)
                    for half in range(2):
                        last = act.activation(qkv[:, bass.ds(t, 1), 384 * half:384 * half + 384].rearrange("p a c -> p (a c)"),
                                              bank[5 + half][0:P, 0:384], ACT.Copy)
                    last.then_inc(s.qkv_evac, 1)
                    act.wait_ge(s.m_mm, t + 1)
                    if not at(g, (0,)):
                        act.wait_ge(m_out[j], g * 16)
                    act.activation(m_rows[:, j, :], bank[4][0:P, 0:D], ACT.Copy).then_inc(s.m_evac, 1)
                    if not at(t, (0,)):
                        squares(t - 1)
                    if at(t, (2,)):
                        root(G, T, 2)

            front(0, False)
            act.wait_ge(s.ln_stats, 3)
            with act.Fori(1, T // G - 1) as g:
                front(g, True)
            front(T // G - 1, False)
            squares(T - 1)
            act.wait_ge(s.norm_part, T)
            act.activation(norm[:, :, 0:H], norm[:, :, 0:H], ACT.Sqrt, scale=SCALE2)
            act.activation(norm[:, :, H:2 * H], norm[:, :, H:2 * H], ACT.Sqrt).then_inc(s.norm_root, 1)

            act.wait_ge(s.v1_ones, 1)

            def k_rows(t, turn):
                act.wait_ge(s.kd_ok, t + 1)
                if not at(t, (0, 1)):
                    act.wait_ge(s.lin_mm, t - 1)
                act.activation(k_row[:, turn, :, :], kd[:, turn, :, 0:DH], ACT.Copy).then_inc(s.k_row_ok, 1)
                if not at(t, (0, 1)):
                    act.wait_ge(s.head_mm, t * H - H)
                    act.wait_ge(s.diag_mm, t - 1)
                apart(act)
                act.activation(v1[:, turn, :, 1:HV], qkv[:, bass.ds(t, 1), 2 * D:3 * D].rearrange("p a (h d) -> p (a h) d", h=H),
                               ACT.Copy).then_inc(s.v1_ok, 1)

            sum_tiles(act, k_rows)
            k_rows(T - 1, 0)

            def qT_of(t):
                act.wait_ge(s.q_partsT_mm, t + 1)
                if not at(t, (0,)):
                    act.wait_ge(s.sel_mm, t * H)
                act.activation(qT[:, :, 0:P], q_partsT_ps[:, :, 0:P], ACT.Copy).then_inc(s.qT_ok, 1)
                act.wait_ge(s.qnT_mm, t + 1)
                if not at(t, (0,)):
                    act.wait_ge(s.y_ld_mm, t)
                act.activation(q_lin, bview(1, 2, P), ACT.Copy)
                act.activation(q_sq, bview(1, 2, P), ACT.Square).then_inc(s.q_ld_ok, 1)

            def mixT_of(t):
                act.wait_ge(s.mixT_mm, t + 1)
                act.activation(mixT, bview(6, 2, P), ACT.Copy).then_inc(s.mixT_ok, 1)

            def q_tile(t):
                for h in range(H):
                    act.wait_ge(s.sel_mm, t * H + h + 1)
                    if not (at(t, (0,)) and h < 4):
                        act.wait_ge(s.y_mm, t * H + h - 3)
                    act.activation(q_pairs[:, h % 4, :, :], bview(2 + h % 2, 4, P), ACT.Square).then_inc(s.q_pairs_ok, 1)
                    if h == 1 and not at(t, (0,)):
                        mixT_of(t - 1)
                if not at(t, (T - 1,)):
                    qT_of(t + 1)

            act.wait_ge(s.kv_ok, 1)
            qT_of(0)
            q_tile(0)
            with act.Fori(1, T - 1) as t:
                q_tile(t)
            q_tile(T - 1)
            mixT_of(T - 1)

            act.wait_ge(s.b1_mm, 1)
            act.activation(b1T, bank[7][:, 0:NX * 4], ACT.Copy).then_inc(s.b1_ok, 1)

            def second_pass(g):
                for j in range(G):
                    t = g * G + j
                    act.wait_ge(s.f1_mm, t + 1)
                    act.wait_ge(s.f2_mm, t - 1 if j >= 2 else g * G)
                    for k in range(2):
                        last = act.activation(hT2[:, j % 2, k, :], bview(j % 2, 2, P)[:, k, :], ACT.Relu, bias=gnn_b1T[:, k:k + 1])
                    last.then_inc(s.h2_ok, 1)
                act.wait_ge(s.ln2_stats, g + 1)
                act.activation(rstd[:, 0:G], mv[:, 0:G, 1], ACT.Sqrt, bias=eps_t).then_inc(s.ln2_root, 1)

            def xn2T_of(g):
                for j in range(G):
                    t = g * G + j
                    act.wait_ge(s.xn2T_mm, t + 1)
                    act.wait_ge(s.gate_mm, t - 1 if j >= 2 else g * G)
                    act.activation(xn2T[:, j % 2, :, :], bview(3 + j % 2, 2, P), ACT.Copy).then_inc(s.xn2T_ok, 1)

            second_pass(0)
            with act.Fori(1, T // G) as g:
                second_pass(g)
                xn2T_of(g - 1)
            xn2T_of(T // G - 1)
            act.wait_ge(s.gap_ok, 1)
            act.activation(weight[:, :, 1:2], weight[:, :, 0:1], ACT.Exp).then_inc(s.exp_ok, 1)

            act.wait_ge(s.tok_ok, 1)
            act.wait_ge(s.b1_ok, 1)

            def relu_tile(i, j, expert):
                n = i * 4 + 1 + j
                act.wait_ge(s.hidT_mm, n + 1)
                if not (isinstance(i, int) and n < 2):
                    act.wait_ge(s.ffn2_mm, n - 1)
                apart(act)
                for c in range(4):
                    last = act.activation(hidT[:, (1 + j) % 2, c, :], bview(4 + (1 + j) % 2, 4, 128)[:, c, :], ACT.Relu,
                                          bias=b1T[:, bass.ds(expert * 4 + c, 1)])
                last.then_inc(s.relu_ok, 1)

            def hid_tile(i, j):
                n = i * 4 + 2 + j
                act.wait_ge(s.ffn1_mm, n + 1)
                if not (isinstance(i, int) and n < 2):
                    act.wait_ge(s.hidT_mm, n - 1)
                act.activation(hid[:, j % 2, :], bank[2 + j % 2][:, :], ACT.Copy).then_inc(s.hid_ok, 1)

            def chosen(at, count):
                return nc.values_load_multi_w_load_instructions(
                    tok_expert[:, bass.ds(at, count)], engines=[mybir.EngineType.Activation], min_val=0, max_val=NX - 1,
                    skip_runtime_bounds_check_because="clamped to the last expert when written")[1]

            e = chosen(0, 1)
            hid_tile(-1, 2)
            hid_tile(-1, 3)
            relu_tile(-1, 3, e[0])
            with act.Fori(0, (NT - 4) // 4) as i:
                e = chosen(i * 4 + 1, 4)
                for j in range(4):
                    hid_tile(i, j)
                    relu_tile(i, j, e[j])
            i = (NT - 4) // 4
            e = chosen(NT - 3, 3)
            for j in range(2):
                hid_tile(i, j)
                relu_tile(i, j, e[j])
            relu_tile(i, 2, e[2])
            for g in range(T // G):
                act.wait_ge(s.fin_stats, g + 1)
                act.activation(rstd[:, g * G:g * G + G], mv[:, g * G:g * G + G, 1], ACT.Sqrt, bias=eps_t).then_inc(s.fin_root, 1)

        @block.vector
        def _(dve):
            chain = Chain(dve, s.dve_chain)
            def step(ins):
                chain.add(ins)
                chain.wait()

            def moments(lo, hi):
                for t in range(lo, hi):
                    if t % G == 0:
                        dve.wait_ge(s.x_in, 32 * (t // G + 1))
                    last = dve.bn_stats(stats[:, t, :], x_sb[:, t, :])
                step(last)
                for t in range(lo, hi):
                    last = dve.bn_aggr(mv[:, t, :], stats[:, t, :])
                last.then_inc(s.ln_stats, 1)

            def inverse(lo, hi, n):
                dve.wait_ge(s.rstd_sd, n)
                step(dve.reciprocal(rstd[:, lo:hi], rstd[:, lo:hi]))

            def normalise(g):
                if g:
                    dve.wait_ge(s.xnT_mm, G * g)
                for j in range(G):
                    t = g * G + j
                    dve.tensor_scalar(xn_rows[:, j, :], x_sb[:, t, :], mv[:, t, 0:1], rstd[:, t:t + 1],
                                      ALU.subtract, ALU.mult).then_inc(s.xn_ready, 1)

            moments(0, G)
            inverse(0, G, 1)
            normalise(0)
            moments(G, T)
            dve.wait_ge(s.edges_in, 32)
            step(dve.tensor_scalar(loc_f, src_i, 0.5, 1.0 / T, ALU.add, ALU.mult))
            step(dve.tensor_scalar(loc_f, loc_f, -0.5, MAGIC, ALU.add, ALU.add))
            step(dve.tensor_scalar(loc_f, loc_f, MAGIC, None, ALU.subtract))
            step(dve.scalar_tensor_tensor(bkt_h, loc_f, -float(T), src_i, ALU.mult, ALU.add))
            dve.tensor_scalar(val_dst, dst_i, -float(MID), None, ALU.add)
            dve.tensor_scalar(val_loc, loc_f, 1.0, None, ALU.add)
            for w in range(NB // G):
                for j in range(G):
                    last = dve.tensor_scalar(wave_hot[:, j, :], bkt_h, float(w * G + j), 0.0, ALU.is_equal, ALU.add,
                                             accum_out=cnt[:, w * G + j:w * G + j + 1])
                chain.add(last)
                chain.wait()
                if w == 2:
                    inverse(G, T, 2)
                    dve.scalar_tensor_tensor(shift[:, G:T], mv[:, G:T, 0], -1.0, rstd[:, G:T], ALU.mult,
                                             ALU.mult).then_inc(s.ln_stats, 1)
                    normalise(1)
            dve.memset(pos, 0.0).then_inc(s.cnt_ok, 1)
            dve.wait_ge(s.prefix_mm, 1)
            before, total, col = bank[7][0:P, 0:NB], bank[7][0:P, 64:64 + NB], bank[7][0:NB, 128:129]
            half = (SLOT - 1) / 2.0
            for dst_, src_ in ((n_tiles, total), (n_col, col)):
                chain.add(dve.tensor_scalar(dst_, src_, half, 1.0 / SLOT, ALU.add, ALU.mult))
            chain.wait()
            for dst_ in (n_tiles, n_col):
                chain.add(dve.tensor_scalar(dst_, dst_, MAGIC, None, ALU.add))
            chain.wait()
            chain.add(dve.tensor_scalar(n_tiles, n_tiles, MAGIC, None, ALU.subtract))
            dve.tensor_scalar(n_col, n_col, MAGIC, None, ALU.subtract).then_inc(s.n_col_ok, 1)
            chain.wait()
            step(dve.tensor_tensor_scan(incl, ones[0:P, 0:NB], n_tiles, 0.0, ALU.mult, ALU.add))
            step(dve.tensor_tensor(incl, incl, n_tiles, ALU.subtract))
            step(dve.scalar_tensor_tensor(off, incl, float(SLOT), before, ALU.mult, ALU.add))
            step(dve.tensor_scalar(off, off, -1.0, None, ALU.add))
            dve.wait_ge(s.preps, 1)
            for w in range(NB // G):
                for j in range(G):
                    last = dve.tensor_scalar(wave_hot[:, j, :], bkt_h, float(w * G + j), None, ALU.is_equal)
                step(last)
                for j in range(G):
                    last = dve.tensor_tensor_scan(wave_pos[:, j, :], ones[0:P, 0:1].broadcast_to([P, EC]), wave_hot[:, j, :],
                                                  off[:, w * G + j:w * G + j + 1], ALU.mult, ALU.add)
                step(last)
                step(dve.tensor_tensor(wave_pos, wave_pos, wave_hot, ALU.mult))
                for j in range(G):
                    step(dve.tensor_tensor(pos, pos, wave_pos[:, j, :], ALU.add))
            step(dve.tensor_scalar(slot_q, pos, -half, 1.0 / SLOT, ALU.add, ALU.mult))
            step(dve.tensor_scalar(slot_q, slot_q, MAGIC, None, ALU.add))
            step(dve.tensor_scalar(slot_q, slot_q, MAGIC, None, ALU.subtract))
            step(dve.scalar_tensor_tensor(slot_r, slot_q, -float(SLOT), pos, ALU.mult, ALU.add))
            def columns(i, which):
                for c in which:
                    hot_q, hot_d, hot_l = col_hot[c % 8]
                    col = lambda a: a[:, bass.ds(i * 16 + c, 1)]
                    if c >= 8 or not at(i, (0,)):
                        dve.wait_ge(s.col_mm, i * 16 + c - 7)
                    dve.tensor_scalar(hot_q, iota_q[0:P, :], col(slot_q), None, ALU.is_equal)
                    dve.tensor_scalar(hot_d, iota_r[0:P, :], col(slot_r), col(val_dst), ALU.is_equal, ALU.mult)
                    dve.tensor_scalar(hot_l, iota_r[0:P, :], col(slot_r), col(val_loc), ALU.is_equal, ALU.mult).then_inc(s.col_hot_ok, 1)

            columns(0, range(16))
            dve.wait_ge(s.norm_root, 1)
            step(dve.tensor_scalar(norm, norm, 1e-12, None, ALU.max))
            step(dve.reciprocal(norm, norm))
            dve.tensor_tensor(norm[:, :, 0:H], norm[:, :, 0:H], temp_t.unsqueeze(1).broadcast_to([P, T, H]), ALU.mult)
            dve.tensor_scalar(norm[:, :, H:2 * H], norm[:, :, H:2 * H], SCALE2 ** 0.5, None, ALU.mult).then_inc(s.norm_ok, 1)

            def k_tile(t, turn):
                k = kd[:, turn, :, 0:DH]
                for h in range(H):
                    if not at(t, (T - 1,)):
                        columns(t + 1, (2 * h, 2 * h + 1))
                    if h == 1:
                        dve.wait_ge(s.kd_ok, t + 1)
                        chain.add(dve.reduce_sum(k_sum, k, axis=AX.X))
                    if h == 2:
                        chain.wait()
                        chain.add(dve.scalar_tensor_tensor(k_tmp, k, 2.0, k_sum.unsqueeze(2).broadcast_to([P, H, DH]),
                                                           ALU.mult, ALU.subtract))
                    if h == 3:
                        chain.wait()
                        if not at(t, (0,)):
                            dve.wait_ge(s.diag_mm, t)
                        dve.tensor_tensor(k_diag, k, k_tmp, ALU.mult).then_inc(s.k_diag_ok, 1)

            def chained(t, turn):
                if isinstance(t, int):
                    k_tile(t, turn)
                else:
                    if turn == 1:
                        chain.enter(t, 1, 2)
                    k_tile(t, turn)
                    if turn == 0:
                        chain.n -= 2
                        chain.leave(T - 3)

            sum_tiles(dve, chained)
            dve.wait_ge(s.ends_mm, 1)
            step(dve.tensor_copy(ends, bank[7][0:NB, 0:1]))
            dve.tensor_scalar(past_end, iota_q[0:NB, :], ends, None, ALU.is_ge).then_inc(s.past_ok, 1)
            dve.wait_ge(s.bucket_mm, 1)
            dve.tensor_scalar(edge_bucket, bank[7][0:1, 0:NQ], float(NB - 1), None, ALU.min)
            dve.wait_ge(s.col_mm, EC)
            dve.tensor_scalar(edge_idx, bank[4][:, 0:NQ], float(MID), None, ALU.add)
            dve.tensor_copy(edge_loc, bank[5][:, 0:NQ]).then_inc(s.sorted_ok, 1)

            def hot_batch(n, turn):
                dve.tensor_tensor(hot_src[:, turn, :, :], iota_loc.unsqueeze(1).broadcast_to([128, GB, P]),
                                  edge_loc[:, bass.ds(n * GB, GB)].unsqueeze(2).broadcast_to([128, GB, P]),
                                  ALU.is_equal).then_inc(s.hot_src_ok, 1)

            def buckets(m, count):
                return nc.values_load_multi_w_load_instructions(
                    edge_bucket[:, bass.ds(m, count)], engines=[mybir.EngineType.DVE], min_val=0, max_val=NB - 1,
                    skip_runtime_bounds_check_because="clamped to the last bucket when written")[1]

            def add_pair(m, half, bucket):
                dve.wait_ge(s.agg_mm, m + 2)
                for j in range(2):
                    if not at(m + j, (0,)):
                        dve.wait_ge(s.agg_add, m + j)
                    rows = node[:, bass.ds(bucket[j], 1), 0:2 * P].rearrange("p a c -> p (a c)")
                    dve.tensor_tensor(rows, rows, agg_ps[2 * half + j], ALU.add).then_inc(s.agg_add, 1)

            dve.wait_ge(s.sorted_ok, 1)
            dve.wait_ge(s.xnT_ready, T)
            hot_batch(0, 0)
            hot_batch(1, 1)
            k_tile(T - 1, 0)
            dve.wait_ge(s.head_mm, T * H)
            dve.wait_ge(s.diag_mm, T)
            for i in range(3):
                n = min(3, H - 3 * i)
                dve.tensor_tensor(kv[:, 3 * i:3 * i + n, :, :],
                                  bank[i][:, 0:n * 4 * HV].rearrange("p (h c e) -> p h c e", h=n, c=4),
                                  pair_w.unsqueeze(1).unsqueeze(3).broadcast_to([128, n, 4, HV]), ALU.mult)
            for i in range(2):
                mask = head_mask.unsqueeze(2).broadcast_to([128, 4, HV])
                dve.scalar_tensor_tensor(kv_lin[:, i, :].rearrange("p (h e) -> p h e", h=4),
                                         lin_ps[i].rearrange("p (h e) -> p h e", h=4), SCALE2 / N, mask, ALU.mult, ALU.mult)
                dve.scalar_tensor_tensor(kv_diag[:, i, :].rearrange("p (h e) -> p h e", h=4),
                                         diag_ps[i].rearrange("p (h e) -> p h e", h=4), 0.5 / N, mask, ALU.mult, ALU.mult)
            dve.tensor_scalar(v_sum, bank[6][0:P, 0:H * HV], SCALE2 ** 2 / N, None, ALU.mult).then_inc(s.kv_ok, 1)

            def split(t, part):
                if part == 0:
                    if not at(t, (0,)):
                        dve.wait_ge(s.qnT_mm, t)
                    chain.add(dve.tensor_tensor(
                        q_row, qkv[:, bass.ds(t, 1), 0:D].rearrange("p a (h d) -> p (a h) d", h=H),
                        norm[:, bass.ds(t, 1), 0:H].rearrange("p a h -> p (a h)").unsqueeze(2).broadcast_to([P, H, DH]), ALU.mult))
                if part == 1:
                    if not at(t, (0,)):
                        dve.wait_ge(s.q_partsT_mm, t)
                    chain.wait()
                    chain.add(dve.tensor_copy(q_parts[:, :, 0, :], q_row))
                if part == 2:
                    chain.wait()
                    chain.add(dve.tensor_tensor(q_rest, q_row, q_parts[:, :, 0, :], ALU.subtract))
                if part == 3:
                    chain.wait()
                    chain.add(dve.tensor_copy(q_parts[:, :, 1, :], q_rest))
                if part == 4:
                    chain.wait()
                    dve.tensor_tensor(q_parts[:, :, 2, :], q_rest, q_parts[:, :, 1, :], ALU.subtract).then_inc(s.split_ok, 1)

            def add_mix(t):
                dve.wait_ge(s.proj_mm, t + 1)
                rows = x_sb[:, bass.ds(t, 1), :].rearrange("p a c -> p (a c)")
                dve.tensor_tensor(rows, rows, bank[6][0:P, 256:512], ALU.add).then_inc(s.x_ok, 1)

            def q_tile(t):
                m = (t + 1) * 2 * GB
                bucket = buckets(m - 2, 2 * GB)
                for h in range(H):
                    add_pair(m + 2 * h - 2, (h + 1) % 2, bucket[2 * h:2 * h + 2])
                    if h == 0:
                        if not at(t, (0,)):
                            hot_batch(t * 2 + 3, 1)
                    if h == 4 and not at(t, (T - 1,)):
                        hot_batch(t * 2 + 4, 0)
                    if h < 5 and not at(t, (T - 1,)):
                        split(t + 1, h)
                    if h == 6 and not at(t, (0,)):
                        add_mix(t - 1)
                dve.wait_ge(s.y_mm, t * H + H)
                y = bank[7][0:P, 0:H * HV].rearrange("p (h e) -> p h e", h=H)
                chain.add(dve.reciprocal(y_rcp.unsqueeze(2), y[:, :, 0:1]))
                chain.wait()
                if not at(t, (0,)):
                    dve.wait_ge(s.mixT_mm, t)
                dve.tensor_tensor(mix_row, y[:, :, 1:HV], y_rcp.unsqueeze(2).broadcast_to([P, H, DH]),
                                  ALU.mult).then_inc(s.mix_row_ok, 1)

            bucket = buckets(0, 2 * GB - 2)
            for h in range(H - 1):
                if h < 5:
                    split(0, h)
                add_pair(2 * h, h % 2, bucket[2 * h:2 * h + 2])
                if h == 3:
                    hot_batch(2, 0)
            dve.wait_ge(s.agg_mm, 2 * GB)
            hot_batch(3, 1)
            q_tile(0)
            with dve.Fori(1, T - 1) as t:
                chain.enter(t, 1, 5)
                q_tile(t)
            chain.leave(T - 2)
            q_tile(T - 1)
            add_mix(T - 1)
            add_pair(NQ - 2, 1, buckets(NQ - 2, 2))

            def second_pass(g, first=False):
                for j in range(G):
                    t = g * G + j
                    dve.wait_ge(s.f2_mm, t + 1)
                    rows = x_sb[:, bass.ds(t, 1), :].rearrange("p a c -> p (a c)")
                    dve.tensor_tensor(rows, rows, bank[2][0:P, 0:D], ALU.add).then_inc(s.x2_add, 1)
                    dve.wait_ge(s.x2_add, t + 1)
                    apart(dve)
                    last = dve.bn_stats(stats[:, j, :], rows)
                chain.add(last)
                chain.wait()
                apart(dve)
                for j in range(G):
                    last = dve.bn_aggr(mv[:, j, :], stats[:, j, :])
                last.then_inc(s.ln2_stats, 1)
                dve.wait_ge(s.ln2_root, g + 1)
                chain.add(dve.reciprocal(rstd[:, 0:G], rstd[:, 0:G]))
                chain.wait()
                dve.wait_ge(s.xn2T_mm, g * G)
                dve.wait_ge(s.xn2_out, g * 16)
                for j in range(G):
                    t = g * G + j
                    rows = x_sb[:, bass.ds(t, 1), :].rearrange("p a c -> p (a c)")
                    dve.tensor_scalar(xn2[:, j, :], rows, mv[:, j, 0:1], rstd[:, j:j + 1], ALU.subtract,
                                      ALU.mult).then_inc(s.xn2_ok, 1)

            def choose(g):
                dve.wait_ge(s.gate_mm, g * G + G)
                dve.tensor_tensor(logits, bview(5, G, NX, P), gate_b_bc.unsqueeze(1).broadcast_to([P, G, NX]),
                                  ALU.add).then_inc(s.gate_ok, 1)
                dve.wait_ge(s.gate_ok, g + 1)
                apart(dve)
                for j in range(G):
                    last = dve.max(top_val[:, j, :], logits[:, j, :])
                chain.add(last)
                chain.wait()
                apart(dve)
                for j in range(G):
                    last = dve.max_index(top_idx[:, j, :], top_val[:, j, :], logits[:, j, :])
                chain.add(last)
                chain.wait()
                dve.tensor_copy(score[:, bass.ds(g * G, G), :], top_val[:, :, 0:2])
                chain.add(dve.tensor_copy(choice[:, bass.ds(g * G, G), :], top_idx[:, :, 0:2]))
                chain.wait()

            dve.wait_ge(s.gate_in, 32)
            second_pass(0)
            with dve.Fori(1, T // G) as g:
                chain.enter(g, 1, 5)
                second_pass(g)
                choose(g - 1)
            chain.leave(T // G - 1)
            choose(T // G - 1)
            dve.tensor_tensor(weight[:, :, 0:1], score[:, :, 1:2], score[:, :, 0:1], ALU.subtract).then_inc(s.gap_ok, 1)
            pick = choice.rearrange("p t k -> p (t k)")
            dve.wait_ge(s.xn2_out, 16 * (T // G))
            step(dve.tensor_tensor(hot_x, iota_x[0:P, :].unsqueeze(2).broadcast_to([P, NX, 2 * T]),
                                   pick.unsqueeze(1).broadcast_to([P, NX, 2 * T]), ALU.is_equal))
            step(dve.tensor_tensor_scan(run_x.rearrange("p e c -> p (e c)"), ones[0:P, 0:1].broadcast_to([P, NX * 2 * T]),
                                        hot_x.rearrange("p e c -> p (e c)"), 0.0, ALU.mult, ALU.add))
            step(dve.tensor_copy(last_slot.unsqueeze(2), run_x[:, :, 2 * T - 1:2 * T]))
            step(dve.tensor_copy(count_x, last_slot))
            dve.tensor_tensor(count_x[:, 1:NX], last_slot[:, 1:NX], last_slot[:, 0:NX - 1], ALU.subtract).then_inc(s.count_ok, 1)
            dve.wait_ge(s.count_ok, 1)
            step(dve.tensor_tensor(last_slot, last_slot, count_x, ALU.subtract))
            dve.wait_ge(s.route_mm, 1)
            for dst_, src_ in ((tiles_x, bank[7][0:P, 128:128 + NX]), (col_x, bank[7][0:NX, 192:193])):
                chain.add(dve.tensor_scalar(dst_, src_, half, 1.0 / SLOT, ALU.add, ALU.mult))
            chain.wait()
            for dst_ in (tiles_x, col_x):
                chain.add(dve.tensor_scalar(dst_, dst_, MAGIC, None, ALU.add))
            chain.wait()
            chain.add(dve.tensor_scalar(tiles_x, tiles_x, MAGIC, None, ALU.subtract))
            dve.tensor_scalar(col_x, col_x, MAGIC, None, ALU.subtract).then_inc(s.col_x_ok, 1)
            chain.wait()
            step(dve.tensor_tensor_scan(incl_x, ones[0:P, 0:NX], tiles_x, 0.0, ALU.mult, ALU.add))
            step(dve.tensor_tensor(incl_x, incl_x, tiles_x, ALU.subtract))
            step(dve.scalar_tensor_tensor(off_x, incl_x, float(SLOT), bank[7][0:P, 64:64 + NX], ALU.mult, ALU.add))
            step(dve.scalar_tensor_tensor(off_x, off_x, -1.0, last_slot, ALU.add, ALU.subtract))
            step(dve.tensor_tensor(run_x, run_x, off_x.unsqueeze(2).broadcast_to([P, NX, 2 * T]), ALU.add))
            step(dve.tensor_tensor(run_x, run_x, hot_x, ALU.mult))
            step(dve.reduce_sum(pos_x, run_x.rearrange("p e c -> p c e"), axis=AX.X))
            step(dve.tensor_scalar(slot_qx, pos_x, -half, 1.0 / SLOT, ALU.add, ALU.mult))
            step(dve.tensor_scalar(slot_qx, slot_qx, MAGIC, None, ALU.add))
            step(dve.tensor_scalar(slot_qx, slot_qx, MAGIC, None, ALU.subtract))
            step(dve.scalar_tensor_tensor(slot_rx, slot_qx, -float(SLOT), pos_x, ALU.mult, ALU.add))
            wide = lambda v, n: v.unsqueeze(2).broadcast_to([P, 2 * T, n])
            dve.tensor_tensor(hot_rx, iota_r[0:P, :].unsqueeze(1).broadcast_to([P, 2 * T, 128]), wide(slot_rx, 128), ALU.is_equal)
            step(dve.tensor_tensor(hot_qx, iota_q[0:P, 0:NT].unsqueeze(1).broadcast_to([P, 2 * T, NT]), wide(slot_qx, NT), ALU.is_equal))
            dve.tensor_tensor(val_qx[:, :, 0, :], hot_qx, wide(tok_val.rearrange("p t k -> p (t k)"), NT), ALU.mult)
            dve.tensor_tensor(val_qx[:, :, 1, :], hot_qx, wide(tok_pick.rearrange("p t k -> p (t k)"), NT),
                              ALU.mult).then_inc(s.tok_hot_ok, 1)
            dve.wait_ge(s.exp_ok, 1)
            step(dve.tensor_scalar(weight[:, :, 0:1], weight[:, :, 1:2], 1.0, None, ALU.add))
            step(dve.reciprocal(weight[:, :, 0:1], weight[:, :, 0:1]))
            chain.add(dve.tensor_tensor(weight[:, :, 1:2], weight[:, :, 1:2], weight[:, :, 0:1], ALU.mult))
            dve.wait_ge(s.ends_x_mm, 1)
            step(dve.tensor_copy(ends_x, bank[6][0:NX, 0:1]))
            dve.tensor_scalar(past_x, iota_q[0:NX, 0:NT], ends_x, None, ALU.is_ge).then_inc(s.past_x_ok, 1)
            dve.wait_ge(s.expert_mm, 1)
            chain.add(dve.tensor_scalar(tok_expert, bank[6][0:1, 64:64 + NT], float(NX - 1), None, ALU.min))
            dve.wait_ge(s.tok_mm, 1)
            ids, picks = bank[5][:, 0:NT], bank[5][:, NT:2 * NT]
            dve.tensor_scalar(tok_gather, ids, float(MID), None, ALU.add)
            dve.wait_ge(s.trash_ok, 1)
            step(dve.scalar_tensor_tensor(unused, picks, 0.0, trash.rearrange("p a b -> p (a b)"), ALU.is_equal, ALU.mult))
            step(dve.scalar_tensor_tensor(out_row, picks, float(N), unused, ALU.mult, ALU.add))
            dve.scalar_tensor_tensor(tok_scatter, ids, float(MID - N), out_row, ALU.add, ALU.add).then_inc(s.tok_ok, 1)

            def tokT_tile(n, par, first=False):
                dve.wait_ge(s.tokT_mm, n + 1)
                if not first:
                    dve.wait_ge(s.ffn1_mm, n - 1)
                dve.tensor_copy(tokT[:, par, :, :], bview(par, 2, 128)).then_inc(s.tokT_ok, 1)

            def y_tile(i, j, expert):
                n = i * 4 + j
                dve.wait_ge(s.ffn2_mm, n + 1)
                dve.wait_ge(y_out[j % 2], (i * 2 + j // 2) * 16)
                dve.tensor_tensor(y_rows[:, j % 2, :], bank[6 + j % 2][:, 0:D],
                                  b2_x[:, bass.ds(expert, 1), :].rearrange("p a c -> p (a c)"), ALU.add).then_inc(s.y_ok, 1)

            def chosen(at, count):
                return nc.values_load_multi_w_load_instructions(
                    tok_expert[:, bass.ds(at, count)], engines=[mybir.EngineType.DVE], min_val=0, max_val=NX - 1,
                    skip_runtime_bounds_check_because="clamped to the last expert when written")[1]

            dve.wait_ge(s.tok_ok, 1)
            for n in range(3):
                tokT_tile(n, n % 2, first=n < 2)
            dve.wait_ge(s.late_in, 48)
            with dve.Fori(0, (NT - 4) // 4) as i:
                e = chosen(i * 4, 4)
                for j in range(4):
                    tokT_tile(i * 4 + 3 + j, (3 + j) % 2)
                    y_tile(i, j, e[j])
            tokT_tile(NT - 1, 1)
            e = chosen(NT - 4, 4)
            for j in range(4):
                y_tile((NT - 4) // 4, j, e[j])

            for g in range(T // G):
                tiles = range(G * g, G * g + G)
                dve.wait_ge(fin_in[g], 6 * 16)
                for t in tiles:
                    last = dve.scalar_tensor_tensor(pick0[:, t, :], pick0[:, t, :], weight[:, t, 0:1], own[:, t, :], ALU.mult, ALU.add)
                step(last)
                for t in tiles:
                    last = dve.scalar_tensor_tensor(pick1[:, t, :], pick1[:, t, :], weight[:, t, 1:2], pick0[:, t, :], ALU.mult, ALU.add)
                step(last)
                for t in tiles:
                    last = dve.bn_stats(stats[:, t, :], pick1[:, t, :])
                step(last)
                for t in tiles:
                    last = dve.bn_aggr(mv[:, t, :], stats[:, t, :])
                last.then_inc(s.fin_stats, 1)
                dve.wait_ge(s.fin_root, g + 1)
                step(dve.reciprocal(rstd[:, G * g:G * g + G], rstd[:, G * g:G * g + G]))
                for t in tiles:
                    dve.tensor_scalar(pick0[:, t, :], pick1[:, t, :], mv[:, t, 0:1], rstd[:, t:t + 1], ALU.subtract,
                                      ALU.mult).then_inc(s.fin_norm, 1)

        @block.tensor
        def _(pe):
            mm = pe.matmul
            pe.wait_ge(s.consts, 1)
            pe.wait_ge(s.raw_in, 32)
            for k in range(4):
                for i in range(2):
                    for c in range(2):
                        last = pe.transpose(bview(4 + k, 4, 128)[:, 2 * i + c, :], raw_w[:, 2 * k + i, 128 * c:128 * c + 128], ident)
                last.then_inc(s.wT_mm, 1)

            def transpose_rows(g, j):
                t = g * G + j
                if at(g, (0, 1)):
                    pe.wait_ge(s.xn_ready, t + 1)
                else:
                    pe.wait_ge(s.xn_row_ok, t + 1 - 2 * G)
                if not (at(g, (0,)) and j < 2):
                    pe.wait_ge(s.xnT_ready, t - 1 if j >= 2 else g * G)
                for k in range(2):
                    last = pe.transpose(bview(j % 2, 2, P)[:, k, :],
                                        xn_rows[:, j, 128 * k:128 * k + 128], ident[0:P, 0:P])
                last.then_inc(s.xnT_mm, 1)

            def front(g):
                transpose_rows(g, 0)
                for j in range(G):
                    t = g * G + j
                    pe.wait_ge(s.xnT_ready, t + 1)
                    if not (at(g, (0,)) and j < 2):
                        pe.wait_ge(s.h_ready, t - 1 if j >= 2 else g * G)
                    for f in range(2):
                        for k in range(2):
                            last = mm(bview(2 + j % 2, 2, P)[:, f, :], w1_sb[:, k, 128 * f:128 * f + 128],
                                      xnT[:, j, k, :], start=k == 0, stop=k == 1)
                    last.then_inc(s.l1_mm, 1)
                    if j < G - 1:
                        transpose_rows(g, j + 1)
                    if not at(t, (0,)):
                        pe.wait_ge(s.qkv_evac, t)
                    for half in range(2):
                        for k in range(2):
                            last = mm(bank[5 + half][0:P, 0:384], xnT[:, j, k, :], wqkvT[:, k, 384 * half:384 * half + 384],
                                      start=k == 0, stop=k == 1)
                    last.then_inc(s.qkv_mm, 1)
                    pe.wait_ge(s.h_ready, t + 1)
                    if not at(t, (0,)):
                        pe.wait_ge(s.m_evac, t)
                    for k in range(2):
                        last = mm(bank[4][0:P, 0:D], hT[:, j, k, :], w2_sb[:, k, :], start=k == 0, stop=k == 1)
                    last.then_inc(s.m_mm, 1)

            pe.wait_ge(s.gnn_in, 32)
            pe.wait_ge(s.act_chain, 4)
            front(0)
            front(1)
            pe.wait_ge(s.cnt_ok, 1)
            mm(bank[7][0:P, 0:NB], tri, cnt, start=True, stop=True)
            mm(bank[7][0:P, 64:64 + NB], ones[0:P, :], cnt, start=True, stop=True)
            mm(bank[7][0:NB, 128:129], cnt, ones[0:P, 0:1], start=True, stop=True).then_inc(s.prefix_mm, 1)
            with pe.Fori(2, T // G) as g:
                front(g)
            pe.wait_ge(s.n_col_ok, 1)
            pe.wait_ge(s.col_hot_ok, 1)
            mm(bank[7][0:NB, 0:1], tri_in, n_col, start=True, stop=True).then_inc(s.ends_mm, 1)
            pe.wait_ge(s.m_evac, T)
            pe.wait_ge(s.qkv_evac, T)

            def columns(i, which):
                for c in which:
                    hot_q, hot_d, hot_l = col_hot[c % 8]
                    pe.wait_ge(s.col_hot_ok, i * 16 + c + 1)
                    group = dict(start=at(i, (0,)) and c == 0, stop=at(i, (T - 1,)) and c == 15)
                    mm(bank[4][:, 0:NQ], hot_d, hot_q, skip_group_check=True, **group)
                    mm(bank[5][:, 0:NQ], hot_l, hot_q, skip_group_check=True, **group).then_inc(s.col_mm, 1)

            def k_tile(t, turn):
                first = at(t, (0,))
                pe.wait_ge(s.k_row_ok, t + 1)
                pe.wait_ge(s.v1_ok, t + 1)
                group = dict(stop=at(t, (T - 1,)), skip_group_check=True)
                values = v1[:, turn, :, :]
                for i in range(2):
                    mm(lin_ps[i], k_row[:, turn, 4 * i:4 * i + 4, :], values[:, 4 * i:4 * i + 4, :], start=first, **group)
                mm(bank[6][0:P, 0:H * HV], ones[0:P, :], values, start=first, **group).then_inc(s.lin_mm, 1)
                for h in range(H):
                    if not at(t, (T - 1,)):
                        columns(t + 1, (2 * h, 2 * h + 1))
                    pe.wait_ge(s.pairs_ok, t * H + h + 1)
                    for c in range(4):
                        last = mm(bank[h // 3][:, (h % 3 * 4 + c) * HV:(h % 3 * 4 + c + 1) * HV], pairs[:, h, 128 * c:128 * c + 128],
                                  values[:, h, :], start=first and h in (0, 3) and c == 0, **group)
                    last.then_inc(s.head_mm, 1)
                    if h == 5:
                        pe.wait_ge(s.k_diag_ok, t + 1)
                        for i in range(2):
                            last = mm(diag_ps[i], k_diag[:, 4 * i:4 * i + 4, :], values[:, 4 * i:4 * i + 4, :], start=False, **group)
                        last.then_inc(s.diag_mm, 1)

            columns(0, range(16))
            sum_tiles(pe, k_tile)
            pe.wait_ge(s.past_ok, 1)
            mm(bank[7][0:1, 0:NQ], ones[0:NB, 0:1], past_end, start=True, stop=True).then_inc(s.bucket_mm, 1)
            k_tile(T - 1, 0)

            def agg_pair(n, turn, q):
                if q == 0:
                    pe.wait_ge(s.hot_src_ok, n + 1)
                if not (at(n, (0,)) and q < 2):
                    pe.wait_ge(s.agg_add, n * GB + 2 * q - 2)
                for k in (2 * q, 2 * q + 1):
                    pe.wait_ge(msgs_in[k], n * 16 + 16)
                    for c in range(2):
                        last = mm(agg_ps[k % 4][:, P * c:P * c + P], msgs[:, k, 128 * c:128 * c + 128], hot_src[:, turn, k, :],
                                  start=True, stop=True, skip_group_check=True)
                    last.then_inc(s.agg_mm, 1)

            for n in range(2):
                for q in range(4):
                    agg_pair(n, n, q)

            def mixT_of(t):
                pe.wait_ge(s.mix_row_ok, t + 1)
                if not at(t, (0,)):
                    pe.wait_ge(s.mixT_ok, t)
                for k in range(2):
                    last = pe.transpose(bview(6, 2, P)[:, k, :], mix_row[:, 4 * k:4 * k + 4, :], ident[0:P, 0:P])
                last.then_inc(s.mixT_mm, 1)

            def project(t):
                pe.wait_ge(s.mixT_ok, t + 1)
                if not at(t, (0,)):
                    pe.wait_ge(s.x_ok, t)
                for k in range(2):
                    last = mm(bank[6][0:P, 256:512], mixT[:, k, :], wprojT[:, k, :], start=k == 0, stop=k == 1)
                last.then_inc(s.proj_mm, 1)

            def qT_of(t):
                pe.wait_ge(s.split_ok, t + 1)
                if not at(t, (0,)):
                    pe.wait_ge(s.qT_ok, t)
                for h in range(H):
                    last = pe.transpose(q_partsT_ps[:, h, 0:P], q_parts[:, h, :, :].rearrange("p a b -> p (a b)"), ident_h[0:P, 0:P])
                last.then_inc(s.q_partsT_mm, 1)
                if not at(t, (0,)):
                    pe.wait_ge(s.q_ld_ok, t)
                for k in range(2):
                    last = pe.transpose(bview(1, 2, P)[:, k, :], q_row[:, 4 * k:4 * k + 4, :], ident[0:P, 0:P])
                last.then_inc(s.qnT_mm, 1)

            def q_tile(t):
                y = bank[7][0:P, 0:H * HV]

                def sums(h):
                    if not (at(t, (0,)) and h < 2):
                        pe.wait_ge(s.q_pairs_ok, t * H + h - 1)
                    for c in range(4):
                        last = mm(bview(2 + h % 2, 4, P)[:, c, :], sel[:, c, :], qT[:, h, 0:P], start=True, stop=True,
                                  skip_group_check=True)
                    last.then_inc(s.sel_mm, 1)

                group = dict(stop=False, skip_group_check=True)
                pe.wait_ge(s.qT_ok, t + 1)
                sums(0)
                sums(1)
                if not at(t, (0,)):
                    mixT_of(t - 1)
                mm(y, row0, v_sum, start=True, **group)
                pe.wait_ge(s.q_ld_ok, t + 1)
                for i in range(2):
                    mm(y[:, 4 * HV * i:4 * HV * (i + 1)], q_lin[:, i, :], kv_lin[:, i, :], start=False, **group)
                    last = mm(y[:, 4 * HV * i:4 * HV * (i + 1)], q_sq[:, i, :], kv_diag[:, i, :], start=False, **group)
                last.then_inc(s.y_ld_mm, 1)
                for h in range(H):
                    pe.wait_ge(s.q_pairs_ok, t * H + h + 1)
                    for c in range(4):
                        last = mm(y[:, HV * h:HV * h + HV], q_pairs[:, h % 4, c, :], kv[:, h, c, :], start=False,
                                  stop=c == 3, skip_group_check=True)
                    last.then_inc(s.y_mm, 1)
                    if h < H - 2:
                        sums(h + 2)
                    if h == 3 and not at(t, (0,)):
                        project(t - 1)
                    if h == 5 and not at(t, (T - 1,)):
                        qT_of(t + 1)
                    agg_pair(t * 2 + 2 + h // 4, h // 4, h % 4)

            pe.wait_ge(s.kv_ok, 1)
            qT_of(0)
            q_tile(0)
            with pe.Fori(1, T - 1) as t:
                q_tile(t)
            q_tile(T - 1)
            mixT_of(T - 1)
            project(T - 1)

            pe.wait_ge(s.gate_in, 48)
            pe.transpose(bank[7][:, 0:NX * 4], b1_rows, ident[0:NX * 4, 0:NX * 4]).then_inc(s.b1_mm, 1)
            pe.wait_ge(s.agg_add, NBATCH * GB)
            pe.wait_ge(s.x_ok, T)

            def second_pass(g):
                def up(j):
                    t = g * G + j
                    pe.wait_ge(s.h2_ok, t - 1 if j >= 2 else g * G)
                    h = node[:, bass.ds(t, 1), :].rearrange("p a c -> p (a c)")
                    for f in range(2):
                        for k in range(2):
                            last = mm(bview(j % 2, 2, P)[:, f, :], w1_sb[:, k, 128 * f:128 * f + 128], h[:, P * k:P * k + P],
                                      start=k == 0, stop=k == 1)
                    last.then_inc(s.f1_mm, 1)

                up(0)
                for j in range(G):
                    if j < G - 1:
                        up(j + 1)
                    t = g * G + j
                    pe.wait_ge(s.h2_ok, t + 1)
                    pe.wait_ge(s.x2_add, t)
                    for k in range(2):
                        last = mm(bank[2][0:P, 0:D], hT2[:, j % 2, k, :], w2_sb[:, k, :], start=k == 0, stop=k == 1)
                    last.then_inc(s.f2_mm, 1)

            def gate(g):
                def rows(j):
                    t = g * G + j
                    pe.wait_ge(s.xn2_ok, t + 1)
                    pe.wait_ge(s.xn2T_ok, t - 1 if j >= 2 else g * G)
                    for k in range(2):
                        last = pe.transpose(bview(3 + j % 2, 2, P)[:, k, :], xn2[:, j, 128 * k:128 * k + 128], ident[0:P, 0:P])
                    last.then_inc(s.xn2T_mm, 1)

                rows(0)
                for j in range(G):
                    if j < G - 1:
                        rows(j + 1)
                    t = g * G + j
                    pe.wait_ge(s.xn2T_ok, t + 1)
                    if j == 0:
                        pe.wait_ge(s.gate_ok, g)
                    for k in range(2):
                        last = mm(bank[5][0:P, NX * j:NX * j + NX], xn2T[:, j % 2, k, :], gate_w_sb[:, k, :], start=k == 0, stop=k == 1)
                    last.then_inc(s.gate_mm, 1)

            second_pass(0)
            with pe.Fori(1, T // G) as g:
                second_pass(g)
                gate(g - 1)
            gate(T // G - 1)
            pe.wait_ge(s.count_ok, 1)
            mm(bank[7][0:P, 64:64 + NX], tri, count_x, start=True, stop=True)
            mm(bank[7][0:P, 128:128 + NX], ones[0:P, :], count_x, start=True, stop=True)
            mm(bank[7][0:NX, 192:193], count_x, ones[0:P, 0:1], start=True, stop=True).then_inc(s.route_mm, 1)
            pe.wait_ge(s.col_x_ok, 1)
            mm(bank[6][0:NX, 0:1], tri_in[0:NX, 0:NX], col_x, start=True, stop=True).then_inc(s.ends_x_mm, 1)
            pe.wait_ge(s.tok_hot_ok, 1)
            for c in range(2 * T):
                last = mm(bank[5][:, 0:2 * NT], hot_rx[:, c, :], val_qx[:, c, :, :].rearrange("p a b -> p (a b)"),
                          start=c == 0, stop=c == 2 * T - 1)
            last.then_inc(s.tok_mm, 1)
            pe.wait_ge(s.past_x_ok, 1)
            mm(bank[6][0:1, 64:64 + NT], ones[0:NX, 0:1], past_x, start=True, stop=True).then_inc(s.expert_mm, 1)

            def tokT_of(i, j):
                n = i * 4 + j
                pe.wait_ge(tok_in[j % 4], (i + j // 4) * 16 + 16)
                if not (isinstance(i, int) and n < 2):
                    pe.wait_ge(s.tokT_ok, n - 1)
                for k in range(2):
                    last = pe.transpose(bview(j % 2, 2, 128)[:, k, :], tok_rows[:, j % 4, 128 * k:128 * k + 128], ident)
                last.then_inc(s.tokT_mm, 1)

            def up_of(i, j, expert):
                n = i * 4 + j
                pe.wait_ge(s.tokT_ok, n + 1)
                if not (isinstance(i, int) and n < 2):
                    pe.wait_ge(s.hid_ok, n - 1)
                w = experts[:, bass.ds(expert, 1), 0:1024].rearrange("p a n -> p (a n)")
                for k in range(2):
                    last = mm(bank[2 + j % 2][:, :], tokT[:, j % 2, k, :], w[:, FF * k:FF * k + FF], start=k == 0, stop=k == 1)
                last.then_inc(s.ffn1_mm, 1)

            def hidT_of(i, j):
                n = i * 4 + j
                pe.wait_ge(s.hid_ok, n + 1)
                if not (isinstance(i, int) and n < 2):
                    pe.wait_ge(s.relu_ok, n - 1)
                for c in range(4):
                    last = pe.transpose(bview(4 + j % 2, 4, 128)[:, c, :], hid[:, j % 2, 128 * c:128 * c + 128], ident)
                last.then_inc(s.hidT_mm, 1)

            def down_of(i, j, expert):
                n = i * 4 + j
                pe.wait_ge(s.relu_ok, n + 1)
                if not (isinstance(i, int) and n < 2):
                    pe.wait_ge(s.y_ok, n - 1)
                w = experts[:, bass.ds(expert, 1), 1024:2048].rearrange("p a n -> p (a n)")
                for c in range(4):
                    last = mm(bank[6 + j % 2][:, 0:D], hidT[:, j % 2, c, :], w[:, D * c:D * c + D], start=c == 0, stop=c == 3)
                last.then_inc(s.ffn2_mm, 1)

            def chosen(at, count):
                return nc.values_load_multi_w_load_instructions(
                    tok_expert[:, bass.ds(at, count)], engines=[mybir.EngineType.PE], min_val=0, max_val=NX - 1,
                    skip_runtime_bounds_check_because="clamped to the last expert when written")[1]

            pe.wait_ge(s.tok_ok, 1)
            pe.wait_ge(s.w_in, 32 * NX)
            tokT_of(0, 0)
            tokT_of(0, 1)
            e = chosen(0, 2)
            up_of(0, 0, e[0])
            up_of(0, 1, e[1])
            hidT_of(0, 0)
            tokT_of(0, 2)

            def four_tiles(i):
                e = chosen(i * 4, 6)
                for j in range(4):
                    up_of(i, j + 2, e[j + 2])
                    hidT_of(i, j + 1)
                    tokT_of(i, j + 3)
                    down_of(i, j, e[j])

            four_tiles(0)
            with pe.Fori(1, (NT - 4) // 4) as i:
                four_tiles(i)
            i = (NT - 4) // 4
            e = chosen(NT - 4, 4)
            for j in range(4):
                if j < 2:
                    up_of(i, j + 2, e[j + 2])
                if j < 3:
                    hidT_of(i, j + 1)
                if j < 1:
                    tokT_of(i, j + 3)
                down_of(i, j, e[j])


INPUTS = ("x src dst L0_gnn_w1 L0_gnn_b1 L0_gnn_w2 L0_gnn_b2 L0_mix_Wqkv L0_mix_bqkv L0_mix_Wproj L0_mix_bproj "
          "L0_mix_temperature L0_ffn_gate_w L0_ffn_gate_b L0_ffn_w1 L0_ffn_b1 L0_ffn_w2 L0_ffn_b2 L0_ffn_gamma "
          "L0_ffn_beta").split()


def kernel(**inputs):
    import concourse.bacc as _bacc
    from concourse.bass_utils import run_bass_kernel_spmd as _run

    nc = _bacc.Bacc("TRN2", target_bir_lowering=False, num_devices=1)
    arrays, args = {}, []
    for name in INPUTS:
        a = np.ascontiguousarray(inputs[name])
        arrays[name] = a
        args.append(nc.dram_tensor(name, a.shape, mybir.dt.from_np(a.dtype), kind="ExternalInput").ap())
    args.append(nc.dram_tensor("out", (N, D), F32, kind="ExternalOutput").ap())
    program(nc, *args)
    return _run(nc, [arrays], core_ids=[0]).results[0]["out"]
```

```python
import numpy as np
import concourse.bass as bass
from concourse import mybir
from contextlib import ExitStack

F32 = mybir.dt.float32
F16 = mybir.dt.float16
BF16 = mybir.dt.bfloat16
I32 = mybir.dt.int32
U32 = mybir.dt.uint32
ALU = mybir.AluOpType
ACT = mybir.ActivationFunctionType
AX = mybir.AxisListType

N, D, E = 3125, 256, 50000
P, T = 125, 25
G = 5
EC = E // P
SLOT = 128
NB = T
NQ = 416
GB = 8
NBATCH = NQ // GB
H, DH = 8, 32
HV = DH + 1
NX, FF = 16, 512
NT = 64
BEHIND = [[], [], [0, 1], [2, 3], [4]]
VECTOR_ADDS = (3, 4)
MAGIC = 12582912.0
MID = 1562
SCALE2 = float(DH) ** 0.5
LN_EPS = 1e-5
assert NQ * SLOT >= E + NB * (SLOT - 1) - SLOT + 1 and NT * SLOT > 2 * N + NX * (SLOT - 1) - SLOT


class Region:

    def __init__(self, tensor, start=0, end=None):
        self.tensor, self.at, self.end = tensor, start, end

    def take(self, shape, dt=F32, parts=128):
        size = int(np.prod(shape))
        words = size if dt in (F32, I32, U32) else (size + 1) // 2
        view = self.tensor[0:parts, self.at:self.at + words]
        self.at += words
        assert self.end is None or self.at <= self.end, (self.at, self.end)
        if dt is not F32:
            view = view.bitcast(dt)
        if len(shape) == 2:
            view = view.rearrange("p (a b) -> p a b", a=shape[0])
        if len(shape) == 3:
            view = view.rearrange("p (a b c) -> p a b c", a=shape[0], b=shape[1])
        return view


class Chain:

    def __init__(self, eng, sem):
        self.eng, self.sem, self.base, self.n = eng, sem, 0, 0

    def add(self, ins):
        ins.then_inc(self.sem, 1)
        self.n += 1

    def wait(self):
        self.eng.wait_ge(self.sem, self.base + self.n)

    def enter(self, i, first, per):
        self.start, self.per = self.base + self.n, per
        self.base, self.n = self.start + (i - first) * per, 0

    def leave(self, rounds):
        assert self.n == self.per, (self.n, self.per)
        self.base, self.n = self.start + rounds * self.per, 0


class Semaphores:

    def __init__(self, sem):
        self.x_in = sem("x_in")
        self.edges_in = sem("edges_in")
        self.gnn_in = sem("gnn_in")
        self.raw_in = sem("raw_in")
        self.bias_in = sem("bias_in")
        self.gate_in = sem("gate_in")
        self.b1_in = sem("b1_in")
        self.w_in = sem("w_in")
        self.late_in = sem("late_in")
        self.consts = sem("consts")
        self.preps = sem("preps")
        self.wT_mm = sem("wT_mm")
        self.dve_chain = sem("dve_chain")
        self.pool_chain = sem("pool_chain")
        self.act_chain = sem("act_chain")
        self.apart = sem("apart")
        self.ln_stats = sem("ln_stats")
        self.rstd_sd = sem("rstd_sd")
        self.xn_ready = sem("xn_ready")
        self.xnT_mm = sem("xnT_mm")
        self.xnT_ready = sem("xnT_ready")
        self.l1_mm = sem("l1_mm")
        self.h_ready = sem("h_ready")
        self.m_mm = sem("m_mm")
        self.m_evac = sem("m_evac")
        self.m_biased = sem("m_biased")
        self.qkv_mm = sem("qkv_mm")
        self.qkv_evac = sem("qkv_evac")
        self.qkv_biased = sem("qkv_biased")
        self.xn_row_ok = sem("xn_row_ok")
        self.sq_ok = sem("sq_ok")
        self.norm_part = sem("norm_part")
        self.norm_root = sem("norm_root")
        self.norm_ok = sem("norm_ok")
        self.cnt_ok = sem("cnt_ok")
        self.prefix_mm = sem("prefix_mm")
        self.n_col_ok = sem("n_col_ok")
        self.ends_mm = sem("ends_mm")
        self.past_ok = sem("past_ok")
        self.bucket_mm = sem("bucket_mm")
        self.col_hot_ok = sem("col_hot_ok")
        self.col_mm = sem("col_mm")
        self.sorted_ok = sem("sorted_ok")
        self.msg_idx_ok = sem("msg_idx_ok")
        self.hot_src_ok = sem("hot_src_ok")
        self.agg_mm = sem("agg_mm")
        self.agg_add = sem("agg_add")
        self.v1_ones = sem("v1_ones")
        self.v_acc_ok = sem("v_acc_ok")
        self.part_rows_ok = sem("part_rows_ok")
        self.kd_ok = sem("kd_ok")
        self.k_row_ok = sem("k_row_ok")
        self.v1_ok = sem("v1_ok")
        self.lin_mm = sem("lin_mm")
        self.k_diag_ok = sem("k_diag_ok")
        self.diag_mm = sem("diag_mm")
        self.pairs_ok = sem("pairs_ok")
        self.head_mm = sem("head_mm")
        self.v_sum_mm = sem("v_sum_mm")
        self.kv_ok = sem("kv_ok")
        self.split_ok = sem("split_ok")
        self.q_partsT_mm = sem("q_partsT_mm")
        self.qT_ok = sem("qT_ok")
        self.qnT_mm = sem("qnT_mm")
        self.q_ld_ok = sem("q_ld_ok")
        self.sel_mm = sem("sel_mm")
        self.q_pairs_ok = sem("q_pairs_ok")
        self.y_mm = sem("y_mm")
        self.y_ld_mm = sem("y_ld_mm")
        self.mix_row_ok = sem("mix_row_ok")
        self.mixT_mm = sem("mixT_mm")
        self.mixT_ok = sem("mixT_ok")
        self.proj_mm = sem("proj_mm")
        self.x_ok = sem("x_ok")
        self.b1_mm = sem("b1_mm")
        self.b1_ok = sem("b1_ok")
        self.f1_mm = sem("f1_mm")
        self.h2_ok = sem("h2_ok")
        self.f2_mm = sem("f2_mm")
        self.x2_add = sem("x2_add")
        self.ln2_stats = sem("ln2_stats")
        self.ln2_root = sem("ln2_root")
        self.xn2_ok = sem("xn2_ok")
        self.xn2T_mm = sem("xn2T_mm")
        self.xn2T_ok = sem("xn2T_ok")
        self.gate_mm = sem("gate_mm")
        self.gate_ok = sem("gate_ok")
        self.gap_ok = sem("gap_ok")
        self.exp_ok = sem("exp_ok")
        self.trash_ok = sem("trash_ok")
        self.count_ok = sem("count_ok")
        self.route_mm = sem("route_mm")
        self.col_x_ok = sem("col_x_ok")
        self.ends_x_mm = sem("ends_x_mm")
        self.past_x_ok = sem("past_x_ok")
        self.expert_mm = sem("expert_mm")
        self.hot_qx_ok = sem("hot_qx_ok")
        self.tok_pick_ok = sem("tok_pick_ok")
        self.tok_hot_ok = sem("tok_hot_ok")
        self.tok_mm = sem("tok_mm")
        self.tok_ok = sem("tok_ok")
        self.tokT_mm = sem("tokT_mm")
        self.tokT_ok = sem("tokT_ok")
        self.ffn1_mm = sem("ffn1_mm")
        self.w1_ok = sem("w1_ok")
        self.relu_ok = sem("relu_ok")
        self.ffn2_mm = sem("ffn2_mm")
        self.y_ok = sem("y_ok")
        self.beta_ok = sem("beta_ok")
        self.fin_stats = sem("fin_stats")
        self.fin_root = sem("fin_root")
        self.fin_norm = sem("fin_norm")
        self.fin_gamma = sem("fin_gamma")
        self.fin_shift = sem("fin_shift")
        self.fin_ok = sem("fin_ok")
        self.fin_ok_too = sem("fin_ok_too")
        self.stored = sem("stored")


def windows(ap, shifts, step):
    dims = list(ap.ap)
    return bass.AP(ap.tensor, ap.offset, [dims[0], [step, shifts], *dims[1:]])


def program(nc, x, src, dst, gnn_w1, gnn_b1, gnn_w2, gnn_b2, Wqkv, bqkv, Wproj, bproj, temperature,
            gate_w, gate_b, ffn_w1, ffn_b1, ffn_w2, ffn_b2, gamma, beta, out):
    ctx = ExitStack()
    with ctx:
        def sb(name, words):
            return ctx.enter_context(nc.sbuf_tensor(name, [128, words], F32))

        def sem(name):
            return ctx.enter_context(nc.semaphore(name))

        x_buf = sb("x_buf", T * D)
        node_buf = sb("node_buf", T * D)
        big = sb("big", NX * 2048)
        mid = sb("mid", 4352)
        const = Region(sb("const", 3288), 0, 3288)

        x_sb = x_buf[0:P, :].rearrange("p (t c) -> p t c", t=T)
        node = node_buf[:, :].rearrange("p (t c) -> p t c", t=T)

        xn_rows = node[0:P, T - G:T, :]

        ident = const.take([128])
        ident_h = const.take([128], BF16)
        iota_q = const.take([NQ], F16)
        iota_r = const.take([128], F16)
        iota_loc = const.take([P])
        iota_x = const.take([NX])
        tri = const.take([P], parts=P)
        tri_in = const.take([NB], parts=NB)
        ones = const.take([P])
        head_mask = const.take([4])
        pair_w = const.take([4])
        sel = const.take([4, 128], BF16, parts=96)
        trash_pad = const.take([1])
        edges_at = const.at
        edge_idx = const.take([NQ], I32)
        edge_loc = const.take([NQ])
        edge_bucket = const.take([NQ], I32, parts=1)
        stats = const.take([T, 6], parts=P)
        mv = const.take([T, 2], parts=P)
        rstd = const.take([T], parts=P)
        eps_t = const.take([1], parts=P)
        temp_t = const.take([H], parts=P)
        gnn_b1T = const.take([2])
        gate_w_sb = const.take([2, NX])
        gate_b_bc = const.take([NX], parts=P)
        tok_val = const.take([T, 2], parts=P)
        tok_pick = const.take([T, 2], parts=P)
        logits = const.take([G, NX], parts=P)
        top_val = const.take([G, 8], parts=P)
        top_idx = const.take([G, 8], U32, parts=P)
        b1T = const.take([NX * 4])
        score = const.take([T, 2], parts=P)
        choice = const.take([T, 2], parts=P)
        weight = const.take([T, 2], parts=P)

        c = Region(const.tensor, edges_at, edges_at + 3 * NQ)
        tok_gather = c.take([NT], I32)
        tok_scatter = c.take([NT], I32)
        tok_expert = c.take([NT], I32, parts=1)
        last_slot = c.take([NX], parts=P)
        count_x = c.take([NX], parts=P)
        tiles_x = c.take([NX], parts=P)
        incl_x = c.take([NX], parts=P)
        off_x = c.take([NX], parts=P)
        col_x = c.take([1], parts=NX)
        ends_x = c.take([1], parts=NX)
        past_x = c.take([NT], parts=NX)
        pos_x = c.take([2 * T], parts=P)
        slot_qx = c.take([2 * T], parts=P)
        slot_rx = c.take([2 * T], parts=P)
        unused = c.take([NT])
        out_row = c.take([NT])
        trash = c.take([NT // 2, 2])
        hT2 = c.take([2, 2, P])
        fin_shift = c.take([T], parts=P)

        m = Region(mid, 0, 4352)
        w1_sb = m.take([2, D])
        w2_sb = m.take([2, D])
        wqkvT = m.take([2, 3 * D])
        wprojT = m.take([2, D])
        bqkv_bc = m.take([3 * D], parts=P)
        b2_bc = m.take([D], parts=P)
        bsum_bc = m.take([D], parts=P)

        m = Region(mid, 4 * D, 4352)
        xn2 = m.take([2, G, D], parts=P)
        xn2T = m.take([2, 2, P])
        b1_rows = m.take([128], parts=NX * 4)
        m = Region(mid, 0, 4352)
        hot_x = m.take([NX, 2 * T], parts=P)
        run_x = m.take([NX, 2 * T], parts=P)
        hot_qx = m.take([2 * T, NT], F16, parts=P)
        m = Region(node_buf, 0, T * D)
        hot_rx = m.take([2 * T, 128], F16, parts=P)
        val_qx = m.take([2 * T, 2, NT], F16, parts=P)
        m = Region(mid, 0, 4352)
        tok_rows = m.take([4, D])
        tokT = m.take([2, 2, 128])
        w1_turn = [m.take([2 * FF])]
        hidT = m.take([2, 4, 128])
        y_rows = m.take([2, D])
        m = Region(node_buf, 0, T * D)
        b2_x = m.take([NX, D])
        gamma_bc = m.take([D], parts=P)
        beta_bc = m.take([D], parts=P)
        w1_turn.append(m.take([2 * FF]))
        experts = big[:, :].rearrange("p (e n) -> p e n", e=NX)
        m = Region(big, 0, NX * 2048)
        pick0 = m.take([T, D], parts=P)
        pick1 = m.take([T, D], parts=P)
        own = m.take([T, D], parts=P)

        b = Region(big, 0, NX * 2048)
        qkv = b.take([T, 3 * D], parts=P)
        phase = b.at
        src_i = b.take([EC], I32, parts=P)
        dst_i = b.take([EC], I32, parts=P)
        loc_f = b.take([EC], parts=P)
        bkt_h = b.take([EC], F16, parts=P)
        pos = b.take([EC], parts=P)
        slot_q = b.take([EC], parts=P)
        slot_r = b.take([EC], parts=P)
        val_dst = b.take([EC], parts=P)
        val_loc = b.take([EC], parts=P)
        cnt = b.take([NB], parts=P)
        n_tiles = b.take([NB], parts=P)
        incl = b.take([NB], parts=P)
        off = b.take([NB], parts=P)
        n_col = b.take([1], parts=NB)
        ends = b.take([1], parts=NB)
        shift = b.take([T], parts=P)
        past_end = big[0:NB, phase:phase + NQ]
        sorting = b.at
        wave_hot = b.take([G, EC], F16, parts=P)
        wave_at = b.at
        wave_pos = b.take([G, EC], parts=P)
        after = b.at
        b.at = sorting
        col_hot = [(b.take([NQ], F16, parts=P), b.take([128], F16, parts=P), b.take([128], F16, parts=P))
                   for _ in range(8)]
        assert b.at + D <= after
        b.at = after - D
        v_acc = b.take([D], parts=P)
        sort_end = b.at
        norm = b.take([T, 2 * H], parts=P)
        features = b.at
        xnT = b.take([G, 2, P])
        hT = b.take([G, 2, P])
        m_rows = b.take([G, D], parts=P)
        raw_w = b.take([8, D])
        wave_pos_flat = big[0:96, wave_at:wave_at + 512]
        bproj_bc = b.take([D], parts=P)
        sq = raw_w.rearrange("p a b -> p (a b)")[0:P, 0:512]

        b = Region(big, phase, sort_end)
        msgs = [big[:, (D * 3) * (k // 2) + D + D * (k % 2):(D * 3) * (k // 2) + 2 * D + D * (k % 2)] for k in range(2 * GB)]
        hot_src = b.take([2, GB, P])
        kv = b.take([H, 4, HV])
        kv_lin = b.take([2, 4 * HV])
        kv_diag = b.take([2, 4 * HV])
        v_sum = b.take([H * HV], parts=96)
        v_parts = b.take([H * HV], BF16, parts=96)
        part_rows = b.take([128], BF16, parts=96)
        idx_ring = b.take([2, 2 * GB], I32)
        b = Region(big, features, NX * 2048)
        pairs = b.take([H, 512], parts=P)
        kd = b.take([2, H, 48], parts=P)
        k_row = b.take([2, H, DH], parts=P)
        v1 = b.take([2, H, HV], parts=P)
        k_diag = b.take([H, DH], parts=P)
        k_tmp = b.take([H, DH], parts=P)
        k_sum = b.take([H], parts=P)
        b.at = features
        q_pairs = b.take([4, 4, P])
        q_row = b.take([H, DH], parts=P)
        q_rest = b.take([H, DH], parts=P)
        q_parts = b.take([H, 3, DH], BF16, parts=P)
        qT = b.take([H, 128], BF16, parts=96)
        q_lin = b.take([2, P])
        q_sq = b.take([2, P])
        y_rcp = b.take([H], parts=P)
        mix_row = b.take([H, DH], parts=P)
        mixT = b.take([2, P])

        bank = [ctx.enter_context(nc.psum_tensor(f"bank{i}", [128, 512], F32)) for i in range(8)]

        def bview(i, a, c, parts=128, at=0):
            return bank[i][0:parts, at:at + a * c].rearrange("p (a c) -> p a c", a=a)

        lin_ps = [bank[2][:, 264:264 + 4 * HV], bank[3][:, 264:264 + 4 * HV]]
        diag_ps = [bank[3][:, 0:4 * HV], bank[3][:, 4 * HV:8 * HV]]
        agg_ps = [bank[4 + k // 2][:, 256 * (k % 2):256 * (k % 2) + 2 * P] for k in range(4)]
        q_partsT_ps = bank[0][0:96, :].bitcast(BF16).rearrange("p (h n) -> p h n", h=H)

        msg_rows = nc.dram_tensor("msg_rows", (N, D), F32).ap()
        xn2_rows = nc.dram_tensor("xn2_rows", (N, D), F32).ap()
        moe_rows = nc.dram_tensor("moe_rows", (2 * N + 2 * SLOT, D), F32).ap()
        tiled = lambda rows: rows.rearrange("(p t) c -> p t c", t=T)

        s = Semaphores(sem)
        m_out = [sem(f"m_out{j}") for j in range(G)]
        msgs_in = [sem(f"msgs_in{k}") for k in range(2 * GB)]
        tok_in = [sem(f"tok_in{k}") for k in range(4)]
        xn2_out = [sem(f"xn2_out{k}") for k in range(2)]
        y_out = [sem(f"y_out{k}") for k in range(2)]
        fin_in = [sem(f"fin_in{g}") for g in range(T // G)]

        block = ctx.enter_context(nc.Block())

        def sum_tiles(eng, tile):
            tile(0, 0)
            with eng.Fori(0, (T - 5) // 2) as i:
                tile(i * 2 + 1, 1)
                tile(i * 2 + 2, 0)
            tile(T - 4, 1)
            tile(T - 3, 0)

        def group_turns(eng, group):
            group(0, 0)
            with eng.Fori(0, (T // G - 1) // 2) as i:
                group(i * 2 + 1, 1)
                group(i * 2 + 2, 0)

        def at(t, tiles):
            return isinstance(t, int) and t in tiles

        def apart(eng):
            eng.sem_inc(s.apart, 1)

        SMALL = [(bqkv_bc, bqkv.partition_broadcast(P)), (b2_bc, gnn_b2.partition_broadcast(P)),
                 (bsum_bc, gnn_b2.partition_broadcast(P)), (bproj_bc, bproj.partition_broadcast(P)),
                 (temp_t, temperature.rearrange("a h b c -> (a h b c)").partition_broadcast(P)),
                 *[(gnn_b1T[:, k:k + 1], gnn_b1[128 * k:128 * k + 128].rearrange("(p o) -> p o", o=1)) for k in range(2)]]

        @block.sync
        def _(sp):
            xt = tiled(x)
            def load_x(g):
                for lo, hi in ((0, 112), (112, P)):
                    sp.dma_start(x_sb[lo:hi, G * g:G * g + G, :], xt[lo:hi, G * g:G * g + G, :]).then_inc(s.x_in, 16)
            load_x(0)
            sp.dma_start(src_i, src.rearrange("(p e) -> p e", e=EC)).then_inc(s.edges_in, 16)
            sp.dma_start(dst_i, dst.rearrange("(p e) -> p e", e=EC)).then_inc(s.edges_in, 16)
            sp.dma_start(w1_sb, gnn_w1.rearrange("(k p) f -> p k f", p=128)).then_inc(s.gnn_in, 16)
            sp.dma_start(w2_sb, gnn_w2.rearrange("(k p) f -> p k f", p=128)).then_inc(s.gnn_in, 16)
            for g in range(1, T // G):
                sp.wait_ge(s.x_in, 32 * g)
                load_x(g)
                if g == 1:
                    sp.dma_start(raw_w[:, 0:6, :], Wqkv.rearrange("(k p) c -> p k c", p=128)).then_inc(s.raw_in, 16)
                    sp.dma_start(raw_w[:, 6:8, :], Wproj.rearrange("(k p) c -> p k c", p=128)).then_inc(s.raw_in, 16)
                    for view, dram in SMALL:
                        sp.dma_start(view, dram).then_inc(s.bias_in, 16)
            with sp.Fori(0, T // G) as g:
                for j in range(G):
                    sp.wait_ge(s.m_biased, g * G + j + 1)
                    sp.dma_start(tiled(msg_rows)[:, bass.ds(g * G + j, 1), :].rearrange("p a c -> p (a c)"),
                                 m_rows[:, j, :]).then_inc(m_out[j], 16)
            sp.dma_start(gate_w_sb, gate_w.rearrange("(k p) e -> p k e", p=128)).then_inc(s.gate_in, 16)
            sp.dma_start(gate_b_bc, gate_b.partition_broadcast(P)).then_inc(s.gate_in, 16)
            def load_expert(e):
                sp.dma_start(experts[:, e, 0:1024].rearrange("p (k f) -> p k f", k=2),
                             ffn_w1[e].rearrange("(k p) f -> p k f", p=128)).then_inc(s.w_in, 16)
                sp.dma_start(experts[:, e, 1024:2048].rearrange("p (c h) -> p c h", c=4),
                             ffn_w2[e].rearrange("(c p) h -> p c h", p=128)).then_inc(s.w_in, 16)

            early = range(-(-GB * 3 * D // 2048), phase // 2048)
            for e in early:
                sp.wait_ge(s.split_ok, (2048 * (e + 1) - 1) // (3 * D) + 1)
                load_expert(e)
            sp.wait_ge(s.x_ok, T)
            sp.dma_start(b1_rows, ffn_b1.rearrange("e (c p) -> (e c) p", p=128)).then_inc(s.b1_in, 16)
            sp.wait_ge(s.agg_add, NBATCH * GB)
            for i, e in enumerate([e for e in range(NX) if e not in early]):
                if i:
                    sp.wait_ge(s.x2_add, 2 * i)
                load_expert(e)
            sp.wait_ge(s.tok_mm, 1)
            sp.dma_start(b2_x, ffn_b2.partition_broadcast(128)).then_inc(s.late_in, 16)
            sp.dma_start(gamma_bc, gamma.partition_broadcast(P)).then_inc(s.late_in, 16)
            sp.dma_start(beta_bc, beta.partition_broadcast(P)).then_inc(s.late_in, 16)
            for k in range(2):
                sp.wait_ge(y_out[k], 16 * (NT // 2))
            for g in range(T // G):
                rows = slice(G * g, G * g + G)
                for view, dram in ((pick0, moe_rows[0:N]), (pick1, moe_rows[N:2 * N]), (own, xn2_rows)):
                    for lo, hi in ((0, 112), (112, P)):
                        sp.dma_start(view[lo:hi, rows, :], tiled(dram)[lo:hi, rows, :]).then_inc(fin_in[g], 16)
            for g in range(T // G):
                rows = slice(G * g, G * g + G)
                sp.wait_ge(s.fin_ok, (G - len(VECTOR_ADDS)) * (g + 1))
                sp.wait_ge(s.fin_ok_too, len(VECTOR_ADDS) * (g + 1))
                for lo, hi in ((0, 112), (112, P)):
                    sp.dma_start(tiled(out)[lo:hi, rows, :], pick0[lo:hi, rows, :]).then_inc(s.stored, 16)
            sp.wait_ge(s.stored, 32 * (T // G))

        @block.gpsimd
        def _(pool):
            chain = Chain(pool, s.pool_chain)
            def zero(ap):
                chain.add(pool.memset(ap, 0.0))
            zero(ident)
            zero(tri)
            zero(tri_in)
            zero(head_mask)
            pool.memset(ones, 1.0)
            pool.memset(eps_t, LN_EPS)
            chain.add(pool.memset(pair_w, 0.5 / N))
            pool.iota(iota_q, [[1, NQ]], base=0, channel_multiplier=0, allow_small_or_imprecise_dtypes=True)
            pool.iota(iota_r, [[1, 128]], base=0, channel_multiplier=0, allow_small_or_imprecise_dtypes=True)
            pool.iota(iota_loc, [[1, P]], base=1, channel_multiplier=0, allow_small_or_imprecise_dtypes=True)
            pool.iota(iota_x, [[1, NX]], base=0, channel_multiplier=0, allow_small_or_imprecise_dtypes=True)
            pool.iota(tok_val, [[1, T], [0, 2]], base=-MID, channel_multiplier=T, allow_small_or_imprecise_dtypes=True)
            pool.iota(tok_pick, [[0, T], [1, 2]], base=1, channel_multiplier=0, allow_small_or_imprecise_dtypes=True)
            chain.wait()
            pool.affine_select(out=ident, in_=ident, compare_op=ALU.not_equal, fill=1.0, base=0,
                               pattern=[[-1, 128]], channel_multiplier=1)
            pool.affine_select(out=tri, in_=tri, compare_op=ALU.is_ge, fill=1.0, base=0,
                               pattern=[[-1, P]], channel_multiplier=1)
            pool.affine_select(out=tri_in, in_=tri_in, compare_op=ALU.is_gt, fill=1.0, base=0,
                               pattern=[[-1, NB]], channel_multiplier=1)
            def alone(ins):
                chain.add(ins)
                chain.wait()

            alone(pool.memset(trash_pad, 0.0))
            for h in range(4):
                alone(pool.memset(head_mask[32 * h:32 * h + 32, h:h + 1], 1.0))
            alone(pool.memset(pair_w[96:128, 3:4], 0.25 / N))
            pool.tensor_copy(ident_h, ident).then_inc(s.consts, 1)
            selw = wave_pos_flat
            chain.add(pool.memset(selw, 0.0))
            chain.wait()
            for base, step in ((0, 0), (-1, -1), (31, -1)):
                for k in range(3):
                    v = selw[32 * k:32 * k + 32, :].rearrange("p (d i) -> p d i", i=32)
                    alone(pool.affine_select(out=v, in_=v, compare_op=ALU.not_equal, fill=1.0, base=base,
                                             pattern=[[step, 16], [-1, 32]], channel_multiplier=1))
            pool.tensor_copy(sel.rearrange("p a b -> p (a b)"), selw).then_inc(s.preps, 1)
            pool.wait_ge(s.bias_in, 16 * len(SMALL))
            pool.tensor_tensor(bsum_bc, bsum_bc, bproj_bc, ALU.add).then_inc(s.preps, 1)
            pool.tensor_scalar(temp_t, temp_t, SCALE2, None, ALU.mult).then_inc(s.preps, 1)
            def halve(t):
                part = sq.rearrange("p (h d) -> p h d", h=2 * H)
                pool.wait_ge(s.sq_ok, t + 1)
                for w in (16, 8, 4, 2):
                    chain.add(pool.tensor_tensor(part[:, :, 0:w], part[:, :, 0:w], part[:, :, w:2 * w], ALU.add))
                    chain.wait()
                pool.tensor_tensor(norm[:, bass.ds(t, 1), :].rearrange("p a h -> p (a h)").unsqueeze(2),
                                   part[:, :, 0:1], part[:, :, 1:2], ALU.add).then_inc(s.norm_part, 1)

            def front(g):
                for j in range(G):
                    t = g * G + j
                    pool.wait_ge(s.qkv_evac, t + 1)
                    row = qkv[:, bass.ds(t, 1), :].rearrange("p a c -> p (a c)")
                    pool.tensor_tensor(row, row, bqkv_bc, ALU.add).then_inc(s.qkv_biased, 1)
                    pool.wait_ge(s.m_evac, t + 1)
                    pool.tensor_tensor(m_rows[:, j, :], m_rows[:, j, :], b2_bc, ALU.add).then_inc(s.m_biased, 1)
                    if not at(t, (0,)):
                        halve(t - 1)

            front(0)
            with pool.Fori(1, T // G) as g:
                chain.enter(g, 1, 4 * G)
                front(g)
            chain.leave(T // G - 1)
            halve(T - 1)
            for j in range(G):
                pool.wait_ge(m_out[j], 16 * (T // G))
            chain.add(pool.memset(v1[:, :, :, 0:1], 1.0))
            chain.wait()
            pool.memset(trash_pad, 0.0).then_inc(s.v1_ones, 1)
            pool.wait_ge(s.preps, 3)
            pool.wait_ge(s.norm_ok, 1)

            def k_features(t, turn):
                k = kd[:, turn, :, :]
                if not at(t, (0, 1)):
                    pool.wait_ge(s.k_diag_ok, t - 1)
                    pool.wait_ge(s.k_row_ok, t - 1)
                heads = qkv[:, bass.ds(t, 1), D:2 * D].rearrange("p a (h d) -> p (a h) d", h=H)
                by = norm[:, bass.ds(t, 1), H:2 * H].rearrange("p a h -> p (a h)").unsqueeze(2)
                pool.tensor_tensor(k[:, :, 0:DH], heads, by.broadcast_to([P, H, DH]), ALU.mult)
                pool.tensor_tensor(k[:, :, DH:48], heads[:, :, 0:16], by.broadcast_to([P, H, 16]), ALU.mult).then_inc(s.kd_ok, 1)
                rows = x_sb[:, bass.ds(t, 1), :].rearrange("p a c -> p (a c)")
                pool.tensor_tensor(rows, rows, bsum_bc, ALU.add)
                values = qkv[:, bass.ds(t, 1), 2 * D:3 * D].rearrange("p a c -> p (a c)")
                if at(t, (0,)):
                    pool.tensor_copy(v_acc, values).then_inc(s.v_acc_ok, 1)
                else:
                    pool.wait_ge(s.v_acc_ok, t)
                    pool.tensor_tensor(v_acc, v_acc, values, ALU.add).then_inc(s.v_acc_ok, 1)
                pool.wait_ge(s.kd_ok, t + 1)
                for h in range(H):
                    if not at(t, (0,)):
                        pool.wait_ge(s.head_mm, t * H + h - (H - 1))
                    pool.tensor_tensor(pairs[:, h, :].rearrange("p (d i) -> p d i", i=DH),
                                       k[:, h, 0:DH].unsqueeze(1).broadcast_to([P, 16, DH]),
                                       windows(k[:, h, 1:DH + 1], 16, 1), ALU.mult).then_inc(s.pairs_ok, 1)

            sum_tiles(pool, k_features)
            k_features(T - 2, 1)
            k_features(T - 1, 0)
            pool.wait_ge(s.sorted_ok, 1)
            alone(pool.memset(part_rows, 0.0))
            alone(pool.memset(part_rows[0:1, :], 1.0))
            alone(pool.memset(part_rows[32:33, :], 1.0))
            pool.memset(part_rows[64:65, :], 1.0).then_inc(s.part_rows_ok, 1)
            pool.wait_ge(s.part_rows_ok, 1)

            def gather(n, half):
                pool.tensor_copy(idx_ring[:, half, :], edge_idx[:, bass.ds(n * 2 * GB, 2 * GB)]).then_inc(s.msg_idx_ok, 1)
                pool.wait_ge(s.msg_idx_ok, n + 1)
                for k in range(2 * GB):
                    if not at(n, (0,)):
                        pool.wait_ge(s.agg_mm, n * 2 * GB + k - (2 * GB - 1))
                        apart(pool)
                    pool.indirect_dma_start(msgs[k], None, msg_rows,
                                            bass.IndirectOffsetOnAxis(idx_ring[:, half, k:k + 1], 0)).then_inc(msgs_in[k], 16)

            gather(0, 0)
            gather(1, 1)
            with pool.Fori(1, NBATCH // 4) as i:
                gather(i * 2, 0)
                gather(i * 2 + 1, 1)
            pool.wait_ge(s.agg_add, NBATCH * GB)
            pool.iota(trash, [[0, NT // 2], [SLOT, 2]], base=3 * N - MID, channel_multiplier=1,
                      allow_small_or_imprecise_dtypes=True).then_inc(s.trash_ok, 1)
            def rows_out(g, turn):
                pool.wait_ge(s.xn2_ok, g * G + G)
                pool.dma_start(tiled(xn2_rows)[:, bass.ds(g * G, G), :], xn2[:, turn, :, :]).then_inc(xn2_out[turn], 16)

            group_turns(pool, rows_out)
            pool.wait_ge(s.hot_qx_ok, 1)
            pool.tensor_tensor(val_qx[:, :, 1, :], hot_qx, tok_pick.rearrange("p t k -> p (t k)").unsqueeze(2).broadcast_to([P, 2 * T, NT]),
                               ALU.mult).then_inc(s.tok_pick_ok, 1)
            pool.wait_ge(xn2_out[0], 16 * 3)
            pool.wait_ge(xn2_out[1], 16 * 2)
            pool.wait_ge(s.tok_ok, 1)
            pool.wait_ge(s.tok_mm, 1)

            def gather_tokens(n):
                if n >= 4:
                    pool.wait_ge(s.tokT_mm, n - 3)
                pool.indirect_dma_start(tok_rows[:, n % 4, :], None, xn2_rows,
                                        bass.IndirectOffsetOnAxis(tok_gather[:, n:n + 1], 0)).then_inc(tok_in[n % 4], 16)

            for n in range(4):
                gather_tokens(n)
            for n in range(NT):
                if n + 4 < NT:
                    gather_tokens(n + 4)
                pool.wait_ge(s.y_ok, n + 1)
                pool.indirect_dma_start(moe_rows, bass.IndirectOffsetOnAxis(tok_scatter[:, n:n + 1], 0),
                                        y_rows[:, n % 2, :], None).then_inc(y_out[n % 2], 16)
                if n == 8:
                    pool.wait_ge(s.late_in, 48)
                if 8 <= n < 8 + T:
                    pool.tensor_tensor(x_sb[:, n - 8, :], x_sb[:, n - 8, :], beta_bc, ALU.add).then_inc(s.beta_ok, 1)
            pool.wait_ge(s.beta_ok, T)
            for t in range(T):
                pool.wait_ge(s.fin_norm, t + 1)
                pool.tensor_tensor(pick0[:, t, :], pick0[:, t, :], gamma_bc, ALU.mult).then_inc(s.fin_gamma, 1)
                if t % G not in VECTOR_ADDS:
                    pool.wait_ge(s.fin_gamma, t + 1)
                    pool.tensor_tensor(pick0[:, t, :], pick0[:, t, :], x_sb[:, t, :], ALU.add).then_inc(s.fin_ok, 1)

        @block.scalar
        def _(act):
            act.wait_ge(s.consts, 1)
            def root(lo, hi, n):
                act.wait_ge(s.ln_stats, n)
                act.activation(rstd[:, lo:hi], mv[:, lo:hi, 1], ACT.Sqrt, bias=eps_t).then_inc(s.rstd_sd, 1)

            root(0, G, 1)
            def evac_xnT(g, j):
                t = g * G + j
                act.wait_ge(s.xnT_mm, t + 1)
                act.activation(xnT[:, j, :, :], bview(j % 2, 2, P), ACT.Copy)
                act.activation(node[:, bass.ds(t, 1), :].rearrange("p a c -> p (a c)")[:, 0:2 * P],
                               bank[j % 2][:, 0:2 * P], ACT.Copy).then_inc(s.xnT_ready, 1)

            def squares(t):
                act.wait_ge(s.qkv_biased, t + 1)
                if not at(t, (0,)):
                    act.wait_ge(s.norm_part, t)
                apart(act)
                act.activation(sq, qkv[:, bass.ds(t, 1), 0:2 * D].rearrange("p a c -> p (a c)"), ACT.Square).then_inc(s.sq_ok, 1)

            def front(g, rows_follow):
                for j in range(G):
                    t = g * G + j
                    act.wait_ge(s.l1_mm, t + 1)
                    for k in range(2):
                        last = act.activation(hT[:, j, k, :], bview(2 + j % 2, 2, P)[:, k, :], ACT.Relu, bias=gnn_b1T[:, k:k + 1])
                    last.then_inc(s.h_ready, 1)
                    if rows_follow:
                        act.activation(xn_rows[:, j, :], x_sb[:, bass.ds(t + G, 1), :].rearrange("p a c -> p (a c)"), ACT.Identity,
                                       scale=rstd[:, bass.ds(t + G, 1)], bias=shift[:, bass.ds(t + G, 1)]).then_inc(s.xn_row_ok, 1)
                    if j < G - 1:
                        evac_xnT(g, j + 1)
                    elif not at(g, (T // G - 1,)):
                        evac_xnT(g + 1, 0)
                    act.wait_ge(s.qkv_mm, t + 1)
                    for half in range(2):
                        last = act.activation(qkv[:, bass.ds(t, 1), 384 * half:384 * half + 384].rearrange("p a c -> p (a c)"),
                                              bank[5 + half][0:P, 0:384], ACT.Copy)
                    last.then_inc(s.qkv_evac, 1)
                    act.wait_ge(s.m_mm, t + 1)
                    if not at(g, (0,)):
                        act.wait_ge(m_out[j], g * 16)
                    act.activation(m_rows[:, j, :], bank[4][0:P, 0:D], ACT.Copy).then_inc(s.m_evac, 1)
                    if not at(t, (0,)):
                        squares(t - 1)
                    if at(t, (2,)):
                        root(G, T, 2)

            evac_xnT(0, 0)
            for k in range(4):
                act.wait_ge(s.wT_mm, k + 1)
                got = bview(4 + k, 4, 128)
                if k < 3:
                    for i in range(2):
                        last = act.activation(wqkvT[:, :, (2 * k + i) * 128:(2 * k + i + 1) * 128],
                                              got[:, 2 * i:2 * i + 2, :], ACT.Copy)
                else:
                    for i in range(2):
                        last = act.activation(wprojT[:, :, i * 128:(i + 1) * 128], got[:, 2 * i:2 * i + 2, :], ACT.Copy)
                last.then_inc(s.act_chain, 1)
            act.wait_ge(s.gnn_in, 32)
            act.wait_ge(s.bias_in, 16 * len(SMALL))
            front(0, False)
            act.wait_ge(s.ln_stats, 3)
            with act.Fori(1, T // G - 1) as g:
                front(g, True)
            front(T // G - 1, False)
            squares(T - 1)
            act.wait_ge(s.norm_part, T)
            act.activation(norm[:, :, 0:H], norm[:, :, 0:H], ACT.Sqrt, scale=SCALE2)
            act.activation(norm[:, :, H:2 * H], norm[:, :, H:2 * H], ACT.Sqrt).then_inc(s.norm_root, 1)

            act.wait_ge(s.v1_ones, 1)

            def k_rows(t, turn):
                act.wait_ge(s.kd_ok, t + 1)
                if not at(t, (0, 1)):
                    act.wait_ge(s.lin_mm, t - 1)
                act.activation(k_row[:, turn, :, :], kd[:, turn, :, 0:DH], ACT.Copy).then_inc(s.k_row_ok, 1)
                if not at(t, (0, 1)):
                    act.wait_ge(s.head_mm, t * H - H)
                    act.wait_ge(s.diag_mm, t - 1)
                apart(act)
                act.activation(v1[:, turn, :, 1:HV], qkv[:, bass.ds(t, 1), 2 * D:3 * D].rearrange("p a (h d) -> p (a h) d", h=H),
                               ACT.Copy).then_inc(s.v1_ok, 1)

            sum_tiles(act, k_rows)
            k_rows(T - 2, 1)
            k_rows(T - 1, 0)

            def qT_of(t):
                act.wait_ge(s.q_partsT_mm, t + 1)
                if not at(t, (0,)):
                    act.wait_ge(s.sel_mm, t * H)
                act.activation(qT[:, :, 0:P], q_partsT_ps[:, :, 0:P], ACT.Copy).then_inc(s.qT_ok, 1)
                act.wait_ge(s.qnT_mm, t + 1)
                if not at(t, (0,)):
                    act.wait_ge(s.y_ld_mm, t)
                act.activation(q_lin, bview(1, 2, P), ACT.Copy)
                act.activation(q_sq, bview(1, 2, P), ACT.Square).then_inc(s.q_ld_ok, 1)

            def mixT_of(t):
                act.wait_ge(s.mixT_mm, t + 1)
                act.activation(mixT, bview(6, 2, P), ACT.Copy).then_inc(s.mixT_ok, 1)

            def q_tile(t):
                for h in range(H):
                    act.wait_ge(s.sel_mm, t * H + h + 1)
                    if not (at(t, (0,)) and h < 4):
                        act.wait_ge(s.y_mm, t * H + h - 3)
                    act.activation(q_pairs[:, h % 4, :, :], bview(2 + h % 2, 4, P), ACT.Square).then_inc(s.q_pairs_ok, 1)
                    if h == 1 and not at(t, (0,)):
                        mixT_of(t - 1)
                if not at(t, (T - 1,)):
                    qT_of(t + 1)

            act.wait_ge(s.kv_ok, 1)
            qT_of(0)
            q_tile(0)
            with act.Fori(1, T - 1) as t:
                q_tile(t)
            q_tile(T - 1)
            mixT_of(T - 1)

            def xn2T_of(g, turn, j):
                t = g * G + j
                act.wait_ge(s.xn2T_mm, t + 1)
                if not (at(g, (0,)) and j < 2):
                    act.wait_ge(s.gate_mm, t - 1 if j else g * G)
                act.activation(xn2T[:, (turn + j) % 2, :, :], bview(3 + (turn + j) % 2, 2, P), ACT.Copy).then_inc(s.xn2T_ok, 1)

            def second_pass(g, turn):
                for j in range(G):
                    t = g * G + j
                    slot = (turn + j) % 2
                    act.wait_ge(s.f1_mm, t + 1)
                    if not (at(g, (0,)) and j < 2):
                        act.wait_ge(s.f2_mm, t - 1)
                    for k in range(2):
                        last = act.activation(hT2[:, slot, k, :], bview(slot, 2, P)[:, k, :], ACT.Relu, bias=gnn_b1T[:, k:k + 1])
                    last.then_inc(s.h2_ok, 1)
                    if not at(g, (0,)):
                        for i in BEHIND[j]:
                            xn2T_of(g - 1, 1 - turn, i)
                act.wait_ge(s.ln2_stats, g + 1)
                act.activation(rstd[:, 0:G], mv[:, 0:G, 1], ACT.Sqrt, bias=eps_t).then_inc(s.ln2_root, 1)

            group_turns(act, second_pass)
            act.wait_ge(s.b1_mm, 1)
            act.activation(b1T, bank[7][:, 0:NX * 4], ACT.Copy).then_inc(s.b1_ok, 1)
            for i in range(G):
                xn2T_of(T // G - 1, 0, i)
            act.wait_ge(s.gap_ok, 1)
            act.activation(weight[:, :, 1:2], weight[:, :, 0:1], ACT.Exp).then_inc(s.exp_ok, 1)

            act.wait_ge(s.tok_ok, 1)
            act.wait_ge(s.b1_ok, 1)

            def relu_tile(i, j, expert):
                n = i * 4 + j
                act.wait_ge(s.ffn1_mm, n + 1)
                if not at(n, (0, 1)):
                    act.wait_ge(s.ffn2_mm, n - 1)
                apart(act)
                for c in range(4):
                    last = act.activation(hidT[:, j % 2, c, :], bview(2 + j % 2, 4, 128)[:, c, :], ACT.Relu,
                                          bias=b1T[:, bass.ds(expert * 4 + c, 1)])
                last.then_inc(s.relu_ok, 1)

            def relu_four(i):
                e = nc.values_load_multi_w_load_instructions(
                    tok_expert[:, bass.ds(i * 4, 4)], engines=[mybir.EngineType.Activation], min_val=0, max_val=NX - 1,
                    skip_runtime_bounds_check_because="clamped to the last expert when written")[1]
                for j in range(4):
                    relu_tile(i, j, e[j])

            relu_four(0)
            with act.Fori(1, NT // 4) as i:
                relu_four(i)
            for g in range(T // G):
                act.wait_ge(s.fin_stats, g + 1)
                act.activation(rstd[:, g * G:g * G + G], mv[:, g * G:g * G + G, 1], ACT.Sqrt, bias=eps_t).then_inc(s.fin_root, 1)
                act.wait_ge(s.fin_shift, g + 1)
                for t in range(G * g, G * g + G):
                    act.activation(pick0[:, t, :], pick1[:, t, :], ACT.Identity, scale=rstd[:, t:t + 1],
                                   bias=fin_shift[:, t:t + 1]).then_inc(s.fin_norm, 1)

        @block.vector
        def _(dve):
            chain = Chain(dve, s.dve_chain)
            def step(ins):
                chain.add(ins)
                chain.wait()

            def moments(lo, hi):
                for t in range(lo, hi):
                    if t % G == 0:
                        dve.wait_ge(s.x_in, 32 * (t // G + 1))
                    last = dve.bn_stats(stats[:, t, :], x_sb[:, t, :])
                step(last)
                for t in range(lo, hi):
                    last = dve.bn_aggr(mv[:, t, :], stats[:, t, :])
                last.then_inc(s.ln_stats, 1)

            def inverse(lo, hi, n):
                dve.wait_ge(s.rstd_sd, n)
                step(dve.reciprocal(rstd[:, lo:hi], rstd[:, lo:hi]))

            def normalise(g):
                if g:
                    dve.wait_ge(s.xnT_mm, G * g)
                for j in range(G):
                    t = g * G + j
                    dve.tensor_scalar(xn_rows[:, j, :], x_sb[:, t, :], mv[:, t, 0:1], rstd[:, t:t + 1],
                                      ALU.subtract, ALU.mult).then_inc(s.xn_ready, 1)

            moments(0, G)
            inverse(0, G, 1)
            normalise(0)
            moments(G, T)
            dve.wait_ge(s.edges_in, 32)
            step(dve.tensor_scalar(loc_f, src_i, 0.5, 1.0 / T, ALU.add, ALU.mult))
            step(dve.tensor_scalar(loc_f, loc_f, -0.5, MAGIC, ALU.add, ALU.add))
            step(dve.tensor_scalar(loc_f, loc_f, MAGIC, None, ALU.subtract))
            step(dve.scalar_tensor_tensor(bkt_h, loc_f, -float(T), src_i, ALU.mult, ALU.add))
            dve.tensor_scalar(val_dst, dst_i, -float(MID), None, ALU.add)
            dve.tensor_scalar(val_loc, loc_f, 1.0, None, ALU.add)
            for w in range(NB // G):
                for j in range(G):
                    last = dve.tensor_scalar(wave_hot[:, j, :], bkt_h, float(w * G + j), 0.0, ALU.is_equal, ALU.add,
                                             accum_out=cnt[:, w * G + j:w * G + j + 1])
                chain.add(last)
                chain.wait()
                if w == 2:
                    inverse(G, T, 2)
                    dve.scalar_tensor_tensor(shift[:, G:T], mv[:, G:T, 0], -1.0, rstd[:, G:T], ALU.mult,
                                             ALU.mult).then_inc(s.ln_stats, 1)
                    normalise(1)
            dve.memset(pos, 0.0).then_inc(s.cnt_ok, 1)
            dve.wait_ge(s.prefix_mm, 1)
            before, total, col = bank[7][0:P, 0:NB], bank[7][0:P, 64:64 + NB], bank[7][0:NB, 128:129]
            half = (SLOT - 1) / 2.0
            for dst_, src_ in ((n_tiles, total), (n_col, col)):
                chain.add(dve.tensor_scalar(dst_, src_, half, 1.0 / SLOT, ALU.add, ALU.mult))
            chain.wait()
            for dst_ in (n_tiles, n_col):
                chain.add(dve.tensor_scalar(dst_, dst_, MAGIC, None, ALU.add))
            chain.wait()
            chain.add(dve.tensor_scalar(n_tiles, n_tiles, MAGIC, None, ALU.subtract))
            dve.tensor_scalar(n_col, n_col, MAGIC, None, ALU.subtract).then_inc(s.n_col_ok, 1)
            chain.wait()
            step(dve.tensor_tensor_scan(incl, ones[0:P, 0:NB], n_tiles, 0.0, ALU.mult, ALU.add))
            step(dve.tensor_tensor(incl, incl, n_tiles, ALU.subtract))
            step(dve.scalar_tensor_tensor(off, incl, float(SLOT), before, ALU.mult, ALU.add))
            step(dve.tensor_scalar(off, off, -1.0, None, ALU.add))
            dve.wait_ge(s.preps, 1)
            for w in range(NB // G):
                for j in range(G):
                    last = dve.tensor_scalar(wave_hot[:, j, :], bkt_h, float(w * G + j), None, ALU.is_equal)
                step(last)
                for j in range(G):
                    last = dve.tensor_tensor_scan(wave_pos[:, j, :], ones[0:P, 0:1].broadcast_to([P, EC]), wave_hot[:, j, :],
                                                  off[:, w * G + j:w * G + j + 1], ALU.mult, ALU.add)
                step(last)
                step(dve.tensor_tensor(wave_pos, wave_pos, wave_hot, ALU.mult))
                for j in range(G):
                    step(dve.tensor_tensor(pos, pos, wave_pos[:, j, :], ALU.add))
            step(dve.tensor_scalar(slot_q, pos, -half, 1.0 / SLOT, ALU.add, ALU.mult))
            step(dve.tensor_scalar(slot_q, slot_q, MAGIC, None, ALU.add))
            step(dve.tensor_scalar(slot_q, slot_q, MAGIC, None, ALU.subtract))
            step(dve.scalar_tensor_tensor(slot_r, slot_q, -float(SLOT), pos, ALU.mult, ALU.add))
            def columns(i, which):
                for c in which:
                    hot_q, hot_d, hot_l = col_hot[c % 8]
                    col = lambda a: a[:, bass.ds(i * 16 + c, 1)]
                    if c >= 8 or not at(i, (0,)):
                        dve.wait_ge(s.col_mm, i * 16 + c - 7)
                    dve.tensor_scalar(hot_q, iota_q[0:P, :], col(slot_q), None, ALU.is_equal)
                    dve.tensor_scalar(hot_d, iota_r[0:P, :], col(slot_r), col(val_dst), ALU.is_equal, ALU.mult)
                    dve.tensor_scalar(hot_l, iota_r[0:P, :], col(slot_r), col(val_loc), ALU.is_equal, ALU.mult).then_inc(s.col_hot_ok, 1)

            columns(0, range(16))
            columns(1, range(8))
            dve.wait_ge(s.norm_root, 1)
            step(dve.tensor_scalar(norm, norm, 1e-12, None, ALU.max))
            step(dve.reciprocal(norm, norm))
            dve.tensor_tensor(norm[:, :, 0:H], norm[:, :, 0:H], temp_t.unsqueeze(1).broadcast_to([P, T, H]), ALU.mult)
            dve.tensor_scalar(norm[:, :, H:2 * H], norm[:, :, H:2 * H], SCALE2 ** 0.5, None, ALU.mult).then_inc(s.norm_ok, 1)

            columns(1, range(8, 16))

            def k_tile(t, turn):
                k = kd[:, turn, :, 0:DH]
                for h in range(H):
                    if not at(t, (T - 2, T - 1)):
                        columns(t + 2, (2 * h, 2 * h + 1))
                    if h == 1:
                        dve.wait_ge(s.kd_ok, t + 1)
                        chain.add(dve.reduce_sum(k_sum, k, axis=AX.X))
                    if h == 2:
                        chain.wait()
                        chain.add(dve.scalar_tensor_tensor(k_tmp, k, 2.0, k_sum.unsqueeze(2).broadcast_to([P, H, DH]),
                                                           ALU.mult, ALU.subtract))
                    if h == 3:
                        chain.wait()
                        if not at(t, (0,)):
                            dve.wait_ge(s.diag_mm, t)
                        dve.tensor_tensor(k_diag, k, k_tmp, ALU.mult).then_inc(s.k_diag_ok, 1)

            def chained(t, turn):
                if isinstance(t, int):
                    k_tile(t, turn)
                else:
                    if turn == 1:
                        chain.enter(t, 1, 2)
                    k_tile(t, turn)
                    if turn == 0:
                        chain.n -= 2
                        chain.leave(T - 5)

            sum_tiles(dve, chained)
            dve.wait_ge(s.ends_mm, 1)
            step(dve.tensor_copy(ends, bank[7][0:NB, 0:1]))
            dve.tensor_scalar(past_end, iota_q[0:NB, :], ends, None, ALU.is_ge).then_inc(s.past_ok, 1)
            dve.wait_ge(s.bucket_mm, 1)
            dve.tensor_scalar(edge_bucket, bank[7][0:1, 0:NQ], float(NB - 1), None, ALU.min)
            dve.wait_ge(s.col_mm, EC)
            dve.tensor_scalar(edge_idx, bank[4][:, 0:NQ], float(MID), None, ALU.add)
            dve.tensor_copy(edge_loc, bank[5][:, 0:NQ]).then_inc(s.sorted_ok, 1)

            def hot_batch(n, turn):
                dve.tensor_tensor(hot_src[:, turn, :, :], iota_loc.unsqueeze(1).broadcast_to([128, GB, P]),
                                  edge_loc[:, bass.ds(n * GB, GB)].unsqueeze(2).broadcast_to([128, GB, P]),
                                  ALU.is_equal).then_inc(s.hot_src_ok, 1)

            def buckets(m, count):
                return nc.values_load_multi_w_load_instructions(
                    edge_bucket[:, bass.ds(m, count)], engines=[mybir.EngineType.DVE], min_val=0, max_val=NB - 1,
                    skip_runtime_bounds_check_because="clamped to the last bucket when written")[1]

            def add_pair(m, half, bucket):
                dve.wait_ge(s.agg_mm, m + 2)
                for j in range(2):
                    if not at(m + j, (0,)):
                        dve.wait_ge(s.agg_add, m + j)
                    rows = node[:, bass.ds(bucket[j], 1), 0:2 * P].rearrange("p a c -> p (a c)")
                    dve.tensor_tensor(rows, rows, agg_ps[2 * half + j], ALU.add).then_inc(s.agg_add, 1)

            dve.wait_ge(s.sorted_ok, 1)
            dve.wait_ge(s.xnT_ready, T)
            hot_batch(0, 0)
            hot_batch(1, 1)
            k_tile(T - 2, 1)
            k_tile(T - 1, 0)
            dve.wait_ge(s.head_mm, T * H)
            dve.wait_ge(s.diag_mm, T)
            for i in range(3):
                n = min(3, H - 3 * i)
                dve.tensor_tensor(kv[:, 3 * i:3 * i + n, :, :],
                                  bank[i][:, 0:n * 4 * HV].rearrange("p (h c e) -> p h c e", h=n, c=4),
                                  pair_w.unsqueeze(1).unsqueeze(3).broadcast_to([128, n, 4, HV]), ALU.mult)
            for i in range(2):
                mask = head_mask.unsqueeze(2).broadcast_to([128, 4, HV])
                dve.scalar_tensor_tensor(kv_lin[:, i, :].rearrange("p (h e) -> p h e", h=4),
                                         lin_ps[i].rearrange("p (h e) -> p h e", h=4), SCALE2 / N, mask, ALU.mult, ALU.mult)
                dve.scalar_tensor_tensor(kv_diag[:, i, :].rearrange("p (h e) -> p h e", h=4),
                                         diag_ps[i].rearrange("p (h e) -> p h e", h=4), 0.5 / N, mask, ALU.mult, ALU.mult)
            dve.wait_ge(s.v_sum_mm, 1)
            total = v_sum.rearrange("p (h e) -> p h e", h=H)
            chain.add(dve.memset(total[:, :, 0:1], SCALE2 ** 2))
            step(dve.tensor_scalar(total[:, :, 1:HV], bank[6][0:96, 0:D].rearrange("p (h e) -> p h e", h=H), SCALE2 ** 2 / N,
                                   None, ALU.mult))
            step(dve.tensor_copy(v_parts, v_sum))
            step(dve.tensor_tensor(v_sum, v_sum, v_parts, ALU.subtract))
            dve.tensor_copy(v_parts[32:64, :], v_sum[32:64, :])
            step(dve.tensor_copy(v_parts[64:96, :], v_sum[64:96, :]))
            step(dve.tensor_tensor(v_sum[64:96, :], v_sum[64:96, :], v_parts[64:96, :], ALU.subtract))
            dve.tensor_copy(v_parts[64:96, :], v_sum[64:96, :]).then_inc(s.kv_ok, 1)

            def split(t, part):
                if part == 0:
                    if not at(t, (0,)):
                        dve.wait_ge(s.qnT_mm, t)
                    chain.add(dve.tensor_tensor(
                        q_row, qkv[:, bass.ds(t, 1), 0:D].rearrange("p a (h d) -> p (a h) d", h=H),
                        norm[:, bass.ds(t, 1), 0:H].rearrange("p a h -> p (a h)").unsqueeze(2).broadcast_to([P, H, DH]), ALU.mult))
                if part == 1:
                    if not at(t, (0,)):
                        dve.wait_ge(s.q_partsT_mm, t)
                    chain.wait()
                    chain.add(dve.tensor_copy(q_parts[:, :, 0, :], q_row))
                if part == 2:
                    chain.wait()
                    chain.add(dve.tensor_tensor(q_rest, q_row, q_parts[:, :, 0, :], ALU.subtract))
                if part == 3:
                    chain.wait()
                    chain.add(dve.tensor_copy(q_parts[:, :, 1, :], q_rest))
                if part == 4:
                    chain.wait()
                    dve.tensor_tensor(q_parts[:, :, 2, :], q_rest, q_parts[:, :, 1, :], ALU.subtract).then_inc(s.split_ok, 1)

            def add_mix(t):
                dve.wait_ge(s.proj_mm, t + 1)
                rows = x_sb[:, bass.ds(t, 1), :].rearrange("p a c -> p (a c)")
                dve.tensor_tensor(rows, rows, bank[6][0:P, 256:512], ALU.add).then_inc(s.x_ok, 1)

            def q_tile(t):
                m = (t + 1) * 2 * GB
                bucket = buckets(m - 2, 2 * GB)
                for h in range(H):
                    if h < 5 and not at(t, (T - 1,)):
                        split(t + 1, h)
                    add_pair(m + 2 * h - 2, (h + 1) % 2, bucket[2 * h:2 * h + 2])
                    if h == 0 and not at(t, (0,)):
                        hot_batch(t * 2 + 3, 1)
                    if h == 4 and not at(t, (T - 1,)):
                        hot_batch(t * 2 + 4, 0)
                    if h == 6 and not at(t, (0,)):
                        add_mix(t - 1)
                dve.wait_ge(s.y_mm, t * H + H)
                y = bank[7][0:P, 0:H * HV].rearrange("p (h e) -> p h e", h=H)
                chain.add(dve.reciprocal(y_rcp.unsqueeze(2), y[:, :, 0:1]))
                chain.wait()
                if not at(t, (0,)):
                    dve.wait_ge(s.mixT_mm, t)
                dve.tensor_tensor(mix_row, y[:, :, 1:HV], y_rcp.unsqueeze(2).broadcast_to([P, H, DH]),
                                  ALU.mult).then_inc(s.mix_row_ok, 1)

            bucket = buckets(0, 2 * GB - 2)
            for h in range(H - 1):
                if h < 5:
                    split(0, h)
                add_pair(2 * h, h % 2, bucket[2 * h:2 * h + 2])
                if h == 3:
                    hot_batch(2, 0)
            dve.wait_ge(s.agg_mm, 2 * GB)
            hot_batch(3, 1)
            q_tile(0)
            with dve.Fori(1, T - 1) as t:
                chain.enter(t, 1, 5)
                q_tile(t)
            chain.leave(T - 2)
            q_tile(T - 1)
            add_mix(T - 1)
            add_pair(NQ - 2, 1, buckets(NQ - 2, 2))

            def choose(g):
                dve.wait_ge(s.gate_mm, g * G + G)
                dve.tensor_tensor(logits, bview(5, G, NX, P), gate_b_bc.unsqueeze(1).broadcast_to([P, G, NX]),
                                  ALU.add).then_inc(s.gate_ok, 1)
                dve.wait_ge(s.gate_ok, g + 1)
                apart(dve)
                for j in range(G):
                    last = dve.max(top_val[:, j, :], logits[:, j, :])
                chain.add(last)
                chain.wait()
                apart(dve)
                for j in range(G):
                    last = dve.max_index(top_idx[:, j, :], top_val[:, j, :], logits[:, j, :])
                chain.add(last)
                chain.wait()
                dve.tensor_copy(score[:, bass.ds(g * G, G), :], top_val[:, :, 0:2])
                chain.add(dve.tensor_copy(choice[:, bass.ds(g * G, G), :], top_idx[:, :, 0:2]))
                chain.wait()

            def second_pass(g, turn):
                for j in range(G + 1):
                    t = g * G + j
                    if j < G:
                        dve.wait_ge(s.f2_mm, t + 1)
                        rows = x_sb[:, bass.ds(t, 1), :].rearrange("p a c -> p (a c)")
                        dve.tensor_tensor(rows, rows, bank[2 + 4 * ((turn + j) % 2)][0:P, 0:D], ALU.add).then_inc(s.x2_add, 1)
                    if j:
                        dve.wait_ge(s.x2_add, t)
                        apart(dve)
                        rows = x_sb[:, bass.ds(t - 1, 1), :].rearrange("p a c -> p (a c)")
                        last = dve.bn_stats(stats[:, j - 1, :], rows)
                chain.add(last)
                chain.wait()
                apart(dve)
                for j in range(G):
                    last = dve.bn_aggr(mv[:, j, :], stats[:, j, :])
                last.then_inc(s.ln2_stats, 1)
                if not at(g, (0,)):
                    choose(g - 1)
                dve.wait_ge(s.ln2_root, g + 1)
                chain.add(dve.reciprocal(rstd[:, 0:G], rstd[:, 0:G]))
                chain.wait()
                if not at(g, (0, 1)):
                    dve.wait_ge(s.xn2T_mm, g * G - G)
                    dve.wait_ge(xn2_out[turn], (g - turn) * 8)
                for j in range(G):
                    t = g * G + j
                    rows = x_sb[:, bass.ds(t, 1), :].rearrange("p a c -> p (a c)")
                    dve.tensor_scalar(xn2[:, turn, j, :], rows, mv[:, j, 0:1], rstd[:, j:j + 1], ALU.subtract,
                                      ALU.mult).then_inc(s.xn2_ok, 1)

            def chained_groups(g, turn):
                if isinstance(g, int):
                    second_pass(g, turn)
                else:
                    if turn == 1:
                        chain.enter(g, 1, 5)
                    second_pass(g, turn)
                    if turn == 0:
                        chain.n -= 5
                        chain.leave(T // G - 1)

            dve.wait_ge(s.gate_in, 32)
            group_turns(dve, chained_groups)
            choose(T // G - 1)
            dve.tensor_tensor(weight[:, :, 0:1], score[:, :, 1:2], score[:, :, 0:1], ALU.subtract).then_inc(s.gap_ok, 1)
            pick = choice.rearrange("p t k -> p (t k)")
            dve.wait_ge(xn2_out[0], 16 * 3)
            dve.wait_ge(xn2_out[1], 16 * 2)
            step(dve.tensor_tensor(hot_x, iota_x[0:P, :].unsqueeze(2).broadcast_to([P, NX, 2 * T]),
                                   pick.unsqueeze(1).broadcast_to([P, NX, 2 * T]), ALU.is_equal))
            step(dve.tensor_tensor_scan(run_x.rearrange("p e c -> p (e c)"), ones[0:P, 0:1].broadcast_to([P, NX * 2 * T]),
                                        hot_x.rearrange("p e c -> p (e c)"), 0.0, ALU.mult, ALU.add))
            step(dve.tensor_copy(last_slot.unsqueeze(2), run_x[:, :, 2 * T - 1:2 * T]))
            step(dve.tensor_copy(count_x, last_slot))
            dve.tensor_tensor(count_x[:, 1:NX], last_slot[:, 1:NX], last_slot[:, 0:NX - 1], ALU.subtract).then_inc(s.count_ok, 1)
            dve.wait_ge(s.count_ok, 1)
            step(dve.tensor_tensor(last_slot, last_slot, count_x, ALU.subtract))
            dve.wait_ge(s.route_mm, 1)
            for dst_, src_ in ((tiles_x, bank[7][0:P, 128:128 + NX]), (col_x, bank[7][0:NX, 192:193])):
                chain.add(dve.tensor_scalar(dst_, src_, half, 1.0 / SLOT, ALU.add, ALU.mult))
            chain.wait()
            for dst_ in (tiles_x, col_x):
                chain.add(dve.tensor_scalar(dst_, dst_, MAGIC, None, ALU.add))
            chain.wait()
            chain.add(dve.tensor_scalar(tiles_x, tiles_x, MAGIC, None, ALU.subtract))
            dve.tensor_scalar(col_x, col_x, MAGIC, None, ALU.subtract).then_inc(s.col_x_ok, 1)
            chain.wait()
            step(dve.tensor_tensor_scan(incl_x, ones[0:P, 0:NX], tiles_x, 0.0, ALU.mult, ALU.add))
            step(dve.tensor_tensor(incl_x, incl_x, tiles_x, ALU.subtract))
            step(dve.scalar_tensor_tensor(off_x, incl_x, float(SLOT), bank[7][0:P, 64:64 + NX], ALU.mult, ALU.add))
            step(dve.scalar_tensor_tensor(off_x, off_x, -1.0, last_slot, ALU.add, ALU.subtract))
            step(dve.tensor_tensor(run_x, run_x, off_x.unsqueeze(2).broadcast_to([P, NX, 2 * T]), ALU.add))
            step(dve.tensor_tensor(run_x, run_x, hot_x, ALU.mult))
            step(dve.reduce_sum(pos_x, run_x.rearrange("p e c -> p c e"), axis=AX.X))
            step(dve.tensor_scalar(slot_qx, pos_x, -half, 1.0 / SLOT, ALU.add, ALU.mult))
            step(dve.tensor_scalar(slot_qx, slot_qx, MAGIC, None, ALU.add))
            step(dve.tensor_scalar(slot_qx, slot_qx, MAGIC, None, ALU.subtract))
            step(dve.scalar_tensor_tensor(slot_rx, slot_qx, -float(SLOT), pos_x, ALU.mult, ALU.add))
            wide = lambda v, n: v.unsqueeze(2).broadcast_to([P, 2 * T, n])
            dve.tensor_tensor(hot_qx, iota_q[0:P, 0:NT].unsqueeze(1).broadcast_to([P, 2 * T, NT]), wide(slot_qx, NT),
                              ALU.is_equal).then_inc(s.hot_qx_ok, 1)
            dve.wait_ge(s.hot_qx_ok, 1)
            dve.tensor_tensor(val_qx[:, :, 0, :], hot_qx, wide(tok_val.rearrange("p t k -> p (t k)"), NT), ALU.mult)
            for c in range(0, 2 * T, 2 * G):
                dve.tensor_tensor(hot_rx[:, c:c + 2 * G, :], iota_r[0:P, :].unsqueeze(1).broadcast_to([P, 2 * G, 128]),
                                  slot_rx[:, c:c + 2 * G].unsqueeze(2).broadcast_to([P, 2 * G, 128]),
                                  ALU.is_equal).then_inc(s.tok_hot_ok, 1)
            dve.wait_ge(s.exp_ok, 1)
            step(dve.tensor_scalar(weight[:, :, 0:1], weight[:, :, 1:2], 1.0, None, ALU.add))
            step(dve.reciprocal(weight[:, :, 0:1], weight[:, :, 0:1]))
            chain.add(dve.tensor_tensor(weight[:, :, 1:2], weight[:, :, 1:2], weight[:, :, 0:1], ALU.mult))
            dve.wait_ge(s.ends_x_mm, 1)
            step(dve.tensor_copy(ends_x, bank[6][0:NX, 0:1]))
            dve.tensor_scalar(past_x, iota_q[0:NX, 0:NT], ends_x, None, ALU.is_ge).then_inc(s.past_x_ok, 1)
            dve.wait_ge(s.expert_mm, 1)
            chain.add(dve.tensor_scalar(tok_expert, bank[6][0:1, 64:64 + NT], float(NX - 1), None, ALU.min))
            dve.wait_ge(s.tok_mm, 1)
            ids, picks = bank[5][:, 0:NT], bank[5][:, NT:2 * NT]
            dve.tensor_scalar(tok_gather, ids, float(MID), None, ALU.add)
            dve.wait_ge(s.trash_ok, 1)
            step(dve.scalar_tensor_tensor(unused, picks, 0.0, trash.rearrange("p a b -> p (a b)"), ALU.is_equal, ALU.mult))
            step(dve.scalar_tensor_tensor(out_row, picks, float(N), unused, ALU.mult, ALU.add))
            dve.scalar_tensor_tensor(tok_scatter, ids, float(MID - N), out_row, ALU.add, ALU.add).then_inc(s.tok_ok, 1)

            def take_in(i, j, expert):
                n = i * 4 + j
                if not at(n, (0, 1)):
                    dve.wait_ge(s.ffn1_mm, n - 1)
                dve.tensor_copy(w1_turn[j % 2], experts[:, bass.ds(expert, 1), 0:2 * FF].rearrange("p a n -> p (a n)")).then_inc(s.w1_ok, 1)
                dve.wait_ge(s.tokT_mm, n + 1)
                dve.tensor_copy(tokT[:, j % 2, :, :], bview(j % 2, 2, 128)).then_inc(s.tokT_ok, 1)

            def y_tile(i, j, expert):
                n = i * 4 + j
                dve.wait_ge(s.ffn2_mm, n + 1)
                if not at(n, (0, 1)):
                    dve.wait_ge(y_out[j % 2], (i * 2 + j // 2) * 16)
                dve.tensor_tensor(y_rows[:, j % 2, :], bank[6 + j % 2][:, 0:D],
                                  b2_x[:, bass.ds(expert, 1), :].rearrange("p a c -> p (a c)"), ALU.add).then_inc(s.y_ok, 1)

            def chosen(at_, count):
                return nc.values_load_multi_w_load_instructions(
                    tok_expert[:, bass.ds(at_, count)], engines=[mybir.EngineType.DVE], min_val=0, max_val=NX - 1,
                    skip_runtime_bounds_check_because="clamped to the last expert when written")[1]

            def four_tiles(i):
                e = chosen(i * 4, 6)
                for j in range(4):
                    take_in(i, j + 2, e[j + 2])
                    y_tile(i, j, e[j])

            dve.wait_ge(s.tok_ok, 1)
            dve.wait_ge(s.w_in, 32 * NX)
            e = chosen(0, 2)
            take_in(0, 0, e[0])
            take_in(0, 1, e[1])
            dve.wait_ge(s.late_in, 48)
            four_tiles(0)
            with dve.Fori(1, NT // 4 - 1) as i:
                four_tiles(i)
            i = NT // 4 - 1
            e = chosen(NT - 4, 4)
            for j in range(4):
                if j < 2:
                    take_in(i, j + 2, e[j + 2])
                y_tile(i, j, e[j])

            def shift_of(g):
                dve.wait_ge(s.fin_root, g + 1)
                tiles = slice(G * g, G * g + G)
                step(dve.reciprocal(rstd[:, tiles], rstd[:, tiles]))
                dve.scalar_tensor_tensor(fin_shift[:, tiles], mv[:, tiles, 0], -1.0, rstd[:, tiles], ALU.mult,
                                         ALU.mult).then_inc(s.fin_shift, 1)

            def residual(g):
                for t in [G * g + j for j in VECTOR_ADDS]:
                    dve.wait_ge(s.fin_gamma, t + 1)
                    dve.tensor_tensor(pick0[:, t, :], pick0[:, t, :], x_sb[:, t, :], ALU.add).then_inc(s.fin_ok_too, 1)

            dve.wait_ge(s.beta_ok, T)
            for g in range(T // G):
                tiles = range(G * g, G * g + G)
                dve.wait_ge(fin_in[g], 6 * 16)
                for t in tiles:
                    last = dve.scalar_tensor_tensor(pick0[:, t, :], pick0[:, t, :], weight[:, t, 0:1], own[:, t, :], ALU.mult, ALU.add)
                step(last)
                for t in tiles:
                    last = dve.scalar_tensor_tensor(pick1[:, t, :], pick1[:, t, :], weight[:, t, 1:2], pick0[:, t, :], ALU.mult, ALU.add)
                step(last)
                for t in tiles:
                    last = dve.bn_stats(stats[:, t, :], pick1[:, t, :])
                step(last)
                for t in tiles:
                    last = dve.bn_aggr(mv[:, t, :], stats[:, t, :])
                last.then_inc(s.fin_stats, 1)
                if g:
                    shift_of(g - 1)
                if g > 1:
                    residual(g - 2)
            shift_of(T // G - 1)
            residual(T // G - 2)
            residual(T // G - 1)

        @block.tensor
        def _(pe):
            mm = pe.matmul
            pe.wait_ge(s.consts, 1)

            def transpose_rows(g, j):
                t = g * G + j
                if at(g, (0, 1)):
                    pe.wait_ge(s.xn_ready, t + 1)
                else:
                    pe.wait_ge(s.xn_row_ok, t + 1 - 2 * G)
                if not (at(g, (0,)) and j < 2):
                    pe.wait_ge(s.xnT_ready, t - 1 if j >= 2 else g * G)
                for k in range(2):
                    last = pe.transpose(bview(j % 2, 2, P)[:, k, :],
                                        xn_rows[:, j, 128 * k:128 * k + 128], ident[0:P, 0:P])
                last.then_inc(s.xnT_mm, 1)

            def front(g):
                for j in range(G):
                    t = g * G + j
                    pe.wait_ge(s.xnT_ready, t + 1)
                    if not (at(g, (0,)) and j < 2):
                        pe.wait_ge(s.h_ready, t - 1 if j >= 2 else g * G)
                    for f in range(2):
                        for k in range(2):
                            last = mm(bview(2 + j % 2, 2, P)[:, f, :], w1_sb[:, k, 128 * f:128 * f + 128],
                                      xnT[:, j, k, :], start=k == 0, stop=k == 1)
                    last.then_inc(s.l1_mm, 1)
                    if j < G - 1:
                        transpose_rows(g, j + 1)
                    elif not at(g, (T // G - 1,)):
                        transpose_rows(g + 1, 0)
                    if not at(t, (0,)):
                        pe.wait_ge(s.qkv_evac, t)
                    for half in range(2):
                        for k in range(2):
                            last = mm(bank[5 + half][0:P, 0:384], xnT[:, j, k, :], wqkvT[:, k, 384 * half:384 * half + 384],
                                      start=k == 0, stop=k == 1)
                    last.then_inc(s.qkv_mm, 1)
                    pe.wait_ge(s.h_ready, t + 1)
                    if not at(t, (0,)):
                        pe.wait_ge(s.m_evac, t)
                    for k in range(2):
                        last = mm(bank[4][0:P, 0:D], hT[:, j, k, :], w2_sb[:, k, :], start=k == 0, stop=k == 1)
                    last.then_inc(s.m_mm, 1)

            transpose_rows(0, 0)
            pe.wait_ge(s.raw_in, 32)
            for k in range(4):
                for i in range(2):
                    for c in range(2):
                        last = pe.transpose(bview(4 + k, 4, 128)[:, 2 * i + c, :], raw_w[:, 2 * k + i, 128 * c:128 * c + 128], ident)
                last.then_inc(s.wT_mm, 1)
            pe.wait_ge(s.gnn_in, 32)
            pe.wait_ge(s.act_chain, 4)
            front(0)
            pe.wait_ge(s.cnt_ok, 1)
            mm(bank[7][0:P, 0:NB], tri, cnt, start=True, stop=True)
            mm(bank[7][0:P, 64:64 + NB], ones[0:P, :], cnt, start=True, stop=True)
            mm(bank[7][0:NB, 128:129], cnt, ones[0:P, 0:1], start=True, stop=True).then_inc(s.prefix_mm, 1)
            front(1)
            with pe.Fori(2, T // G - 1) as g:
                front(g)
            front(T // G - 1)
            pe.wait_ge(s.n_col_ok, 1)
            pe.wait_ge(s.col_hot_ok, 1)
            mm(bank[7][0:NB, 0:1], tri_in, n_col, start=True, stop=True).then_inc(s.ends_mm, 1)
            pe.wait_ge(s.m_evac, T)
            pe.wait_ge(s.qkv_evac, T)

            def columns(i, which):
                for c in which:
                    hot_q, hot_d, hot_l = col_hot[c % 8]
                    pe.wait_ge(s.col_hot_ok, i * 16 + c + 1)
                    group = dict(start=at(i, (0,)) and c == 0, stop=at(i, (T - 1,)) and c == 15)
                    mm(bank[4][:, 0:NQ], hot_d, hot_q, skip_group_check=True, **group)
                    mm(bank[5][:, 0:NQ], hot_l, hot_q, skip_group_check=True, **group).then_inc(s.col_mm, 1)

            def k_tile(t, turn):
                first = at(t, (0,))
                pe.wait_ge(s.k_row_ok, t + 1)
                pe.wait_ge(s.v1_ok, t + 1)
                group = dict(stop=at(t, (T - 1,)), skip_group_check=True)
                values = v1[:, turn, :, :]
                for i in range(2):
                    last = mm(lin_ps[i], k_row[:, turn, 4 * i:4 * i + 4, :], values[:, 4 * i:4 * i + 4, :], start=first, **group)
                last.then_inc(s.lin_mm, 1)
                for h in range(H):
                    if not at(t, (T - 2, T - 1)):
                        columns(t + 2, (2 * h, 2 * h + 1))
                    pe.wait_ge(s.pairs_ok, t * H + h + 1)
                    for c in range(4):
                        last = mm(bank[h // 3][:, (h % 3 * 4 + c) * HV:(h % 3 * 4 + c + 1) * HV], pairs[:, h, 128 * c:128 * c + 128],
                                  values[:, h, :], start=first and h in (0, 3) and c == 0, **group)
                    last.then_inc(s.head_mm, 1)
                    if h == 5:
                        pe.wait_ge(s.k_diag_ok, t + 1)
                        for i in range(2):
                            last = mm(diag_ps[i], k_diag[:, 4 * i:4 * i + 4, :], values[:, 4 * i:4 * i + 4, :], start=False, **group)
                        last.then_inc(s.diag_mm, 1)

            columns(0, range(16))
            columns(1, range(16))
            sum_tiles(pe, k_tile)
            pe.wait_ge(s.past_ok, 1)
            mm(bank[7][0:1, 0:NQ], ones[0:NB, 0:1], past_end, start=True, stop=True).then_inc(s.bucket_mm, 1)
            k_tile(T - 2, 1)
            k_tile(T - 1, 0)
            pe.wait_ge(s.v_acc_ok, T)
            mm(bank[6][0:P, 0:D], ones[0:P, :], v_acc, start=True, stop=True).then_inc(s.v_sum_mm, 1)

            def agg_pair(n, turn, q, rounds):
                if q == 0:
                    pe.wait_ge(s.hot_src_ok, n + 1)
                if not (at(n, (0,)) and q < 2):
                    pe.wait_ge(s.agg_add, n * GB + 2 * q - 2)
                for k in (2 * q, 2 * q + 1):
                    slot = turn * GB + k
                    pe.wait_ge(msgs_in[slot], rounds * 16)
                    for c in range(2):
                        last = mm(agg_ps[k % 4][:, P * c:P * c + P], msgs[slot][:, 128 * c:128 * c + 128], hot_src[:, turn, k, :],
                                  start=True, stop=True, skip_group_check=True)
                    last.then_inc(s.agg_mm, 1)

            for n in range(2):
                for q in range(4):
                    agg_pair(n, n, q, 1)

            def mixT_of(t):
                pe.wait_ge(s.mix_row_ok, t + 1)
                if not at(t, (0,)):
                    pe.wait_ge(s.mixT_ok, t)
                for k in range(2):
                    last = pe.transpose(bview(6, 2, P)[:, k, :], mix_row[:, 4 * k:4 * k + 4, :], ident[0:P, 0:P])
                last.then_inc(s.mixT_mm, 1)

            def project(t):
                pe.wait_ge(s.mixT_ok, t + 1)
                if not at(t, (0,)):
                    pe.wait_ge(s.x_ok, t)
                for k in range(2):
                    last = mm(bank[6][0:P, 256:512], mixT[:, k, :], wprojT[:, k, :], start=k == 0, stop=k == 1)
                last.then_inc(s.proj_mm, 1)

            def qT_of(t):
                pe.wait_ge(s.split_ok, t + 1)
                if not at(t, (0,)):
                    pe.wait_ge(s.qT_ok, t)
                for h in range(H):
                    last = pe.transpose(q_partsT_ps[:, h, 0:P], q_parts[:, h, :, :].rearrange("p a b -> p (a b)"), ident_h[0:P, 0:P])
                last.then_inc(s.q_partsT_mm, 1)
                if not at(t, (0,)):
                    pe.wait_ge(s.q_ld_ok, t)
                for k in range(2):
                    last = pe.transpose(bview(1, 2, P)[:, k, :], q_row[:, 4 * k:4 * k + 4, :], ident[0:P, 0:P])
                last.then_inc(s.qnT_mm, 1)

            def q_tile(t):
                y = bank[7][0:P, 0:H * HV]

                def sums(h):
                    if not (at(t, (0,)) and h < 2):
                        pe.wait_ge(s.q_pairs_ok, t * H + h - 1)
                    for c in range(4):
                        last = mm(bview(2 + h % 2, 4, P)[:, c, :], sel[:, c, :], qT[:, h, 0:P], start=True, stop=True,
                                  skip_group_check=True)
                    last.then_inc(s.sel_mm, 1)

                group = dict(stop=False, skip_group_check=True)
                pe.wait_ge(s.qT_ok, t + 1)
                sums(0)
                sums(1)
                agg_pair(t * 2 + 2, 0, 0, t + 2)
                if not at(t, (0,)):
                    mixT_of(t - 1)
                mm(y, part_rows[:, 0:P], v_parts, start=True, **group)
                pe.wait_ge(s.q_ld_ok, t + 1)
                for i in range(2):
                    mm(y[:, 4 * HV * i:4 * HV * (i + 1)], q_lin[:, i, :], kv_lin[:, i, :], start=False, **group)
                    last = mm(y[:, 4 * HV * i:4 * HV * (i + 1)], q_sq[:, i, :], kv_diag[:, i, :], start=False, **group)
                last.then_inc(s.y_ld_mm, 1)
                for h in range(H):
                    pe.wait_ge(s.q_pairs_ok, t * H + h + 1)
                    for c in range(4):
                        last = mm(y[:, HV * h:HV * h + HV], q_pairs[:, h % 4, c, :], kv[:, h, c, :], start=False,
                                  stop=c == 3, skip_group_check=True)
                    last.then_inc(s.y_mm, 1)
                    if h < H - 2:
                        sums(h + 2)
                    if h == 3 and not at(t, (0,)):
                        project(t - 1)
                    if h == 5 and not at(t, (T - 1,)):
                        qT_of(t + 1)
                    if h:
                        agg_pair(t * 2 + 2 + h // 4, h // 4, h % 4, t + 2)

            pe.wait_ge(s.kv_ok, 1)
            pe.wait_ge(s.part_rows_ok, 1)
            qT_of(0)
            q_tile(0)
            with pe.Fori(1, T - 1) as t:
                q_tile(t)
            q_tile(T - 1)
            mixT_of(T - 1)
            project(T - 1)

            pe.wait_ge(s.agg_add, NBATCH * GB)
            pe.wait_ge(s.x_ok, T)

            def up(g, turn, j):
                t = g * G + j
                if not (at(g, (0,)) and j < 2):
                    pe.wait_ge(s.h2_ok, t - 1)
                h = node[:, bass.ds(t, 1), :].rearrange("p a c -> p (a c)")
                for f in range(2):
                    for k in range(2):
                        last = mm(bview((turn + j) % 2, 2, P)[:, f, :], w1_sb[:, k, 128 * f:128 * f + 128], h[:, P * k:P * k + P],
                                  start=k == 0, stop=k == 1)
                last.then_inc(s.f1_mm, 1)

            def down(g, turn, j):
                t = g * G + j
                pe.wait_ge(s.h2_ok, t + 1)
                if not (at(g, (0,)) and j < 2):
                    pe.wait_ge(s.x2_add, t - 1)
                slot = (turn + j) % 2
                for k in range(2):
                    last = mm(bank[2 + 4 * slot][0:P, 0:D], hT2[:, slot, k, :], w2_sb[:, k, :], start=k == 0, stop=k == 1)
                last.then_inc(s.f2_mm, 1)

            def rows_of(g, turn, j):
                t = g * G + j
                pe.wait_ge(s.xn2_ok, t + 1)
                if not (at(g, (0,)) and j < 2):
                    pe.wait_ge(s.xn2T_ok, t - 1 if j else g * G)
                for k in range(2):
                    last = pe.transpose(bview(3 + (turn + j) % 2, 2, P)[:, k, :], xn2[:, turn, j, 128 * k:128 * k + 128],
                                        ident[0:P, 0:P])
                last.then_inc(s.xn2T_mm, 1)

            def gate(g, turn, j):
                t = g * G + j
                pe.wait_ge(s.xn2T_ok, t + 1)
                if j == 0 and not at(g, (0,)):
                    pe.wait_ge(s.gate_ok, g)
                for k in range(2):
                    last = mm(bank[5][0:P, NX * j:NX * j + NX], xn2T[:, (turn + j) % 2, k, :], gate_w_sb[:, k, :],
                              start=k == 0, stop=k == 1)
                last.then_inc(s.gate_mm, 1)

            def second_pass(g, turn):
                up(g, turn, 0)
                for j in range(G):
                    behind = [] if at(g, (0,)) else BEHIND[j]
                    if j < G - 1:
                        up(g, turn, j + 1)
                    for i in behind:
                        rows_of(g - 1, 1 - turn, i)
                    down(g, turn, j)
                    for i in behind:
                        gate(g - 1, 1 - turn, i)

            pe.wait_ge(s.gate_in, 32)
            group_turns(pe, second_pass)
            pe.wait_ge(s.b1_in, 16)
            pe.transpose(bank[7][:, 0:NX * 4], b1_rows, ident[0:NX * 4, 0:NX * 4]).then_inc(s.b1_mm, 1)
            last_group = T // G - 1
            rows_of(last_group, 0, 0)
            for j in range(G):
                if j < G - 1:
                    rows_of(last_group, 0, j + 1)
                gate(last_group, 0, j)
            pe.wait_ge(s.b1_ok, 1)
            pe.wait_ge(s.count_ok, 1)
            mm(bank[7][0:P, 64:64 + NX], tri, count_x, start=True, stop=True)
            mm(bank[7][0:P, 128:128 + NX], ones[0:P, :], count_x, start=True, stop=True)
            mm(bank[7][0:NX, 192:193], count_x, ones[0:P, 0:1], start=True, stop=True).then_inc(s.route_mm, 1)
            pe.wait_ge(s.col_x_ok, 1)
            mm(bank[6][0:NX, 0:1], tri_in[0:NX, 0:NX], col_x, start=True, stop=True).then_inc(s.ends_x_mm, 1)
            pe.wait_ge(s.tok_pick_ok, 1)
            for c in range(2 * T):
                if c % (2 * G) == 0:
                    pe.wait_ge(s.tok_hot_ok, c // (2 * G) + 1)
                last = mm(bank[5][:, 0:2 * NT], hot_rx[:, c, :], val_qx[:, c, :, :].rearrange("p a b -> p (a b)"),
                          start=c == 0, stop=c == 2 * T - 1)
            last.then_inc(s.tok_mm, 1)
            pe.wait_ge(s.past_x_ok, 1)
            mm(bank[6][0:1, 64:64 + NT], ones[0:NX, 0:1], past_x, start=True, stop=True).then_inc(s.expert_mm, 1)

            def tokT_of(i, j):
                n = i * 4 + j
                pe.wait_ge(tok_in[j % 4], (i + j // 4) * 16 + 16)
                if not at(n, (0, 1)):
                    pe.wait_ge(s.tokT_ok, n - 1)
                for k in range(2):
                    last = pe.transpose(bview(j % 2, 2, 128)[:, k, :], tok_rows[:, j % 4, 128 * k:128 * k + 128], ident)
                last.then_inc(s.tokT_mm, 1)

            def up_of(i, j):
                n = i * 4 + j
                pe.wait_ge(s.tokT_ok, n + 1)
                pe.wait_ge(s.w1_ok, n + 1)
                if not at(n, (0, 1)):
                    pe.wait_ge(s.relu_ok, n - 1)
                for f in range(4):
                    for k in range(2):
                        last = mm(bview(2 + j % 2, 4, 128)[:, f, :], w1_turn[j % 2][:, FF * k + 128 * f:FF * k + 128 * f + 128],
                                  tokT[:, j % 2, k, :], start=k == 0, stop=k == 1, skip_group_check=True)
                last.then_inc(s.ffn1_mm, 1)

            def down_of(i, j, expert):
                n = i * 4 + j
                pe.wait_ge(s.relu_ok, n + 1)
                if not at(n, (0, 1)):
                    pe.wait_ge(s.y_ok, n - 1)
                w = experts[:, bass.ds(expert, 1), 1024:2048].rearrange("p a n -> p (a n)")
                for c in range(4):
                    last = mm(bank[6 + j % 2][:, 0:D], hidT[:, j % 2, c, :], w[:, D * c:D * c + D], start=c == 0, stop=c == 3)
                last.then_inc(s.ffn2_mm, 1)

            def four_tiles(i, last_one=False):
                e = nc.values_load_multi_w_load_instructions(
                    tok_expert[:, bass.ds(i * 4, 4)], engines=[mybir.EngineType.PE], min_val=0, max_val=NX - 1,
                    skip_runtime_bounds_check_because="clamped to the last expert when written")[1]
                for j in range(4):
                    if not (last_one and j == 3):
                        up_of(i, j + 1)
                    if not (last_one and j >= 2):
                        tokT_of(i, j + 2)
                    down_of(i, j, e[j])

            pe.wait_ge(s.tok_ok, 1)
            pe.wait_ge(s.w_in, 32 * NX)
            tokT_of(0, 0)
            tokT_of(0, 1)
            up_of(0, 0)
            four_tiles(0)
            with pe.Fori(1, NT // 4 - 1) as i:
                four_tiles(i)
            four_tiles(NT // 4 - 1, last_one=True)


INPUTS = ("x src dst L0_gnn_w1 L0_gnn_b1 L0_gnn_w2 L0_gnn_b2 L0_mix_Wqkv L0_mix_bqkv L0_mix_Wproj L0_mix_bproj "
          "L0_mix_temperature L0_ffn_gate_w L0_ffn_gate_b L0_ffn_w1 L0_ffn_b1 L0_ffn_w2 L0_ffn_b2 L0_ffn_gamma "
          "L0_ffn_beta").split()


def kernel(**inputs):
    import concourse.bacc as _bacc
    from concourse.bass_utils import run_bass_kernel_spmd as _run

    nc = _bacc.Bacc("TRN2", target_bir_lowering=False, num_devices=1)
    arrays, args = {}, []
    for name in INPUTS:
        a = np.ascontiguousarray(inputs[name])
        arrays[name] = a
        args.append(nc.dram_tensor(name, a.shape, mybir.dt.from_np(a.dtype), kind="ExternalInput").ap())
    args.append(nc.dram_tensor("out", (N, D), F32, kind="ExternalOutput").ap())
    program(nc, *args)
    return _run(nc, [arrays], core_ids=[0]).results[0]["out"]
```
